# Optimizing a Trainium2 kernel written in Bass

```python
import numpy as np
import jax
import jax.numpy as jnp

def _softmax(x, axis=-1):
    return jax.nn.softmax(x, axis=axis)

def _gelu(x):
    return jax.nn.gelu(x, approximate=True)

def _silu(x):
    return jax.nn.silu(x)

def _sigmoid(x):
    return jax.nn.sigmoid(x)

def _layernorm(x, axis=-1, eps=1e-05):
    m = jnp.mean(x, axis=axis, keepdims=True)
    v = jnp.var(x, axis=axis, keepdims=True)
    return (x - m) / jnp.sqrt(v + eps)

def _scatter_add(tgt, idx, src, axis=0):
    return tgt.at[idx].add(src)

def _segment_sum(src, seg, n):
    return jax.ops.segment_sum(src, seg, n)
kernel_name = 'mk_flamingo_gated_d2_seqx_r8_ba23d6'

def setup_inputs(seed: int=0):
    np.random.seed(seed)
    _w = jnp.asarray

    def _rec_inputs():
        import jax
        import jax.numpy as jnp
        _rk = jax.random.key(seed)
        x = -0.000125 + 0.9999 * jax.random.normal(jax.random.fold_in(_rk, 1), (2, 512, 128), jnp.float32)
        _lenS = 512 - jax.random.randint(jax.random.fold_in(_rk, 7), (2,), 0, max(1, 512 // 4) + 1, jnp.int32)
        _lenS2 = 77 - jax.random.randint(jax.random.fold_in(_rk, 8), (2,), 0, max(1, 77 // 4) + 1, jnp.int32)
        _ctx_768P = jax.random.normal(jax.random.fold_in(_rk, 11), (2, 16, 96), jnp.float32)
        _ctx_768c = jax.random.dirichlet(jax.random.fold_in(_rk, 511), 0.3 * jnp.ones((16,), jnp.float32), (2, 77))
        _ctx_768t = jnp.einsum('bsk,bkd->bsd', _ctx_768c, _ctx_768P)
        _ctx_768t = _ctx_768t * jax.lax.rsqrt(jnp.mean(jnp.square(_ctx_768t)) + 1e-12) * 0.953939
        ctx_768 = 0.00272024 + 0.999456 * (_ctx_768t + 0.3 * jax.random.normal(jax.random.fold_in(_rk, 611), (2, 77, 96), jnp.float32))
        _g = jax.random.normal(jax.random.fold_in(_rk, 9001), (2, 2), jnp.float32)
        _g = jnp.sign(_g) * jnp.maximum(jnp.abs(_g), 1.0) + (_g == 0) * 1.0
        g_xattn = _g[0]
        g_ffn = _g[1]
        return (x, ctx_768, g_xattn, g_ffn)
    x, ctx_768, g_xattn, g_ffn = _rec_inputs()

    def _L0_xattn_setup():
        import jax, jax.numpy as jnp
        import numpy as np
        N_HEADS = 16
        DIM_EMBED = 128
        DIM_CROSS = 96
        DIM_HEAD = DIM_EMBED // N_HEADS
        key = jax.random.key(seed)
        ks = jax.random.split(key, 10)
        B, Sq, Sk = (8, 512, 77)
        s_e = 1.0 / np.sqrt(DIM_EMBED)
        s_c = 1.0 / np.sqrt(DIM_CROSS)
        return {'x': jax.random.normal(ks[0], (B, Sq, DIM_EMBED), jnp.float32), 'y': jax.random.normal(ks[1], (B, Sk, DIM_CROSS), jnp.float32), 'wq': jax.random.normal(ks[2], (DIM_EMBED, DIM_EMBED), jnp.float32) * s_e, 'bq': jax.random.normal(ks[3], (DIM_EMBED,), jnp.float32) * 0.01, 'wk': jax.random.normal(ks[4], (DIM_CROSS, DIM_EMBED), jnp.float32) * s_c, 'bk': jax.random.normal(ks[5], (DIM_EMBED,), jnp.float32) * 0.01, 'wv': jax.random.normal(ks[6], (DIM_CROSS, DIM_EMBED), jnp.float32) * s_c, 'bv': jax.random.normal(ks[7], (DIM_EMBED,), jnp.float32) * 0.01, 'wo': jax.random.normal(ks[8], (DIM_EMBED, DIM_EMBED), jnp.float32) * s_e, 'bo': jax.random.normal(ks[9], (DIM_EMBED,), jnp.float32) * 0.01}
    _L0_xattn_all = _L0_xattn_setup()
    _L0_xattn_in = {k: v for k, v in _L0_xattn_all.items() if k in ('wq', 'bq', 'wk', 'bk', 'wv', 'bv', 'wo', 'bo')}
    del _L0_xattn_all

    def _L0_ffn_setup():
        import jax, jax.numpy as jnp
        import numpy as np
        NUM_NOD = 6
        MAX_PREV = 5
        NUM_EDGE = 20
        D = 128
        H = 8
        LN_EPS = 1e-06

        def _layernorm(x, g, b):
            mu = jnp.mean(x, axis=-1, keepdims=True)
            var = jnp.mean(jnp.square(x - mu), axis=-1, keepdims=True)
            return (x - mu) * jax.lax.rsqrt(var + LN_EPS) * g + b

        def _mha(q, k, v, wq, wk, wv, wo):
            B, S, d = q.shape
            dh = d // H
            qh = (q @ wq).reshape(B, S, H, dh)
            kh = (k @ wk).reshape(B, S, H, dh)
            vh = (v @ wv).reshape(B, S, H, dh)
            scores = jnp.einsum('bqhd,bkhd->bhqk', qh, kh) / jnp.sqrt(jnp.asarray(dh, q.dtype))
            attn = jax.nn.softmax(scores, axis=-1)
            ctx = jnp.einsum('bhqk,bkhd->bqhd', attn, vh).reshape(B, S, d)
            return ctx @ wo
        key = jax.random.key(seed)
        ks = jax.random.split(key, 12)
        B, S = (8, 128)
        scale = 1.0 / np.sqrt(D)
        return {'inputs': jax.random.normal(ks[0], (B, S, D), jnp.float32), 'ew': jax.random.uniform(ks[1], (NUM_NOD, 3), jnp.float32), 'act_w': jax.random.uniform(ks[2], (NUM_NOD,), jnp.float32), 'We': jax.random.normal(ks[3], (NUM_EDGE, D, D), jnp.float32) * scale, 'be': jnp.zeros((NUM_EDGE, D), jnp.float32), 'Wq': jax.random.normal(ks[4], (NUM_NOD, D, D), jnp.float32) * scale, 'Wk': jax.random.normal(ks[5], (NUM_NOD, D, D), jnp.float32) * scale, 'Wv': jax.random.normal(ks[6], (NUM_NOD, D, D), jnp.float32) * scale, 'Wo': jax.random.normal(ks[7], (NUM_NOD, D, D), jnp.float32) * scale, 'ln_g': jnp.ones((D,), jnp.float32), 'ln_b': jnp.zeros((D,), jnp.float32)}
    _L0_ffn_all = _L0_ffn_setup()
    _L0_ffn_in = {k: v for k, v in _L0_ffn_all.items() if k in ('ew', 'act_w', 'We', 'be', 'Wq', 'Wk', 'Wv', 'Wo', 'ln_g', 'ln_b')}
    del _L0_ffn_all

    def _L1_xattn_setup():
        import jax, jax.numpy as jnp
        import numpy as np
        NUM_HEADS = 16
        CLAMP = 10000.0
        key = jax.random.key(seed)
        ks = jax.random.split(key, 8)
        B, Nq, Nkv, Cq, Ckv = (4, 256, 256, 128, 96)
        s_q = 1.0 / np.sqrt(Cq)
        s_kv = 1.0 / np.sqrt(Ckv)
        return {'query': jax.random.normal(ks[0], (B, Nq, Cq), jnp.float32), 'key_value': jax.random.normal(ks[1], (B, Nkv, Ckv), jnp.float32), 'Wq': jax.random.normal(ks[2], (Cq, Cq), jnp.float32) * s_q, 'bq': jnp.zeros((Cq,), jnp.float32), 'Wk': jax.random.normal(ks[3], (Ckv, Cq), jnp.float32) * s_kv, 'bk': jnp.zeros((Cq,), jnp.float32), 'Wv': jax.random.normal(ks[4], (Ckv, Cq), jnp.float32) * s_kv, 'bv': jnp.zeros((Cq,), jnp.float32), 'Wo': jax.random.normal(ks[5], (Cq, Cq), jnp.float32) * s_q, 'bo': jnp.zeros((Cq,), jnp.float32)}
    _L1_xattn_all = _L1_xattn_setup()
    _L1_xattn_in = {k: v for k, v in _L1_xattn_all.items() if k in ('Wq', 'bq', 'Wk', 'bk', 'Wv', 'bv', 'Wo', 'bo')}
    del _L1_xattn_all

    def _L1_ffn_setup():
        import jax, jax.numpy as jnp
        import numpy as np
        N_GROUP = 8
        TOPK_GROUP = 4
        TOPK = 8
        ROUTED_SCALE = 2.5
        B, S, D, F, E = (4, 256, 128, 64, 64)

        def _route(x, w_router, b_router):
            scores = jax.nn.sigmoid(jnp.einsum('bsd,de->bse', x, w_router)).astype(jnp.float32)
            swb = scores + b_router
            e = scores.shape[-1]
            group_scores = jnp.sum(jax.lax.top_k(swb.reshape(swb.shape[:-1] + (N_GROUP, -1)), 2)[0], axis=-1)
            group_idx = jax.lax.top_k(group_scores, TOPK_GROUP)[1]
            mask = jnp.any(jnp.arange(N_GROUP)[:, None] == group_idx[..., None, :], axis=-1)
            mask = jnp.repeat(mask, e // N_GROUP, axis=-1)
            masked_scores = jnp.where(mask, swb, 0.0)
            topk_idx = jax.lax.top_k(masked_scores, TOPK)[1]
            topk_w = jnp.take_along_axis(scores, topk_idx, axis=-1).astype(jnp.float32)
            topk_w = ROUTED_SCALE * topk_w / (jnp.sum(topk_w, axis=-1)[..., None] + 1e-20)
            return (topk_w, topk_idx)

        def _moe_forward(x, w_router, b_router, we_gate, we_up, we_down, ws_gate, ws_up, ws_down):
            b, s, d = x.shape
            e = we_gate.shape[0]
            topk_w, topk_idx = _route(x, w_router, b_router)
            x_flat = x.reshape(-1, d)
            idx_flat = topk_idx.reshape(-1)
            sort = jnp.argsort(idx_flat)
            tok = sort // TOPK
            x_sorted = x_flat[tok]
            group_sizes = jnp.bincount(idx_flat, length=e).astype(jnp.int32)
            g = jax.lax.ragged_dot(x_sorted, we_gate, group_sizes)
            u = jax.lax.ragged_dot(x_sorted, we_up, group_sizes)
            o = jax.lax.ragged_dot(jax.nn.silu(g) * u, we_down, group_sizes)
            w_sorted = topk_w.reshape(-1)[sort].astype(o.dtype)
            y = jnp.zeros_like(x_flat).at[tok].add(o * w_sorted[:, None])
            y = y.reshape(b, s, d)
            shared = jnp.einsum('btf,fd->btd', jax.nn.silu(jnp.einsum('btd,df->btf', x, ws_gate)) * jnp.einsum('btd,df->btf', x, ws_up), ws_down)
            return y + shared
        key = jax.random.key(seed)
        ks = jax.random.split(key, 10)
        sd = 1.0 / np.sqrt(D)
        sf = 1.0 / np.sqrt(F)
        return {'x': jax.random.normal(ks[0], (B, S, D), jnp.float32), 'w_router': jax.random.normal(ks[1], (D, E), jnp.float32) * sd, 'b_router': jax.random.normal(ks[2], (E,), jnp.float32) * 0.1, 'we_gate': jax.random.normal(ks[3], (E, D, F), jnp.float32) * sd, 'we_up': jax.random.normal(ks[4], (E, D, F), jnp.float32) * sd, 'we_down': jax.random.normal(ks[5], (E, F, D), jnp.float32) * sf, 'ws_gate': jax.random.normal(ks[6], (D, F), jnp.float32) * sd, 'ws_up': jax.random.normal(ks[7], (D, F), jnp.float32) * sd, 'ws_down': jax.random.normal(ks[8], (F, D), jnp.float32) * sf}
    _L1_ffn_all = _L1_ffn_setup()
    _L1_ffn_in = {k: v for k, v in _L1_ffn_all.items() if k in ('w_router', 'b_router', 'we_gate', 'we_up', 'we_down', 'ws_gate', 'ws_up', 'ws_down')}
    del _L1_ffn_all
    return {'x': x, 'ctx_768': ctx_768, 'g_xattn': g_xattn, 'g_ffn': g_ffn, 'L0_xattn_wq': _L0_xattn_in['wq'], 'L0_xattn_bq': _L0_xattn_in['bq'], 'L0_xattn_wk': _L0_xattn_in['wk'], 'L0_xattn_bk': _L0_xattn_in['bk'], 'L0_xattn_wv': _L0_xattn_in['wv'], 'L0_xattn_bv': _L0_xattn_in['bv'], 'L0_xattn_wo': _L0_xattn_in['wo'], 'L0_xattn_bo': _L0_xattn_in['bo'], 'L0_ffn_ew': _L0_ffn_in['ew'], 'L0_ffn_act_w': _L0_ffn_in['act_w'], 'L0_ffn_We': _L0_ffn_in['We'], 'L0_ffn_be': _L0_ffn_in['be'], 'L0_ffn_Wq': _L0_ffn_in['Wq'], 'L0_ffn_Wk': _L0_ffn_in['Wk'], 'L0_ffn_Wv': _L0_ffn_in['Wv'], 'L0_ffn_Wo': _L0_ffn_in['Wo'], 'L0_ffn_ln_g': _L0_ffn_in['ln_g'], 'L0_ffn_ln_b': _L0_ffn_in['ln_b'], 'L1_xattn_Wq': _L1_xattn_in['Wq'], 'L1_xattn_bq': _L1_xattn_in['bq'], 'L1_xattn_Wk': _L1_xattn_in['Wk'], 'L1_xattn_bk': _L1_xattn_in['bk'], 'L1_xattn_Wv': _L1_xattn_in['Wv'], 'L1_xattn_bv': _L1_xattn_in['bv'], 'L1_xattn_Wo': _L1_xattn_in['Wo'], 'L1_xattn_bo': _L1_xattn_in['bo'], 'L1_ffn_w_router': _L1_ffn_in['w_router'], 'L1_ffn_b_router': _L1_ffn_in['b_router'], 'L1_ffn_we_gate': _L1_ffn_in['we_gate'], 'L1_ffn_we_up': _L1_ffn_in['we_up'], 'L1_ffn_we_down': _L1_ffn_in['we_down'], 'L1_ffn_ws_gate': _L1_ffn_in['ws_gate'], 'L1_ffn_ws_up': _L1_ffn_in['ws_up'], 'L1_ffn_ws_down': _L1_ffn_in['ws_down']}

def reference(x, ctx_768, g_xattn, g_ffn, L0_xattn_wq, L0_xattn_bq, L0_xattn_wk, L0_xattn_bk, L0_xattn_wv, L0_xattn_bv, L0_xattn_wo, L0_xattn_bo, L0_ffn_ew, L0_ffn_act_w, L0_ffn_We, L0_ffn_be, L0_ffn_Wq, L0_ffn_Wk, L0_ffn_Wv, L0_ffn_Wo, L0_ffn_ln_g, L0_ffn_ln_b, L1_xattn_Wq, L1_xattn_bq, L1_xattn_Wk, L1_xattn_bk, L1_xattn_Wv, L1_xattn_bv, L1_xattn_Wo, L1_xattn_bo, L1_ffn_w_router, L1_ffn_b_router, L1_ffn_we_gate, L1_ffn_we_up, L1_ffn_we_down, L1_ffn_ws_gate, L1_ffn_ws_up, L1_ffn_ws_down):
    import jax
    import jax.numpy as jnp

    def _L0_xattn_ref(x, y, wq, bq, wk, bk, wv, bv, wo, bo):
        import jax, jax.numpy as jnp
        import numpy as np
        N_HEADS = 16
        DIM_EMBED = 128
        DIM_CROSS = 96
        DIM_HEAD = DIM_EMBED // N_HEADS
        B, Sq, E = x.shape
        H, D = (N_HEADS, DIM_HEAD)
        q = (x @ wq + bq).reshape(B, Sq, H, D).transpose(0, 2, 1, 3)
        k = (y @ wk + bk).reshape(B, -1, H, D).transpose(0, 2, 1, 3)
        v = (y @ wv + bv).reshape(B, -1, H, D).transpose(0, 2, 1, 3)
        scores = jnp.einsum('bhqd,bhkd->bhqk', q, k) / jnp.sqrt(jnp.asarray(D, x.dtype))
        attn = jax.nn.softmax(scores, axis=-1)
        out = jnp.einsum('bhqk,bhkd->bhqd', attn, v)
        out = out.transpose(0, 2, 1, 3).reshape(B, Sq, E)
        return out @ wo + bo

    def _L0_ffn_ref(inputs, ew, act_w, We, be, Wq, Wk, Wv, Wo, ln_g, ln_b):
        import jax, jax.numpy as jnp
        import numpy as np
        NUM_NOD = 6
        MAX_PREV = 5
        NUM_EDGE = 20
        D = 128
        H = 8
        LN_EPS = 1e-06

        def _layernorm(x, g, b):
            mu = jnp.mean(x, axis=-1, keepdims=True)
            var = jnp.mean(jnp.square(x - mu), axis=-1, keepdims=True)
            return (x - mu) * jax.lax.rsqrt(var + LN_EPS) * g + b

        def _mha(q, k, v, wq, wk, wv, wo):
            B, S, d = q.shape
            dh = d // H
            qh = (q @ wq).reshape(B, S, H, dh)
            kh = (k @ wk).reshape(B, S, H, dh)
            vh = (v @ wv).reshape(B, S, H, dh)
            scores = jnp.einsum('bqhd,bkhd->bhqk', qh, kh) / jnp.sqrt(jnp.asarray(dh, q.dtype))
            attn = jax.nn.softmax(scores, axis=-1)
            ctx = jnp.einsum('bhqk,bkhd->bqhd', attn, vh).reshape(B, S, d)
            return ctx @ wo
        nodes = {-1: inputs}
        lind = 0
        for c in range(NUM_NOD):
            nsrc = min(c + 1, MAX_PREV)
            snode = c - nsrc
            eq, ek, ev = (lind + nsrc - 1, lind, lind + nsrc // 2)
            in_q, in_k, in_v = (c - 1, snode, snode + nsrc // 2)
            q = ew[c, 0] * (nodes[in_q] @ We[eq] + be[eq])
            k = ew[c, 1] * (nodes[in_k] @ We[ek] + be[ek])
            v = ew[c, 2] * (nodes[in_v] @ We[ev] + be[ev])
            o = _mha(q, k, v, Wq[c], Wk[c], Wv[c], Wo[c])
            nodes[c] = act_w[c] * o + q
            lind += nsrc
        out = nodes[NUM_NOD - 1]
        return _layernorm(out, ln_g, ln_b)

    def _L1_xattn_ref(query, key_value, Wq, bq, Wk, bk, Wv, bv, Wo, bo):
        import jax, jax.numpy as jnp
        import numpy as np
        NUM_HEADS = 16
        CLAMP = 10000.0
        B, Nq, Cq = query.shape
        Nkv = key_value.shape[1]
        H = NUM_HEADS
        D = Cq // H
        scale = D ** (-0.5)
        q = (query @ Wq + bq).reshape(B, Nq, H, D).transpose(0, 2, 1, 3)
        k = (key_value @ Wk + bk).reshape(B, Nkv, H, D).transpose(0, 2, 1, 3)
        v = (key_value @ Wv + bv).reshape(B, Nkv, H, D).transpose(0, 2, 1, 3)
        attn = jnp.einsum('bhqd,bhkd->bhqk', q, k) * scale
        attn = jnp.clip(attn, -CLAMP, CLAMP)
        attn = jax.nn.softmax(attn, axis=-1)
        attn = jnp.where(jnp.any(jnp.isnan(attn)), jnp.asarray(1.0 / Nkv, attn.dtype), attn)
        x = jnp.einsum('bhqk,bhkd->bqhd', attn, v).reshape(B, Nq, Cq)
        return x @ Wo + bo

    def _L1_ffn_ref(x, w_router, b_router, we_gate, we_up, we_down, ws_gate, ws_up, ws_down):
        import jax, jax.numpy as jnp
        import numpy as np
        N_GROUP = 8
        TOPK_GROUP = 4
        TOPK = 8
        ROUTED_SCALE = 2.5
        B, S, D, F, E = (4, 256, 128, 64, 64)

        def _route(x, w_router, b_router):
            scores = jax.nn.sigmoid(jnp.einsum('bsd,de->bse', x, w_router)).astype(jnp.float32)
            swb = scores + b_router
            e = scores.shape[-1]
            group_scores = jnp.sum(jax.lax.top_k(swb.reshape(swb.shape[:-1] + (N_GROUP, -1)), 2)[0], axis=-1)
            group_idx = jax.lax.top_k(group_scores, TOPK_GROUP)[1]
            mask = jnp.any(jnp.arange(N_GROUP)[:, None] == group_idx[..., None, :], axis=-1)
            mask = jnp.repeat(mask, e // N_GROUP, axis=-1)
            masked_scores = jnp.where(mask, swb, 0.0)
            topk_idx = jax.lax.top_k(masked_scores, TOPK)[1]
            topk_w = jnp.take_along_axis(scores, topk_idx, axis=-1).astype(jnp.float32)
            topk_w = ROUTED_SCALE * topk_w / (jnp.sum(topk_w, axis=-1)[..., None] + 1e-20)
            return (topk_w, topk_idx)

        def _moe_forward(x, w_router, b_router, we_gate, we_up, we_down, ws_gate, ws_up, ws_down):
            b, s, d = x.shape
            e = we_gate.shape[0]
            topk_w, topk_idx = _route(x, w_router, b_router)
            x_flat = x.reshape(-1, d)
            idx_flat = topk_idx.reshape(-1)
            sort = jnp.argsort(idx_flat)
            tok = sort // TOPK
            x_sorted = x_flat[tok]
            group_sizes = jnp.bincount(idx_flat, length=e).astype(jnp.int32)
            g = jax.lax.ragged_dot(x_sorted, we_gate, group_sizes)
            u = jax.lax.ragged_dot(x_sorted, we_up, group_sizes)
            o = jax.lax.ragged_dot(jax.nn.silu(g) * u, we_down, group_sizes)
            w_sorted = topk_w.reshape(-1)[sort].astype(o.dtype)
            y = jnp.zeros_like(x_flat).at[tok].add(o * w_sorted[:, None])
            y = y.reshape(b, s, d)
            shared = jnp.einsum('btf,fd->btd', jax.nn.silu(jnp.einsum('btd,df->btf', x, ws_gate)) * jnp.einsum('btd,df->btf', x, ws_up), ws_down)
            return y + shared
        return _moe_forward(x, w_router, b_router, we_gate, we_up, we_down, ws_gate, ws_up, ws_down)
    x = x + jnp.tanh(g_xattn[0]) * _L0_xattn_ref(_layernorm(x, axis=-1), ctx_768, L0_xattn_wq, L0_xattn_bq, L0_xattn_wk, L0_xattn_bk, L0_xattn_wv, L0_xattn_bv, L0_xattn_wo, L0_xattn_bo)
    x = x + jnp.tanh(g_ffn[0]) * _L0_ffn_ref(_layernorm(x, axis=-1), L0_ffn_ew, L0_ffn_act_w, L0_ffn_We, L0_ffn_be, L0_ffn_Wq, L0_ffn_Wk, L0_ffn_Wv, L0_ffn_Wo, L0_ffn_ln_g, L0_ffn_ln_b)
    x = x + jnp.tanh(g_xattn[1]) * _L1_xattn_ref(_layernorm(x, axis=-1), ctx_768, L1_xattn_Wq, L1_xattn_bq, L1_xattn_Wk, L1_xattn_bk, L1_xattn_Wv, L1_xattn_bv, L1_xattn_Wo, L1_xattn_bo)
    x = x + jnp.tanh(g_ffn[1]) * _L1_ffn_ref(_layernorm(x, axis=-1), L1_ffn_w_router, L1_ffn_b_router, L1_ffn_we_gate, L1_ffn_we_up, L1_ffn_we_down, L1_ffn_ws_gate, L1_ffn_ws_up, L1_ffn_ws_down)
    return x

_drawn_inputs = setup_inputs


def setup_inputs(seed=0):
    import zlib

    import numpy as np

    out = dict(_drawn_inputs(seed))
    spreads = {'g_ffn': (-1.0, 0.2),
     'L0_ffn_be': (0.0, 0.1),
     'L0_ffn_ln_g': (1.0, 0.2),
     'L0_ffn_ln_b': (0.0, 0.1),
     'L1_xattn_bq': (0.0, 0.1),
     'L1_xattn_bk': (0.0, 2.0),
     'L1_xattn_bv': (0.0, 0.1),
     'L1_xattn_bo': (0.0, 0.1)}
    factors = {'L0_xattn_bq': 4.772,
     'L0_xattn_bk': 200.0,
     'L0_ffn_Wq': 64.0,
     'L0_ffn_Wk': 64.0,
     'L0_xattn_bv': 2.757,
     'L0_xattn_bo': 2.675}
    for name, (base, spread) in spreads.items():
        noise = np.random.default_rng([zlib.crc32(name.encode()), seed]).standard_normal(out[name].shape)
        drawn = base * np.exp(spread * noise) if base else spread * noise
        out[name] = jnp.asarray(drawn.astype(out[name].dtype))
    for name, factor in factors.items():
        out[name] = (out[name] * factor).astype(out[name].dtype)
    return out
```

```python
import concourse.bass as bass
from concourse import mybir
from contextlib import ExitStack


def flamingo_gated_two_layer(
    nc,
    x, ctx_t, g_all,
    x_wq, x_wkv, x_wo, x_bqk, x_bvo,
    f_wpost, f_wk, f_wv, f_ew, f_be, f_actw, ln_gb,
    w_router, b_router, moe_gate, moe_up, moe_down, sh_gate_up, sh_down,
    c_ident, c_ident_bf, c_sel_x, c_sel_f, c_sel_e, c_ident_h,
    out,
):
    f32, bf16, f16 = mybir.dt.float32, mybir.dt.bfloat16, mybir.dt.float16
    u32 = mybir.dt.uint32
    ALU = mybir.AluOpType
    ACT = mybir.ActivationFunctionType
    AX = mybir.AxisListType

    D = 128
    NT = x.shape[1]
    CH = 4
    QW = NT * 128 // CH
    B = 2
    SQ = NT * 128 // B
    SK = ctx_t.shape[2]
    DC = ctx_t.shape[1]
    NN = 6
    G = 4
    ROWS_M = 96
    KR = ROWS_M + 3 * G
    NP = 32
    NE = 64
    FE = 64
    SHIFT = 2048.0
    QPART = (0, 0, 0, 1, 1, 2)
    KPART = (0, 1, 2, 0, 1, 0)
    HEADS = {'X': 16, 'F': 8}
    DH = {'X': 8, 'F': 16}
    KT = {'X': 1, 'F': 4}
    KW = {'X': SK, 'F': 128}
    PR = 3

    def x_slots(L):
        st, n = [], 2 * CH

        def maxima(s, g):
            return [('s', 'X', L, s, g, t) for t in (0, 1)] + [('mp', 'X', L, s, g), ('mT', 'X', L, s, g), ('md', 'X', L, s, g)]

        for s in (0, 1):
            st += maxima(s, 0) + maxima(s, 1)
        prev = None
        for s in range(n):
            for g in (0, 1):
                st.append(('st', 'X', L, s, g, 0))
                if s + 2 < n:
                    st += maxima(s + 2, g)
                if prev:
                    st.append(('pv',) + prev)
                prev = ('X', L, s, g, 0)
                if g == 0 and s >= 1:
                    st.append(('otc', 'X', L, s - 1))
                if g == 1 and s >= 1:
                    st.append(('otT', 'X', L, s - 1))
                if g == 0 and s >= 3 and s % 2 == 1:
                    st.append(('ctxT', 'X', L, s // 2 - 1))
                if g == 1 and s >= 3 and s % 2 == 1:
                    st.append(('wox', L, s // 2 - 1))
        st += [('pv',) + prev, ('otc', 'X', L, n - 1), ('otT', 'X', L, n - 1), ('ctxT', 'X', L, CH - 1), ('wox', L, CH - 1)]
        return st

    def q_moves(kind, c, i):
        return [('qs', kind, c, i), ('qw', kind, c, i), ('qr', kind, c, i)]

    def x_begin(L):
        st = []
        for i in range(CH):
            st += [('ln', 'X', L, i), ('xT', 'X', L, i), ('xq', L, i), ('qs', 'X', L, i)]
            st += [('qw', 'X', L, i), ('qr', 'X', L, i)]
        return st

    def f_tiles(s, g):
        return [('s', 'F', 0, s, g, j) for j in range(8)]

    def f_slot(s):
        c, i = divmod(s, CH)
        last = CH * NN - 1
        st = []
        pc, pi = divmod(s - 1, CH)
        jobs = {0: [], 1: [('va', c, 1), ('vb', c, 1), ('ka', c + 1, 0), ('kb', c + 1, 0)],
                2: [('ka', c + 1, 1), ('kb', c + 1, 1)], 3: [('va', c + 1, 0), ('vb', c + 1, 0)]}[i]
        jobs = [j for j in jobs if j[1] < NN]
        at = {4: (0, 1, 5, 7), 2: (0, 7), 0: ()}[len(jobs)]
        for p in range(8):
            g, kt = divmod(p, 4)
            if p == 0:
                if i == 1:
                    st.append(('wl_post', c))
                if i == 2 and c + 1 < NN:
                    st.append(('wl_v', c + 1))
                if i == 3 and c + 1 < NN:
                    st.append(('wl_k', c + 2))
            st.append(('st', 'F', 0, s, g, kt))
            if s < last:
                st += [('s', 'F', 0, s + 1, g, 2 * kt), ('s', 'F', 0, s + 1, g, 2 * kt + 1)]
            if p == 1:
                st += [('mT', 'F', 0, s, 1), ('md', 'F', 0, s, 1)]
                if s >= 2 and (s - 2) // CH + 1 < NN:
                    qc, qi = divmod(s - 2, CH)
                    st += [('qw', 'F', qc + 1, qi)]
            if s >= 1:
                if p == 2:
                    st.append(('otT', 'F', 0, s - 1))
                    if s >= 2 and (s - 2) // CH + 1 < NN:
                        qc, qi = divmod(s - 2, CH)
                        st += [('qr', 'F', qc + 1, qi)]
                if p == 3:
                    st.append(('ctxT', 'F', 0, s - 1))
                if p == 4:
                    st.append(('wo', pc, pi))
                if p == 6 and pc + 1 < NN:
                    st += [('we', pc + 1, pi)]
                if p == 7 and pc + 1 < NN:
                    st += [('wq', pc + 1, pi), ('qs', 'F', pc + 1, pi)]
            for n, j in enumerate(jobs):
                if at[n] == p:
                    st.append(j)
                    if j[0] == 'kb':
                        st.append(('ks',) + ('F',) + j[1:])
            if i == 2 and p == 3 and c + 1 < NN:
                st += [('kw', 'F', c + 1, 0), ('kr', 'F', c + 1, 0)]
            if i == 3 and p == 3 and c + 1 < NN:
                st += [('kw', 'F', c + 1, 1)]
            if i == 0 and p == 3 and c >= 1:
                st += [('kr', 'F', c, 1)]
            if s < last:
                if p == 3:
                    st.append(('mp', 'F', 0, s + 1, 0))
                if p == 5:
                    st += [('mT', 'F', 0, s + 1, 0), ('md', 'F', 0, s + 1, 0)]
                if p == 7:
                    st.append(('mp', 'F', 0, s + 1, 1))
            if s or p:
                q = 8 * s + p - 1
                st.append(('pv', 'F', 0, q // 8, q % 8 // 4, q % 4))
            if p == 0 and s >= 1:
                st.append(('otc', 'F', 0, s - 1))
        return st

    before = [('init',)]
    for L in (0, 1):
        for b in (0, 1):
            before += [('xk', L, b), ('ks', 'X', L, b), ('kw', 'X', L, b), ('kr', 'X', L, b), ('xv', L, b)]
    before += x_begin(0) + x_slots(0)
    before += [('we_first',)]
    for i in range(CH):
        before += [('ln', 'F', 0, i), ('xT', 'F', 0, i), ('we', 0, i), ('wq', 0, i)] + q_moves('F', 0, i)
    for b in (0, 1):
        before += [('ka', 0, b), ('kb', 0, b), ('ks', 'F', 0, b), ('kw', 'F', 0, b), ('kr', 'F', 0, b)]
    before += [('va', 0, 0), ('vb', 0, 0), ('wl_k', 1)]
    before += f_tiles(0, 0) + [('mp', 'F', 0, 0, 0), ('mT', 'F', 0, 0, 0), ('md', 'F', 0, 0, 0)]
    before += f_tiles(0, 1) + [('mp', 'F', 0, 0, 1)] + f_slot(0)
    turns = [sum((f_slot(CH * c + i) for i in (1, 2, 3, 4)), []) for c in range(NN - 1)]
    after = sum((f_slot(CH * (NN - 1) + i) for i in (1, 2, 3)), [])
    after += [('pv', 'F', 0, 23, 1, 3), ('otc', 'F', 0, 23), ('otT', 'F', 0, 23), ('ctxT', 'F', 0, 23), ('wo', NN - 1, 3)]
    for i in range(CH):
        after += [('fin', i)]
    after += x_begin(1) + x_slots(1)
    for i in range(CH):
        after += [('ln', 'M', 0, i), ('xT', 'M', 0, i)]
    after += [('moe',)]
    everything = before + sum(turns, []) + after

    MISC = ('xk', 'xv', 'xT', 'xq', 'mT', 'otT', 'ctxT', 'wox', 'wo', 'we', 'wq', 'va', 'vb', 'ka', 'kb', 'fin')

    def keys_sem(way, st):
        return f'k_{way}{st[-1]}' if st[1] == 'F' else f'kx_{way}{st[-2]}{st[-1]}'

    group_at = {st[1:]: n for n, st in enumerate(st for st in everything if st[0] == 'mp')}

    def rows_sem(st):
        return f'm_in{group_at[st[1:5]] % 8}' if st[0] in ('md', 'st') else None

    def signals(st):
        k = st[0]
        if k in MISC:
            return (('misc_written', 1), ('misc_read', 1))
        if k in ('kw', 'kr'):
            return ((keys_sem('out', st), 16),) if k == 'kw' else ((keys_sem('in', st), 96),)
        return {
            'st': (('st_done', 1), ('exp_done', 1)), 'pv': (('pv_done', 1),), 's': (('s_done', 1), ('max_done', 1)),
            'mp': (('mparts', 1),), 'otc': (('ot_copied', 1),), 'qs': (('q_split', 1),), 'ks': (('k_split', 1),),
            'ln': (('var_ready', 1), ('rstd_ready', 1), ('xn_ready', 1)),
            'qw': ((f'q_out{st[-1]}', 16),), 'qr': ((f'q_in{st[-1]}', 96),),
            'md': ((rows_sem(st), 16),),
            'wl_post': (('wpost_in', 16),), 'wl_v': (('wv_in', 16),), 'wl_k': (('wk_in', 16),),
        }.get(k, ())

    level, total, ordinal = {}, {}, {}
    for st in everything:
        ordinal[st] = total.setdefault(st[0], 0)
        total[st[0]] += 1
        for name, by in signals(st):
            total[name] = total.get(name, 0) + by
            level[name, st] = total[name]
    per_turn = {}
    for st in turns[0]:
        for name, by in signals(st):
            per_turn[name] = per_turn.get(name, 0) + by

    def count(name, st, turn):
        return level[name, st] if turn is None else level[name, st] + turn * per_turn[name]

    def dyn(v, turn):
        return v if turn is None else v + turn

    kv_split_of = {}

    with ExitStack() as ctx:
        def sb(name, shape, dt=f32):
            return ctx.enter_context(nc.sbuf_tensor(name, shape, dt))

        def pb(name, shape):
            return ctx.enter_context(nc.psum_tensor(name, shape, f32))

        def sem(name):
            return ctx.enter_context(nc.semaphore(name))

        X = sb("x_tok", [128, NT, D])
        NODE = sb("node_t", [128, NN + 1, NT * 128])
        QA = [sb(f"qa{i}", [128, 16, QW], bf16) for i in range(CH)]
        KAF = [sb(f"kaf{b}", [128, 8, SQ], bf16) for b in (0, 1)]
        KAX = [[sb(f"kax{L}{b}", [128, 16, SK], bf16) for b in (0, 1)] for L in (0, 1)]
        VF = [sb(f"vf{b}", [128, 4, 8, 32]) for b in (0, 1)]
        VX = [[sb(f"vx{L}{b}", [128, 16, 32]) for b in (0, 1)] for L in (0, 1)]
        PT = [sb(f"pt{n}", [128, G, QW]) for n in range(PR)]
        NM = [sb(f"nm{n}", [128, 2, G]) for n in range(4)]
        MR = [sb(f"mr{n}", [128, 2, G]) for n in range(4)]
        MP = [sb(f"mp{n}", [128, 2, 3, G], bf16) for n in range(4)]
        MT = [sb(f"mt{n}", [3 * G, QW], bf16) for n in range(4)]
        OTS = [sb(f"ots{n}", [128, 2, QW]) for n in range(2)]
        REC = [sb(f"rec{n}", [128, 2, 8]) for n in range(2)]
        CTX = [sb(f"ctx{n}", [128, 2, D]) for n in range(2)]
        CTXT = [sb(f"ctxt{n}", [128, QW]) for n in range(2)]
        QT = [sb(f"qt{i}", [128, QW]) for i in range(CH)]
        QX = [sb(f"qx{n}", [128, QW]) for n in range(2)]
        QP = [sb(f"qp{n}", [128, 3, QW], bf16) for n in range(2)]
        QR = sb("qr", [128, QW])
        KIN = sb("kin", [128, SQ])
        KX = sb("kx", [128, SQ])
        KP = sb("kp", [128, 3, SQ], bf16)
        KRS = sb("krs", [128, SQ])
        BNS = sb("bns", [128, 2, 6])
        MV = [sb(f"mv{n}", [128, 2, 2]) for n in range(2)]
        VE = [sb(f"ve{n}", [128, 2]) for n in range(2)]
        RSTD = [sb(f"rstd{n}", [128, 2]) for n in range(2)]
        XN = [sb(f"xn{n}", [128, 2, D]) for n in range(2)]
        NEGHALF = sb("neghalf", [128, 2])
        CT = sb("ctx_in", [DC, B, SK])
        XW = sb("xw", [128, 2, 4, D])
        XB = sb("xb", [128, 2, 2])
        XBV = sb("xbv", [128, 2, 2, D])
        WPOST = sb("wpost", [128, 3, D])
        WK = sb("wk", [128, 2, D])
        WV = sb("wv", [128, 2, D])
        EW = sb("ew", [128, 3 * NN])
        BE = sb("be", [128, 3 * NN])
        EWBE = sb("ewbe", [128, 3 * NN])
        ACTW = sb("actw", [128, NN])
        GALL = sb("gall", [128, 4])
        TG = sb("tg", [128, 4])
        LNGB = sb("lngb", [128, 2, D])
        IDENT = sb("ident", [128, 128])
        IDB = sb("identb", [128, 128], bf16)
        IDH = sb("identh", [128, 128], f16)
        WR = sb("wr", [128, NE])
        BR = sb("br", [128, NE])
        WG = sb("wg", [128, NE * FE])
        WU = sb("wu", [128, NE * FE])
        WS = sb("ws", [128, 2 * FE])
        SELE = sb("sele", [128, NP, 128], f16)

        WD = NODE[:, 1:5, :].rearrange("p a t -> p (a t)")
        WSD = NODE[0:FE, 5, 0:D]
        MSC = [NODE[:, 6, 0:512], NODE[:, 6, 512:1024]]
        def qa_f32(i, lo, n):
            return QA[i][:, :, :].rearrange("p h t -> p (h t)").bitcast(f32)[:, lo:lo + n]

        ST = [pb(f"st{n}", [128, G, QW]) for n in range(2)]
        S = [pb(f"s{n}", [128, 512]) for n in range(2)]
        OT = pb("ot", [128, 2, QW])
        MISCB = pb("misc", [128, 512])

        names = ['load_x', 'load_c', 'load_w', 'load_f', 'load_m', 'load_d', 'zeroed', 'ready', 'dve_step', 'act_step', 'pool_step',
                 'tg_ready', 'gu_done', 'silu_done', 'ht_done', 'wb_done', 'y_done', 'yt_copied', 'y_tok', 'y_added', 'out_done',
                 'log_done', 'sig_done', 'w_ready', 'wT_done', 'wT_copied', 'fvar_ready', 'frstd_ready'] + [n for n in total if n not in {s[0] for s in everything}]
        sems = {n: sem(n) for n in dict.fromkeys(names)}

        qd = [nc.dram_tensor(f"q_parts{i}", (3, 128, QW), bf16, kind="Internal").ap() for i in range(CH)]
        kd = [nc.dram_tensor(f"k_parts{b}", (3, 128, SQ), bf16, kind="Internal").ap() for b in (0, 1)]
        kdx = [[nc.dram_tensor(f"kx_parts{L}{b}", (3, 128, SK), bf16, kind="Internal").ap() for b in (0, 1)] for L in (0, 1)]

        block = ctx.enter_context(nc.Block())

        def prior(kind, st, back=1):
            n = ordinal[st] - back
            return by_ordinal[kind][n] if n >= 0 else None

        by_ordinal = {}
        for s_ in everything:
            by_ordinal.setdefault(s_[0], []).append(s_)
        misc_order = [s_ for s_ in everything if s_[0] in MISC]
        misc_at = {s_: n for n, s_ in enumerate(misc_order)}
        tile_order = by_ordinal['st']
        group_order = by_ordinal['mp']

        def chain_of(kind, s):
            return s // 2 if kind == 'X' else s % CH

        def head0(kind, s, g):
            return (8 * (s % 2) if kind == 'X' else 0) + G * g

        def run(eng, emit):
            for st in before:
                emit(st, None)
            if LOOP:
                for turn in eng.Fori(0, NN - 1):
                    for st in turns[0]:
                        emit(st, turn)
            else:
                for t in turns:
                    for st in t:
                        emit(st, None)
            for st in after:
                emit(st, None)

        def node(idx, lo, n, turn_expr=None):
            if isinstance(idx, int):
                return NODE[:, idx, lo:lo + n]
            return NODE[:, :, :].rearrange("p a t -> p (a t)")[:, bass.ds(idx * (NT * 128) + lo, n)]

        def prior_otc(kind, L, s):
            n = ordinal['otc', kind, L, s]
            return by_ordinal['otc'][n - 1] if n else None

        WP = QA[3][:, 0:4, :].rearrange("p h t -> p (h t)").bitcast(f16).rearrange("p (t a e) -> p t a e", t=NT, a=2)
        WT = QA[3][:, 4:8, :].rearrange("p h t -> p (h t)").bitcast(f16)
        SG = [qa_f32(0, 0, 512), qa_f32(0, 512, 512)]
        T1 = [qa_f32(0, 1024, 512), qa_f32(0, 1536, 512)]
        HT = [qa_f32(1, 0, 512), qa_f32(1, 512, 512)]
        YT = qa_f32(1, 1024, 1024)
        def r3(i, lo):
            return qa_f32(i, lo, 512).rearrange("p (t e) -> p t e", t=NT)
        SC, SWB, GT, EQ = (r3(2, 512 * n) for n in range(4))
        MSK, CUM, ONE = r3(3, 1024), r3(3, 1536), MSC[1]
        M8 = MSC[0].rearrange("p (t g k) -> p t g k", t=NT, g=8)
        SM = MSC[1]

        @block.tensor
        def _(pe):
            W = lambda name, st, turn: pe.wait_ge(sems[name], count(name, st, turn))

            def emit(st, turn):
                k = st[0]
                if k in MISC:
                    n = misc_at[st]
                    if n:
                        W('misc_read', misc_order[n - 1], turn)
                if k == 'init':
                    pe.wait_ge(sems['load_c'], 16 * 12)
                    pe.wait_ge(sems['load_w'], 16 * 3)
                    pe.wait_ge(sems['ready'], 1)
                elif k == 'xk':
                    _, L, b = st
                    nc.tensor.matmul(MISCB[:, 0:SK], XW[0:DC, L, 1, :], CT[:, b, :], start=True, stop=True).then_inc(sems['misc_written'], 1)
                elif k == 'xv':
                    _, L, b = st
                    nc.tensor.matmul(MISCB[0:SK, 0:D], CT[:, b, :], XW[0:DC, L, 2, :], start=True, stop=True).then_inc(sems['misc_written'], 1)
                elif k == 'xT':
                    i = st[3]
                    W('xn_ready', ('ln',) + st[1:], turn)
                    n = ordinal['ln', st[1], st[2], i] % 2
                    for t in (0, 1):
                        last = nc.tensor.transpose(MISCB[:, 128 * t:128 * t + 128], XN[n][:, t, :], IDENT[:])
                    last.then_inc(sems['misc_written'], 1)
                elif k == 'xq':
                    _, L, i = st
                    W('misc_read', ('xT', 'X', L, i), turn)
                    nc.tensor.matmul(MISCB[:, 0:QW], XW[:, L, 0, :], node(0, QW * i, QW), start=True, stop=True).then_inc(sems['misc_written'], 1)
                elif k == 's':
                    _, kind, L, s, g, j = st
                    i, b = chain_of(kind, s), chain_of(kind, s) // 2
                    n = ordinal[st]
                    if n >= 2:
                        W('max_done', by_ordinal['s'][n - 2], turn)
                    if g == 0 and j == 0:
                        if kind == 'X':
                            W(f'q_in{i}', ('qr', 'X', L, i), turn)
                            W(f'kx_in{L}{b}', ('kr', 'X', L, b), turn)
                        else:
                            W(f'q_in{i}', ('qr', 'F', s // CH, i), turn)
                            W(f'k_in{b}', ('kr', 'F', s // CH, b), turn)
                    if kind == 'X':
                        for r in range(G):
                            h = head0(kind, s, g) + r
                            last = nc.tensor.matmul(S[n % 2][:, r * SK:(r + 1) * SK], QA[i][0:48, h, 128 * j:128 * j + 128],
                                                    KAX[L][b][0:48, h, :], start=True, stop=True)
                        last.then_inc(sems['s_done'], 1)
                    else:
                        t, r = divmod(j, 4)
                        h = G * g + r
                        nc.tensor.matmul(S[n % 2][:], QA[i][0:ROWS_M, h, 128 * t:128 * t + 128], KAF[b][0:ROWS_M, h, :],
                                         start=True, stop=True).then_inc(sems['s_done'], 1)
                elif k == 'mT':
                    n = group_at[st[1:]]
                    W('mparts', ('mp',) + st[1:], turn)
                    mb = MISCB[:, :].bitcast(bf16)
                    for t in (0, 1):
                        last = nc.tensor.transpose(mb[0:3 * G, 128 * t:128 * t + 128], MP[n % 4][:, t, :, :].rearrange("p a r -> p (a r)"), IDB[:])
                    last.then_inc(sems['misc_written'], 1)
                elif k == 'st':
                    _, kind, L, s, g, kt = st
                    i = chain_of(kind, s)
                    b = i // 2
                    n = ordinal[st]
                    if n >= 2:
                        W('exp_done', tile_order[n - 2], turn)
                    if kt == 0:
                        W(rows_sem(st), ('md', kind, L, s, g), turn)
                    for r in range(G):
                        h = head0(kind, s, g) + r
                        if kind == 'X':
                            last = nc.tensor.matmul(ST[n % 2][0:SK, r, :], KAX[L][b][0:KR, h, :], QA[i][0:KR, h, :], start=True, stop=True)
                        else:
                            last = nc.tensor.matmul(ST[n % 2][:, r, :], KAF[b][0:KR, h, 128 * kt:128 * kt + 128], QA[i][0:KR, h, :], start=True, stop=True)
                    last.then_inc(sems['st_done'], 1)
                elif k == 'pv':
                    _, kind, L, s, g, kt = st
                    i = chain_of(kind, s)
                    b = i // 2
                    tile = ('st',) + st[1:]
                    n = ordinal[tile]
                    W('exp_done', tile, turn)
                    if g == 0 and kt == 0:
                        before_it = prior_otc(kind, L, s)
                        if before_it:
                            W('ot_copied', before_it, turn)
                        if kind == 'F':
                            W('misc_read', ('vb', s // CH, b), turn)
                        else:
                            W('misc_read', ('xv', L, b), turn)
                    for r in range(G):
                        h = head0(kind, s, g) + r
                        if kind == 'X':
                            v, p = VX[L][b][0:SK, h, :], PT[n % PR][0:SK, r, :]
                        else:
                            v, p = VF[b][:, kt, h, :], PT[n % PR][:, r, :]
                        last = nc.tensor.matmul(OT[32 * r:32 * r + 32, g, :], v, p, start=(kt == 0), stop=(kt == KT[kind] - 1))
                    last.then_inc(sems['pv_done'], 1)
                elif k == 'otT':
                    _, kind, L, s = st
                    otc = ('otc',) + st[1:]
                    W('ot_copied', otc, turn)
                    o = OTS[ordinal[otc] % 2]
                    for t in (0, 1):
                        for g in (0, 1):
                            last = nc.tensor.transpose(MISCB[:, (2 * t + g) * 128:(2 * t + g) * 128 + 128], o[:, g, 128 * t:128 * t + 128], IDENT[:])
                    last.then_inc(sems['misc_written'], 1)
                elif k == 'ctxT':
                    i = st[3]
                    n = i % 2
                    for t in (0, 1):
                        last = nc.tensor.transpose(MISCB[:, 128 * t:128 * t + 128], CTX[n][:, t, :], IDENT[:])
                    last.then_inc(sems['misc_written'], 1)
                elif k == 'wox':
                    _, L, i = st
                    for t in (0, 1):
                        last = nc.tensor.matmul(MISCB[:, 128 * t:128 * t + 128], CTXT[i % 2][:, 128 * t:128 * t + 128], XW[:, L, 3, :], start=(t == 0), stop=True, skip_group_check=True)
                    last.then_inc(sems['misc_written'], 1)
                elif k == 'wo':
                    _, c, i = st
                    if i == 0:
                        W('wpost_in', ('wl_post', c), turn)
                    nc.tensor.matmul(MISCB[:, 0:QW], WPOST[:, 0, :], CTXT[i % 2][:, :], start=True, stop=True).then_inc(sems['misc_written'], 1)
                elif k == 'we_first':
                    pe.wait_ge(sems['load_f'], 16 * 8)
                elif k == 'we':
                    _, c, i = st
                    src = node(dyn(c, turn), QW * i, QW)
                    nc.tensor.matmul(MISCB[:, 0:QW], WPOST[:, 1, :], src, start=True, stop=True).then_inc(sems['misc_written'], 1)
                elif k == 'wq':
                    _, c, i = st
                    nc.tensor.matmul(MISCB[:, 0:QW], WPOST[:, 2, :], QT[i][:, :], start=True, stop=True).then_inc(sems['misc_written'], 1)
                elif k == 'ka':
                    _, c, b = st
                    if c and b == 0:
                        W('wk_in', ('wl_k', c), turn)
                    nc.tensor.matmul(MISCB[:], WK[:, 0, :], node(dyn(c, turn) // (NN - 1), SQ * b, SQ), start=True, stop=True).then_inc(sems['misc_written'], 1)
                elif k == 'kb':
                    nc.tensor.matmul(MISCB[:], WK[:, 1, :], KIN[:], start=True, stop=True).then_inc(sems['misc_written'], 1)
                elif k == 'va':
                    _, c, b = st
                    if c and b == 0:
                        W('wv_in', ('wl_v', c), turn)
                    nc.tensor.matmul(MISCB[:], WV[:, 0, :], node((dyn(c, turn) + 1) // 2, SQ * b, SQ), start=True, stop=True).then_inc(sems['misc_written'], 1)
                elif k == 'vb':
                    for kt in range(4):
                        last = nc.tensor.matmul(MISCB[:, 128 * kt:128 * kt + 128], KIN[:, 128 * kt:128 * kt + 128], WV[:, 1, :], start=(kt == 0), stop=True, skip_group_check=True)
                    last.then_inc(sems['misc_written'], 1)
                elif k == 'fin':
                    i = st[1]
                    for t in (0, 1):
                        last = nc.tensor.transpose(MISCB[:, 128 * t:128 * t + 128], node(NN, QW * i + 128 * t, 128), IDENT[:])
                    last.then_inc(sems['misc_written'], 1)
                elif k == 'moe':
                    pe_moe()

            def pe_moe():
                W('misc_read', ('xT', 'M', 0, CH - 1), None)
                pe.wait_ge(sems['load_m'], 16 * 6)
                for t in range(NT):
                    last = nc.tensor.matmul(MISCB[:, NE * t:NE * t + NE], node(0, 128 * t, 128), WR[:, :], start=(t == 0), stop=True, skip_group_check=True)
                last.then_inc(sems['log_done'], 1)
                pe.wait_ge(sems['w_ready'], 1)
                mh = MISCB[:, :].bitcast(f16)
                for t in range(NT):
                    last = nc.tensor.transpose(mh[:, 128 * t:128 * t + 128], WP[:, t, :, :].rearrange("p a e -> p (a e)"), IDH[:])
                last.then_inc(sems['wT_done'], 1)
                pe.wait_ge(sems['wT_copied'], 1)
                pe.wait_ge(sems['load_d'], 32)

                def down(n):
                    p, h = divmod(n, 2)
                    rows = 128 if p < NP else FE
                    pe.wait_ge(sems['ht_done'], n + 1)
                    y = OT[:, :, :].rearrange("p a t -> p (a t)") if h == 0 else MISCB[:, :]
                    w = WD[:, 128 * p:128 * p + 128] if p < NP else WSD
                    last = nc.tensor.matmul(y, w, HT[n % 2][0:rows, :], start=(p == 0), stop=(p == NP))
                    if p == NP:
                        last.then_inc(sems['y_done'], 1)

                for n in range(2 * NP + 2):
                    p, h = divmod(n, 2)
                    tok = node(0, 512 * h, 512)
                    gb, ub = (ST[n % 2][:, 0:2, :].rearrange("p a t -> p (a t)"), ST[n % 2][:, 2:4, :].rearrange("p a t -> p (a t)"))
                    if n >= 2:
                        pe.wait_ge(sems['ht_done'], n - 1)
                    if p < NP:
                        nc.tensor.matmul(gb, WG[:, 128 * p:128 * p + 128], tok, start=True, stop=True).then_inc(sems['gu_done'], 1)
                        nc.tensor.matmul(ub, WU[:, 128 * p:128 * p + 128], tok, start=True, stop=True)
                        nc.tensor.matmul(S[n % 2][:], SELE[:, p, :], WT[:, 512 * h:512 * h + 512], start=True, stop=True).then_inc(sems['wb_done'], 1)
                    else:
                        nc.tensor.matmul(gb[0:FE, :], WS[:, 0:FE], tok, start=True, stop=True).then_inc(sems['gu_done'], 1)
                        nc.tensor.matmul(ub[0:FE, :], WS[:, FE:2 * FE], tok, start=True, stop=True).then_inc(sems['wb_done'], 1)
                    if n >= 1:
                        down(n - 1)
                down(2 * NP + 1)
                pe.wait_ge(sems['yt_copied'], 2)
                for t in range(NT):
                    y = (ST[0] if t < 4 else ST[1])[:, 0:2, :].rearrange("p a t -> p (a t)")
                    last = nc.tensor.transpose(y[:, 128 * (t % 4):128 * (t % 4) + 128], YT[:, 128 * t:128 * t + 128], IDENT[:])
                    if t % 4 == 3:
                        last.then_inc(sems['y_tok'], 1)

            run(pe, emit)

        @block.scalar
        def _(act):
            W = lambda name, st, turn: act.wait_ge(sems[name], count(name, st, turn))

            def emit(st, turn):
                k = st[0]
                if k == 'init':
                    act.wait_ge(sems['load_c'], 16 * 12)
                    act.wait_ge(sems['load_w'], 16 * 3)
                    nc.scalar.activation(TG[:], GALL[:], ACT.Tanh).then_inc(sems['tg_ready'], 1)
                elif k == 'xk':
                    _, L, b = st
                    W('misc_written', st, turn)
                    if ordinal[st]:
                        W('k_split', by_ordinal['ks'][ordinal[st] - 1], turn)
                    nc.scalar.activation(KX[:, 0:SK], MISCB[:, 0:SK], ACT.Identity, bias=XB[:, L, 1:2]).then_inc(sems['misc_read'], 1)
                elif k == 'xT':
                    i = st[3]
                    W('misc_written', st, turn)
                    nc.scalar.activation(node(0, QW * i, QW), MISCB[:, 0:QW], ACT.Copy).then_inc(sems['misc_read'], 1)
                elif k in ('xq', 'wq'):
                    W('misc_written', st, turn)
                    q = ('qs', 'X' if k == 'xq' else 'F') + st[1:]
                    n = ordinal[q]
                    if n >= 2:
                        W('q_split', by_ordinal['qs'][n - 2], turn)
                    if k == 'xq':
                        nc.scalar.activation(QX[n % 2][:], MISCB[:, 0:QW], ACT.Identity, bias=XB[:, st[1], 0:1]).then_inc(sems['misc_read'], 1)
                    else:
                        nc.scalar.activation(QX[n % 2][:], MISCB[:, 0:QW], ACT.Copy).then_inc(sems['misc_read'], 1)
                elif k == 'mT':
                    n = group_at[st[1:]]
                    W('misc_written', st, turn)
                    if n >= 4:
                        W(rows_sem(('md',) + group_order[n - 4][1:]), ('md',) + group_order[n - 4][1:], turn)
                    nc.scalar.activation(MT[n % 4][:], MISCB[:, :].bitcast(bf16)[0:3 * G, 0:QW], ACT.Copy).then_inc(sems['misc_read'], 1)
                elif k == 'st':
                    _, kind, L, s, g, kt = st
                    n = ordinal[st]
                    W('st_done', st, turn)
                    if n >= PR:
                        W('pv_done', ('pv',) + tile_order[n - PR][1:], turn)
                    rows = SK if kind == 'X' else 128
                    nc.scalar.activation(PT[n % PR][0:rows, :, :], ST[n % 2][0:rows, :, :], ACT.Exp, scale=float(DH[kind]) ** -0.5).then_inc(sems['exp_done'], 1)
                elif k == 'otc':
                    _, kind, L, s = st
                    W('pv_done', ('pv', kind, L, s, 1, KT[kind] - 1), turn)
                    n = ordinal[st]
                    if n >= 2:
                        W('misc_written', ('otT',) + by_ordinal['otc'][n - 2][1:], turn)
                    nc.scalar.activation(OTS[n % 2][:, :, :], OT[:, :, :], ACT.Copy).then_inc(sems['ot_copied'], 1)
                elif k == 'ctxT':
                    W('misc_written', st, turn)
                    nc.scalar.activation(CTXT[st[3] % 2][:], MISCB[:, 0:QW], ACT.Copy).then_inc(sems['misc_read'], 1)
                elif k in ('ka', 'va'):
                    _, c, b = st
                    W('misc_written', st, turn)
                    col = dyn(c, turn) * 3 + (1 if k == 'ka' else 2)
                    nc.scalar.activation(KIN[:], MISCB[:], ACT.Identity, scale=EW[:, bass.ds(col, 1)], bias=EWBE[:, bass.ds(col, 1)]).then_inc(sems['misc_read'], 1)
                elif k == 'kb':
                    _, c, b = st
                    W('misc_written', st, turn)
                    ks = ('ks', 'F', c, b)
                    W('k_split', by_ordinal['ks'][ordinal[ks] - 1], turn)
                    nc.scalar.activation(KX[:], MISCB[:], ACT.Copy).then_inc(sems['misc_read'], 1)
                elif k == 'vb':
                    _, c, b = st
                    W('misc_written', st, turn)
                    if c:
                        W('pv_done', ('pv', 'F', 0, CH * (c - 1) + 2 * b + 1, 1, 3), turn)
                    nc.scalar.activation(VF[b][:, :, :, 0:16], MISCB[:, :].rearrange("p (k h d) -> p k h d", k=4, h=8), ACT.Copy).then_inc(sems['misc_read'], 1)
                elif k == 'moe':
                    act_moe()

            def act_moe():
                act.wait_ge(sems['log_done'], 1)
                nc.scalar.activation(SC, MISCB[:, :].rearrange("p (t e) -> p t e", t=NT), ACT.Tanh, scale=0.5).then_inc(sems['sig_done'], 1)
                act.wait_ge(sems['wT_done'], 1)
                nc.scalar.activation(WT, MISCB[:, :].bitcast(f16), ACT.Copy).then_inc(sems['wT_copied'], 1)
                for n in range(2 * NP + 2):
                    rows = 128 if n // 2 < NP else FE
                    act.wait_ge(sems['gu_done'], n + 1)
                    nc.scalar.activation(SG[n % 2][0:rows, :], ST[n % 2][0:rows, 0:2, :].rearrange("p a t -> p (a t)"), ACT.Silu).then_inc(sems['silu_done'], 1)
                act.wait_ge(sems['y_done'], 2)
                nc.scalar.activation(YT[:, 0:512], OT[:, :, :].rearrange("p a t -> p (a t)"), ACT.Copy).then_inc(sems['yt_copied'], 1)

            run(act, emit)

        @block.vector
        def _(dve):
            W = lambda name, st, turn: dve.wait_ge(sems[name], count(name, st, turn))
            steps_in_turn = [0]
            done = [0, 0]

            def link(ins, turn):
                ins.then_inc(sems['dve_step'], 1)
                done[0] += 1
                v = done[0]
                if turn is not None:
                    v = v + turn * dve_per_turn
                dve.wait_ge(sems['dve_step'], v)

            dve_per_turn = sum({'mp': 3, 'otT': 1}.get(s_[0], 0) for s_ in turns[0])

            def emit(st, turn):
                k = st[0]
                if k == 'init':
                    for b in (0, 1):
                        nc.vector.memset(VF[b][:, :, :, 16:32], 1.0)
                    nc.vector.memset(NEGHALF[:], -0.5)
                    for L in (0, 1):
                        for b in (0, 1):
                            link(nc.vector.memset(VX[L][b][:, :, :], 1.0), turn)
                    dve.wait_ge(sems['load_c'], 16 * 12)
                    dve.wait_ge(sems['load_f'], 16 * 8)
                    link(nc.vector.tensor_tensor(EWBE[:], EW[:], BE[:], ALU.mult), turn)
                    nc.vector.memset(REC[0][:, :, :], 0.0).then_inc(sems['ready'], 1)
                    dve.wait_ge(sems['load_x'], 16)
                    dve.wait_ge(sems['tg_ready'], 1)
                elif k == 'xv':
                    _, L, b = st
                    W('misc_written', st, turn)
                    nc.vector.tensor_tensor(VX[L][b][0:SK, :, 0:8], MISCB[0:SK, 0:D].rearrange("p (h d) -> p h d", h=16),
                                            XBV[0:SK, L, 0, :].rearrange("p (h d) -> p h d", h=16), ALU.add).then_inc(sems['misc_read'], 1)
                elif k == 'ln':
                    _, kind, L, i = st
                    n = ordinal[st] % 2
                    if ordinal[st] >= 2:
                        W('misc_written', ('xT',) + by_ordinal['ln'][ordinal[st] - 2][1:], turn)
                    norm(st, [X[:, 2 * i + t, :] for t in (0, 1)], [XN[n][:, t, :] for t in (0, 1)], 1e-5, n, turn)
                elif k == 's':
                    _, kind, L, s, g, j = st
                    n = ordinal[st]
                    m = NM[group_at[kind, L, s, g] % 4]
                    W('s_done', st, turn)
                    if kind == 'X':
                        nc.vector.tensor_reduce(m[:, j, :], S[n % 2][:, 0:G * SK].rearrange("p (r t) -> p r t", r=G), AX.X, ALU.max, negate=True).then_inc(sems['max_done'], 1)
                    else:
                        t, r = divmod(j, 4)
                        nc.vector.tensor_reduce(m[:, t, r:r + 1], S[n % 2][:], AX.X, ALU.max, negate=True).then_inc(sems['max_done'], 1)
                elif k == 'mp':
                    _, kind, L, s, g = st
                    n = group_at[st[1:]] % 4
                    W('max_done', ('s', kind, L, s, g, 1 if kind == 'X' else 7), turn)
                    link(nc.vector.tensor_copy(MP[n][:, :, 0, :], NM[n][:, :, :]), turn)
                    link(nc.vector.tensor_tensor(MR[n][:, :, :], NM[n][:, :, :], MP[n][:, :, 0, :], ALU.subtract), turn)
                    link(nc.vector.tensor_copy(MP[n][:, :, 1, :], MR[n][:, :, :]), turn)
                    nc.vector.tensor_tensor(MP[n][:, :, 2, :], MR[n][:, :, :], MP[n][:, :, 1, :], ALU.subtract).then_inc(sems['mparts'], 1)
                elif k == 'otT':
                    _, kind, L, s = st
                    n = ordinal[st]
                    i = chain_of(kind, s)
                    d = DH[kind]
                    W('misc_written', st, turn)
                    o = MISCB[:, :].rearrange("p (t h e) -> p t h e", t=2, h=8)
                    link(nc.vector.reciprocal(REC[n % 2][:, :, :], o[:, :, :, d]), turn)
                    lo = 64 * (s % 2) if kind == 'X' else 0
                    c = CTX[i % 2][:, :, lo:lo + 8 * d].rearrange("p t (h e) -> p t h e", h=8)
                    nc.vector.tensor_tensor(c, o[:, :, :, 0:d], REC[n % 2][:, :, :].unsqueeze(3).broadcast_to([128, 2, 8, d]), ALU.mult).then_inc(sems['misc_read'], 1)
                elif k == 'wox':
                    _, L, i = st
                    W('misc_written', st, turn)
                    n = i % 2
                    link(nc.vector.tensor_tensor(XN[n][:, :, :], MISCB[:, 0:QW].rearrange("p (t d) -> p t d", t=2),
                                                 XBV[:, L, 1, :].unsqueeze(1).broadcast_to([128, 2, D]), ALU.add), turn)
                    link(nc.vector.scalar_tensor_tensor(X[:, 2 * i:2 * i + 2, :], XN[n][:, :, :], TG[:, L:L + 1], X[:, 2 * i:2 * i + 2, :], ALU.mult, ALU.add), turn)
                    nc.vector.memset(REC[0][:, :, 0:1], 1.0).then_inc(sems['misc_read'], 1)
                elif k == 'wo':
                    _, c, i = st
                    W('misc_written', st, turn)
                    nc.vector.scalar_tensor_tensor(node(dyn(c, turn) + 1, QW * i, QW), MISCB[:, 0:QW], ACTW[:, bass.ds(dyn(c, turn), 1)], QT[i][:, :], ALU.mult, ALU.add).then_inc(sems['misc_read'], 1)
                elif k == 'we':
                    _, c, i = st
                    W('misc_written', st, turn)
                    col = dyn(c, turn) * 3
                    nc.vector.tensor_scalar(QT[i][:, :], MISCB[:, 0:QW], BE[:, bass.ds(col, 1)], EW[:, bass.ds(col, 1)], ALU.add, ALU.mult).then_inc(sems['misc_read'], 1)
                elif k == 'fin':
                    i = st[1]
                    n = i % 2
                    W('misc_written', st, turn)
                    fin_chain(i, n, turn)
                elif k == 'moe':
                    dve_moe()

            def norm(st, src, dst, eps, n, turn):
                for t in (0, 1):
                    link(nc.vector.bn_stats(BNS[:, t, :], src[t]), turn)
                    link(nc.vector.bn_aggr(MV[n][:, t, :], BNS[:, t, :]), turn)
                nc.vector.tensor_scalar(VE[n][:], MV[n][:, :, 1], eps, None, ALU.add).then_inc(sems['var_ready'], 1)
                if st is not None:
                    dve.wait_ge(sems['rstd_ready'], level['rstd_ready', st])
                    for t in (0, 1):
                        last = nc.vector.tensor_scalar(dst[t], src[t], MV[n][:, t, 0:1], RSTD[n][:, t:t + 1], ALU.subtract, ALU.mult)
                    last.then_inc(sems['xn_ready'], 1)

            def fin_chain(i, n, turn):
                link(nc.vector.tensor_copy(CTX[n][:, :, :], MISCB[:, 0:QW].rearrange("p (t d) -> p t d", t=2)), turn)
                for t in (0, 1):
                    link(nc.vector.bn_stats(BNS[:, t, :], CTX[n][:, t, :]), turn)
                    link(nc.vector.bn_aggr(MV[n][:, t, :], BNS[:, t, :]), turn)
                nc.vector.tensor_scalar(VE[n][:], MV[n][:, :, 1], 1e-6, None, ALU.add).then_inc(sems['fvar_ready'], 1)
                dve.wait_ge(sems['frstd_ready'], i + 1)
                for t in (0, 1):
                    link(nc.vector.tensor_scalar(XN[n][:, t, :], CTX[n][:, t, :], MV[n][:, t, 0:1], RSTD[n][:, t:t + 1], ALU.subtract, ALU.mult), turn)
                link(nc.vector.tensor_tensor(XN[n][:, :, :], XN[n][:, :, :], LNGB[:, 0, :].unsqueeze(1).broadcast_to([128, 2, D]), ALU.mult), turn)
                link(nc.vector.tensor_tensor(XN[n][:, :, :], XN[n][:, :, :], LNGB[:, 1, :].unsqueeze(1).broadcast_to([128, 2, D]), ALU.add), turn)
                link(nc.vector.scalar_tensor_tensor(X[:, 2 * i:2 * i + 2, :], XN[n][:, :, :], TG[:, 2:3], X[:, 2 * i:2 * i + 2, :], ALU.mult, ALU.add), turn)
                nc.vector.memset(REC[0][:, :, 0:1], 1.0).then_inc(sems['misc_read'], 1)

            def first_of(sel, gt, eq, cum, src, thr, k, width, flat):
                n = NT
                b = thr.unsqueeze(2).broadcast_to([128, n, width])
                link(nc.vector.tensor_tensor(gt, src, b, ALU.is_gt), None)
                link(nc.vector.tensor_tensor(eq, src, b, ALU.is_equal), None)
                link(nc.vector.tensor_reduce(NEED[:, :], gt, AX.X, ALU.add), None)
                link(nc.vector.tensor_scalar(NEED[:, :], NEED[:, :], -1.0, float(k), ALU.mult, ALU.add), None)
                for t in range(n):
                    last = nc.vector.tensor_tensor_scan(cum[:, t, :], ONES64[:, 0:width], eq[:, t, :], 0.0, ALU.mult, ALU.add)
                link(last, None)
                link(nc.vector.tensor_tensor(cum, cum, NEED[:, :].unsqueeze(2).broadcast_to([128, n, width]), ALU.is_le), None)
                link(nc.vector.tensor_tensor(eq, eq, cum, ALU.mult), None)
                link(nc.vector.tensor_tensor(sel, gt, eq, ALU.add), None)

            NEED = SM[:, 0:8]
            ONES64 = SM[:, 8:72]
            GS = SM[:, 72:136].rearrange("p (t g) -> p t g", t=NT)
            GG = [SM[:, 136 + 64 * a:200 + 64 * a].rearrange("p (t g) -> p t g", t=NT) for a in range(4)]
            M8G = SM[:, 392:456].rearrange("p (t g) -> p t g", t=NT)
            SUM = SM[:, 456:464]

            def dve_moe():
                dve.wait_ge(sems['sig_done'], 1)
                link(nc.vector.memset(ONES64, 1.0), None)
                link(nc.vector.tensor_scalar(SC, SC, 0.5, 0.5, ALU.mult, ALU.add), None)
                link(nc.vector.tensor_tensor(SWB, SC, BR[:, :].unsqueeze(1).broadcast_to([128, NT, NE]), ALU.add), None)
                for t in range(NT):
                    for g in range(8):
                        last = nc.vector.max(M8[:, t, g, :], SWB[:, t, 8 * g:8 * g + 8])
                link(last, None)
                link(nc.vector.tensor_tensor(GS, M8[:, :, :, 0], M8[:, :, :, 1], ALU.add), None)
                for t in range(NT):
                    last = nc.vector.max(M8G[:, t, :], GS[:, t, :])
                link(last, None)
                first_of(GG[3], GG[0], GG[1], GG[2], GS, M8G[:, :, 3], 4, 8, None)
                link(nc.vector.tensor_tensor(SWB.rearrange("p t (g e) -> p t g e", g=8), SWB.rearrange("p t (g e) -> p t g e", g=8),
                                             GG[3].unsqueeze(3).broadcast_to([128, NT, 8, 8]), ALU.mult), None)
                for t in range(NT):
                    last = nc.vector.max(M8G[:, t, :], SWB[:, t, :])
                link(last, None)
                first_of(MSK, GT, EQ, CUM, SWB, M8G[:, :, 7], 8, NE, None)
                link(nc.vector.tensor_tensor(SC, SC, MSK, ALU.mult), None)
                link(nc.vector.tensor_reduce(SUM, SC, AX.X, ALU.add), None)
                link(nc.vector.tensor_scalar(SUM, SUM, 1e-20, None, ALU.add), None)
                link(nc.vector.reciprocal(SUM, SUM), None)
                link(nc.vector.tensor_scalar(SC, SC, 2.5, None, ALU.mult), None)
                link(nc.vector.tensor_tensor(SC, SC, SUM.unsqueeze(2).broadcast_to([128, NT, NE]), ALU.mult), None)
                link(nc.vector.tensor_copy(WP[:, :, 0, :], SC), None)
                link(nc.vector.tensor_tensor(SC, SC, WP[:, :, 0, :], ALU.subtract), None)
                nc.vector.tensor_scalar(WP[:, :, 1, :], SC, SHIFT, None, ALU.mult).then_inc(sems['w_ready'], 1)
                for n in range(2 * NP + 2):
                    shared = n // 2 == NP
                    rows = FE if shared else 128
                    dve.wait_ge(sems['wb_done'], n + 1)
                    dve.wait_ge(sems['silu_done'], n + 1)
                    u = ST[n % 2][0:rows, 2:4, :].rearrange("p a t -> p (a t)")
                    if shared:
                        nc.vector.tensor_tensor(HT[n % 2][0:rows, :], SG[n % 2][0:rows, :], u, ALU.mult).then_inc(sems['ht_done'], 1)
                    else:
                        link(nc.vector.tensor_tensor(T1[n % 2], SG[n % 2], u, ALU.mult), None)
                        nc.vector.tensor_tensor(HT[n % 2], T1[n % 2], S[n % 2][:], ALU.mult).then_inc(sems['ht_done'], 1)
                dve.wait_ge(sems['y_done'], 2)
                nc.vector.tensor_copy(YT[:, 512:1024], MISCB[:]).then_inc(sems['yt_copied'], 1)
                for h in (0, 1):
                    dve.wait_ge(sems['y_tok'], h + 1)
                    y = ST[h][:, 0:2, :].rearrange("p a t -> p (a t)")
                    xx = X[:, 4 * h:4 * h + 4, :].rearrange("p t d -> p (t d)")
                    nc.vector.scalar_tensor_tensor(xx, y, TG[:, 3:4], xx, ALU.mult, ALU.add).then_inc(sems['y_added'], 1)

            run(dve, emit)

        @block.gpsimd
        def _(pool):
            W = lambda name, st, turn: pool.wait_ge(sems[name], count(name, st, turn))
            done = [0]
            pool_per_turn = sum({'qs': 3, 'ks': 3}.get(s_[0], 0) for s_ in turns[0])

            def link(ins, turn):
                ins.then_inc(sems['pool_step'], 1)
                done[0] += 1
                pool.wait_ge(sems['pool_step'], done[0] if turn is None else done[0] + turn * pool_per_turn)

            def parts(src, p, r, signal, turn):
                link(nc.gpsimd.tensor_scalar(p[0], src, 1.0, 1.0, ALU.mult, ALU.mult), turn)
                link(nc.gpsimd.tensor_tensor(r, src, p[0], ALU.subtract), turn)
                link(nc.gpsimd.tensor_scalar(p[1], r, 1.0, 1.0, ALU.mult, ALU.mult), turn)
                nc.gpsimd.tensor_tensor(p[2], r, p[1], ALU.subtract).then_inc(signal, 1)

            def emit(st, turn):
                k = st[0]
                if k == 'init':
                    for L in (0, 1):
                        for b in (0, 1):
                            nc.gpsimd.memset(KAX[L][b][:, :, :], 0.0).then_inc(sems['zeroed'], 1)
                    for i in range(CH):
                        nc.gpsimd.memset(QA[i][:, :, :].rearrange("p h t -> p (h t)").bitcast(u32), 0).then_inc(sems['zeroed'], 1)
                elif k == 'ln' or k == 'fin':
                    if k == 'ln':
                        n, a, b, v = ordinal[st] % 2, 'var_ready', 'rstd_ready', level['var_ready', st]
                    else:
                        n, a, b, v = st[1] % 2, 'fvar_ready', 'frstd_ready', st[1] + 1
                    pool.wait_ge(sems[a], v)
                    nc.gpsimd.tensor_tensor(RSTD[n][:], VE[n][:], NEGHALF[:], ALU.pow).then_inc(sems[b], 1)
                elif k == 'qs':
                    _, kind, c, i = st
                    n = ordinal[st]
                    W('misc_read', ('xq', c, i) if kind == 'X' else ('wq', c, i), turn)
                    if n >= 2:
                        o = by_ordinal['qs'][n - 2]
                        W(f'q_out{o[-1]}', ('qw',) + o[1:], turn)
                    parts(QX[n % 2][:], [QP[n % 2][:, a, :] for a in range(3)], QR[:], sems['q_split'], turn)
                elif k == 'ks':
                    _, kind, c, b = st
                    n = ordinal[st]
                    W('misc_read', ('xk', c, b) if kind == 'X' else ('kb', c, b), turn)
                    if n >= 1:
                        o = by_ordinal['ks'][n - 1]
                        W(keys_sem('out', o), ('kw',) + o[1:], turn)
                    w = SK if kind == 'X' else SQ
                    parts(KX[:, 0:w], [KP[:, a, 0:w] for a in range(3)], KRS[:, 0:w], sems['k_split'], turn)

            run(pool, emit)

        @block.sync
        def _(sp):
            W = lambda name, st, turn: sp.wait_ge(sems[name], count(name, st, turn))

            def blocks(dst, dram, order, d, heads, sem_, w):
                for j in range(6):
                    sp.dma_start(dst[d * j:d * j + d, 0:heads, 0:w], dram[order[j]].rearrange("(h d) t -> d h t", d=d)).then_inc(sem_, 16)

            def emit(st, turn):
                k = st[0]
                if k == 'init':
                    sp.dma_start(X[:, :, :], x).then_inc(sems['load_x'], 16)
                    for dst, src in ((CT[:, :, :], ctx_t.rearrange("b d s -> d b s")), (XB[:, :, :], x_bqk), (XBV[:, :, :, :], x_bvo), (GALL[:], g_all),
                                     (IDENT[:], c_ident), (IDB[:], c_ident_bf), (IDH[:], c_ident_h)):
                        sp.dma_start(dst, src).then_inc(sems['load_c'], 16)
                    sp.dma_start(XW[:, :, 0, :], x_wq).then_inc(sems['load_w'], 16)
                    sp.dma_start(XW[:, :, 3, :], x_wo).then_inc(sems['load_w'], 16)
                    sp.dma_start(XW[0:DC, :, 1:3, :], x_wkv).then_inc(sems['load_w'], 16)
                    sp.wait_ge(sems['zeroed'], 4)
                    for L in (0, 1):
                        for b in (0, 1):
                            sp.dma_start(KAX[L][b][ROWS_M:KR, :, :], c_sel_x).then_inc(sems['load_c'], 16)
                    sp.dma_start(LNGB[:, :, :], ln_gb).then_inc(sems['load_c'], 16)
                    for dst, src in ((EW[:], f_ew), (BE[:], f_be), (ACTW[:], f_actw), (WPOST[:, :, :], f_wpost[0]), (WK[:, :, :], f_wk[0]), (WV[:, :, :], f_wv[0]),
                                     (KAF[0][ROWS_M:KR, :, :], c_sel_f), (KAF[1][ROWS_M:KR, :, :], c_sel_f)):
                        sp.dma_start(dst, src).then_inc(sems['load_f'], 16)
                elif k == 'we_first':
                    for dst, src in ((WR[:], w_router), (BR[:], b_router), (WG[:], moe_gate), (WU[:], moe_up), (WS[:], sh_gate_up), (SELE[:, :, :], c_sel_e)):
                        sp.dma_start(dst, src).then_inc(sems['load_m'], 16)
                elif k == 'qw':
                    _, kind, c, i = st
                    qs = ('qs',) + st[1:]
                    W('q_split', qs, turn)
                    sp.dma_start(qd[i].rearrange("a p t -> p a t"), QP[ordinal[qs] % 2][:, :, :]).then_inc(sems[f'q_out{i}'], 16)
                elif k == 'qr':
                    _, kind, c, i = st
                    if kind == 'X' and c == 0 and i == 0:
                        sp.wait_ge(sems['zeroed'], 8)
                    W(f'q_out{i}', ('qw',) + st[1:], turn)
                    blocks(QA[i], qd[i], QPART, DH[kind], HEADS[kind], sems[f'q_in{i}'], QW)
                elif k == 'kw':
                    _, kind, c, b = st
                    W('k_split', ('ks',) + st[1:], turn)
                    if kind == 'X':
                        sp.dma_start(kdx[c][b].rearrange("a p t -> p a t"), KP[:, :, 0:SK]).then_inc(sems[keys_sem('out', st)], 16)
                    else:
                        sp.dma_start(kd[b].rearrange("a p t -> p a t"), KP[:, :, :]).then_inc(sems[keys_sem('out', st)], 16)
                elif k == 'kr':
                    _, kind, c, b = st
                    W(keys_sem('out', st), ('kw',) + st[1:], turn)
                    if kind == 'X':
                        blocks(KAX[c][b], kdx[c][b], KPART, 8, 16, sems[keys_sem('in', st)], SK)
                    else:
                        if c:
                            W('st_done', ('st', 'F', 0, CH * (c - 1) + 2 * b + 1, 1, 3), turn)
                        blocks(KAF[b], kd[b], KPART, 16, 8, sems[keys_sem('in', st)], SQ)
                elif k == 'md':
                    _, kind, L, s, g = st
                    n = group_at[st[1:]] % 4
                    i, h = chain_of(kind, s), head0(kind, s, g)
                    W('misc_read', ('mT',) + st[1:], turn)
                    sp.dma_start(QA[i][ROWS_M:KR, h:h + G, :], MT[n][:, :].unsqueeze(1).broadcast_to([3 * G, G, QW])).then_inc(sems[rows_sem(st)], 16)
                elif k == 'wl_post':
                    c = st[1]
                    W('misc_written', ('wq', c, CH - 1), turn)
                    sp.dma_start(WPOST[:, :, :], wrow(f_wpost, dyn(c + 1, turn))).then_inc(sems['wpost_in'], 16)
                elif k == 'wl_v':
                    c = st[1]
                    W('misc_written', ('vb', c - 1, 1), turn)
                    sp.dma_start(WV[:, :, :], wrow(f_wv, dyn(c, turn))).then_inc(sems['wv_in'], 16)
                elif k == 'wl_k':
                    c = st[1]
                    W('misc_written', ('kb', c - 1, 1), turn)
                    sp.dma_start(WK[:, :, :], wrow(f_wk, dyn(c, turn))).then_inc(sems['wk_in'], 16)
                elif k == 'ln' and st[1] == 'M' and st[3] == 0:
                    sp.wait_ge(sems['misc_read'], level['misc_read', ('fin', CH - 1)])
                    sp.dma_start(WD, moe_down).then_inc(sems['load_d'], 16)
                    sp.dma_start(WSD, sh_down).then_inc(sems['load_d'], 16)
                elif k == 'moe':
                    for h in (0, 1):
                        sp.wait_ge(sems['y_added'], h + 1)
                        sp.dma_start(out[:, 4 * h:4 * h + 4, :], X[:, 4 * h:4 * h + 4, :]).then_inc(sems['out_done'], 16)
                    sp.wait_ge(sems['out_done'], 32)

            def wrow(w, c):
                if isinstance(c, int):
                    return w[c]
                return w.rearrange("c p a n -> (c p) a n")[bass.ds(c * 128, 128)]

            run(sp, emit)


LOOP = False
_OUT = ((2, 512, 128), 'float32')


def kernel(**inputs):
    import numpy as np
    import concourse.bacc as bacc
    from concourse import mybir as _mybir
    from concourse.bass_utils import run_bass_kernel_spmd as run_spmd

    a = {k: np.asarray(v) for k, v in inputs.items()}
    f = np.float32
    NT, D = 8, 128

    def rows(v, n=128):
        return np.ascontiguousarray(np.broadcast_to(v, (n,) + v.shape))

    edge, lind = [], 0
    for c in range(6):
        n = min(c + 1, 5)
        edge.append((lind + n - 1, lind, lind + n // 2))
        lind += n
    We, be, Wq, Wk, Wv, Wo = (a[f'L0_ffn_{n}'] for n in ('We', 'be', 'Wq', 'Wk', 'Wv', 'Wo'))

    def side(*m):
        return np.stack(m, axis=1)
    wpost = [side(Wo[0], We[edge[0][0]], Wq[0])]
    for c in range(6):
        nx = min(c + 1, 5)
        wpost.append(side(Wo[c], We[edge[nx][0]], Wq[nx]))
    wk = [side(We[edge[c][1]], Wk[c]) for c in range(6)]
    wk.append(wk[-1])
    wv = [side(We[edge[c][2]], Wv[c]) for c in range(6)]
    xl = [{n: a[f'L0_xattn_{n.lower()}' if L == 0 else f'L1_xattn_{n}'] for n in ('Wq', 'bq', 'Wk', 'bk', 'Wv', 'bv', 'Wo', 'bo')} for L in (0, 1)]

    one = np.uint16(0x3F80)
    sel_x = np.zeros((12, 16, 77), np.uint16)
    sel_f = np.zeros((12, 8, 512), np.uint16)
    for p in range(3):
        for r in range(4):
            sel_x[4 * p + r, r::4, :] = one
            sel_f[4 * p + r, r::4, :] = one
    sel_e = np.zeros((128, 32, 128), np.float16)
    for e in range(64):
        sel_e[e, e // 2, 64 * (e % 2):64 * (e % 2) + 64] = 1.0
        sel_e[64 + e, e // 2, 64 * (e % 2):64 * (e % 2) + 64] = 1.0 / 2048.0

    arrays = [
        ('x', a['x'].reshape(NT, 128, D).transpose(1, 0, 2)),
        ('ctx_t', a['ctx_768'].transpose(0, 2, 1)),
        ('g_all', rows(np.concatenate([a['g_xattn'], a['g_ffn']]))),
        ('x_wq', side(xl[0]['Wq'], xl[1]['Wq'])),
        ('x_wkv', np.stack([side(xl[L]['Wk'], xl[L]['Wv']) for L in (0, 1)], axis=1)),
        ('x_wo', side(xl[0]['Wo'], xl[1]['Wo'])),
        ('x_bqk', np.stack([np.stack([xl[L]['bq'], xl[L]['bk']], axis=1) for L in (0, 1)], axis=1)),
        ('x_bvo', rows(np.stack([np.stack([xl[L]['bv'], xl[L]['bo']]) for L in (0, 1)]))),
        ('f_wpost', np.stack(wpost)), ('f_wk', np.stack(wk)), ('f_wv', np.stack(wv)),
        ('f_ew', rows(a['L0_ffn_ew'].reshape(-1))),
        ('f_be', be[np.array(edge).reshape(-1)].T),
        ('f_actw', rows(a['L0_ffn_act_w'])),
        ('ln_gb', rows(np.stack([a['L0_ffn_ln_g'], a['L0_ffn_ln_b']]))),
        ('w_router', a['L1_ffn_w_router']), ('b_router', rows(a['L1_ffn_b_router'])),
        ('moe_gate', a['L1_ffn_we_gate'].transpose(1, 0, 2).reshape(D, 64 * 64)),
        ('moe_up', a['L1_ffn_we_up'].transpose(1, 0, 2).reshape(D, 64 * 64)),
        ('moe_down', a['L1_ffn_we_down'].reshape(32, 128, D).transpose(1, 0, 2).reshape(128, 32 * D)),
        ('sh_gate_up', np.concatenate([a['L1_ffn_ws_gate'], a['L1_ffn_ws_up']], axis=1)),
        ('sh_down', a['L1_ffn_ws_down']),
        ('c_ident', np.eye(128, dtype=f)), ('c_ident_bf', np.where(np.eye(128) > 0, one, np.uint16(0)).astype(np.uint16)),
        ('c_sel_x', sel_x), ('c_sel_f', sel_f), ('c_sel_e', sel_e), ('c_ident_h', np.eye(128, dtype=np.float16)),
    ]
    nc = bacc.Bacc("TRN2", target_bir_lowering=False, num_devices=1)
    feeds, args = {}, {}
    for name, arr in arrays:
        arr = np.ascontiguousarray(arr)
        feeds[f"in_{name}"] = arr
        ap = nc.dram_tensor(f"in_{name}", arr.shape, _mybir.dt.from_np(arr.dtype), kind="ExternalInput").ap()
        args[name] = ap.bitcast(_mybir.dt.bfloat16) if arr.dtype == np.uint16 else ap
    out = nc.dram_tensor("out_x", (NT, 128, D), _mybir.dt.float32, kind="ExternalOutput").ap()
    flamingo_gated_two_layer(nc, out=out.rearrange("t p d -> p t d"), **args)
    r = run_spmd(nc, [feeds], core_ids=[0])
    return r.results[0]["out_x"].reshape(_OUT[0])
```

```python
import concourse.bass as bass
from concourse import mybir
from contextlib import ExitStack


def flamingo_gated_two_layer(
    nc,
    x, ctx_t, g_all,
    x_wq, x_wkv, x_wo, x_bqk, x_bvo,
    f_wpost, f_wk, f_wv, f_ew, f_be, f_actw, ln_gb,
    w_router, b_router, moe_gate, moe_up, moe_down, sh_gate_up, sh_down,
    c_ident, c_ident_bf, c_sel_x, c_sel_f, c_sel_e, c_ident_h,
    out,
):
    f32, bf16, f16 = mybir.dt.float32, mybir.dt.bfloat16, mybir.dt.float16
    u32 = mybir.dt.uint32
    ALU = mybir.AluOpType
    ACT = mybir.ActivationFunctionType
    AX = mybir.AxisListType

    D = 128
    NT = x.shape[1]
    CH = 4
    QW = NT * 128 // CH
    B = 2
    SQ = NT * 128 // B
    SK = ctx_t.shape[2]
    DC = ctx_t.shape[1]
    NN = 6
    G = 4
    ROWS_M = 96
    KR = ROWS_M + 3 * G
    NP = 32
    NE = 64
    FE = 64
    SHIFT = 2048.0
    QPART = (0, 0, 0, 1, 1, 2)
    KPART = (0, 1, 2, 0, 1, 0)
    HEADS = {'X': 16, 'F': 8}
    DH = {'X': 8, 'F': 16}
    KT = {'X': 1, 'F': 4}
    KW = {'X': SK, 'F': 128}
    PR = 4

    def x_slots(L, extras, follow):
        n = 4 * CH
        slots = dict(extras)

        def put(q, *steps):
            slots[q] = list(slots.get(q, [])) + list(steps)

        for s in range(2 * CH):
            put(2 * s + 3, ('otT', 'X', L, s))
            if s % 2:
                put(2 * s + 4, ('ctxT', 'X', L, s // 2))
                put(2 * s + 5, ('wox', L, s // 2))
                for k, steps in enumerate(follow(s // 2)):
                    put(2 * s + 5 + k, *steps)
        st = []
        for q in range(-4, max(slots) + 1):
            if 0 <= q < n:
                st.append(('st', 'X', L, q // 2, q % 2, 0))
            if q + 4 < n:
                at = ('X', L, (q + 4) // 2, q % 2)
                st += [('s',) + at + (t,) for t in (0, 1)] + [('mp',) + at]
            if 0 <= q + 3 < n:
                at = ('X', L, (q + 3) // 2, (q + 3) % 2)
                st += [('mT',) + at, ('md',) + at]
            if 0 <= q - 1 < n:
                st.append(('pv', 'X', L, (q - 1) // 2, (q - 1) % 2, 0))
                if q % 2 == 0:
                    st.append(('otc', 'X', L, (q - 1) // 2))
            st += slots.get(q, [])
        return st

    def x_keys(L, b):
        return [[('xk', L, b), ('ks', 'X', L, b)], [('xv', L, b)], [('kw', 'X', L, b)], [('kr', 'X', L, b)]]

    def x_query(L, i):
        return [[('ls', 'X', L, i)], [('ln', 'X', L, i)], [('xT', 'X', L, i)], [('xq', L, i), ('qs', 'X', L, i)], [('qw', 'X', L, i)], [('qr', 'X', L, i)]]

    def f_query(i):
        b = i // 2
        go = [[('ls', 'F', 0, i)], [('ln', 'F', 0, i)], [('xT', 'F', 0, i)], [('we', 0, i)], [('wq', 0, i), ('qs', 'F', 0, i)], [], [], [], []]
        if i < CH - 1:
            go[5] += [('qw', 'F', 0, i)]
            go[6] += [('qr', 'F', 0, i)]
        if i % 2:
            go[5] += [('ka', 0, b)]
            go[6] += [('kb', 0, b), ('ks', 'F', 0, b)]
            go[7] += [('kw', 'F', 0, b)]
            go[8] += [('kr', 'F', 0, b)]
        if i == 1:
            go[7] += [('va', 0, 0)]
            go[8] += [('vb', 0, 0)]
        return go

    def m_rows(i):
        return [[('ls', 'M', 0, i)], [('ln', 'M', 0, i)], [('xT', 'M', 0, i)]]

    def f_tiles(s, g):
        return [('s', 'F', 0, s, g, j) for j in range(8)]

    def f_slot(s, extras={}):
        c, i = divmod(s, CH)
        last = CH * NN - 1
        st = []
        pc, pi = divmod(s - 1, CH)
        jobs = {0: [], 1: [('va', c, 1), ('vb', c, 1), ('ka', c + 1, 0), ('kb', c + 1, 0)],
                2: [('ka', c + 1, 1), ('kb', c + 1, 1)], 3: [('va', c + 1, 0), ('vb', c + 1, 0)]}[i]
        jobs = [j for j in jobs if j[1] < NN]
        at = {4: (0, 1, 5, 7), 2: (0, 7), 0: ()}[len(jobs)]
        for p in range(8):
            g, kt = divmod(p, 4)
            if p == 0:
                if i == 1:
                    st.append(('wl_post', c))
                if i == 2 and c + 1 < NN:
                    st.append(('wl_v', c + 1))
                if i == 3 and c + 1 < NN:
                    st.append(('wl_k', c + 2))
            st.append(('st', 'F', 0, s, g, kt))
            if s < last:
                st += [('s', 'F', 0, s + 1, g, 2 * kt), ('s', 'F', 0, s + 1, g, 2 * kt + 1)]
            if p == 1:
                st += [('mT', 'F', 0, s, 1), ('md', 'F', 0, s, 1)]
                if s >= 1 and (s - 2) // CH + 1 < NN:
                    qc, qi = divmod(s - 2, CH)
                    st += [('qw', 'F', qc + 1, qi)]
            if s >= 1:
                if p == 2:
                    st.append(('otT', 'F', 0, s - 1))
                    if s >= 1 and (s - 2) // CH + 1 < NN:
                        qc, qi = divmod(s - 2, CH)
                        st += [('qr', 'F', qc + 1, qi)]
                if p == 3:
                    st.append(('ctxT', 'F', 0, s - 1))
                if p == 4:
                    st.append(('wo', pc, pi))
                if p == 6 and pc + 1 < NN:
                    st += [('we', pc + 1, pi)]
                if p == 7 and pc + 1 < NN:
                    st += [('wq', pc + 1, pi), ('qs', 'F', pc + 1, pi)]
            for n, j in enumerate(jobs):
                if at[n] == p:
                    st.append(j)
                    if j[0] == 'kb':
                        st.append(('ks',) + ('F',) + j[1:])
            if i == 2 and p == 3 and c + 1 < NN:
                st += [('kw', 'F', c + 1, 0), ('kr', 'F', c + 1, 0)]
            if i == 3 and p == 3 and c + 1 < NN:
                st += [('kw', 'F', c + 1, 1)]
            if i == 0 and p == 3 and c >= 1:
                st += [('kr', 'F', c, 1)]
            st += extras.get((s, p), [])
            if s < last:
                if p == 3:
                    st.append(('mp', 'F', 0, s + 1, 0))
                if p == 5:
                    st += [('mT', 'F', 0, s + 1, 0), ('md', 'F', 0, s + 1, 0)]
                if p == 7:
                    st.append(('mp', 'F', 0, s + 1, 1))
            if s or p:
                q = 8 * s + p - 1
                st.append(('pv', 'F', 0, q // 8, q % 8 // 4, q % 4))
            if p == 0 and s >= 1:
                st.append(('otc', 'F', 0, s - 1))
        return st

    flat = lambda groups: [st for group in groups for st in group]
    before = [('init',)] + [('ls', 'X', 0, i) for i in range(CH)] + flat(x_keys(0, 0))
    for i in range(CH):
        before += [('ln', 'X', 0, i), ('xT', 'X', 0, i)]
    for i in range(CH):
        before += [('xq', 0, i), ('qs', 'X', 0, i), ('qw', 'X', 0, i)] + ([('qr', 'X', 0, i - 1)] if i else [])
    before += [('qr', 'X', 0, CH - 1)] + flat(x_keys(0, 1))
    more = {k + 2: group for k, group in enumerate(x_keys(1, 0) + x_keys(1, 1))}
    more[10] = [('we_first',)]
    more[20] = f_tiles(0, 0) + [('mp', 'F', 0, 0, 0)]
    more[21] = f_tiles(0, 1) + [('mT', 'F', 0, 0, 0), ('md', 'F', 0, 0, 0), ('mp', 'F', 0, 0, 1)]
    late = {}
    for k, group in enumerate(f_query(CH - 1)):
        late[0, max(k - 3, 0)] = late.get((0, max(k - 3, 0)), []) + group
    late[0, 6] = [('wl_k', 1)]
    before += x_slots(0, more, lambda i: f_query(i) if i < CH - 1 else []) + f_slot(0, late)
    turns = [sum((f_slot(CH * c + i) for i in (1, 2, 3, 4)), []) for c in range(NN - 1)]

    tail = {}
    for i in range(CH):
        go = [[('fin', i)], [('fl', i)]] + x_query(1, i)
        for k, group in enumerate(go):
            s_, p_ = divmod(8 * (CH * (NN - 1) + 1 + i) + 5 + k, 8)
            tail.setdefault((s_, p_), []).extend(group)
    after = sum((f_slot(CH * (NN - 1) + i, tail) for i in (1, 2, 3)), [])
    n = CH * NN
    after += [('pv', 'F', 0, n - 1, 1, 3), ('otc', 'F', 0, n - 1)]
    early = {-4: tail.get((n, 0), []), -3: [('otT', 'F', 0, n - 1)] + tail.get((n, 1), []), -2: [('ctxT', 'F', 0, n - 1)] + tail.get((n, 2), []),
             -1: [('wo', NN - 1, CH - 1)] + tail.get((n, 3), []) + tail.get((n, 4), [])}
    for k in range(5, 16):
        early[k - 5] = tail.get((n + k // 8, k % 8), [])
    after += x_slots(1, early, m_rows) + [('moe',)]
    everything = before + sum(turns, []) + after

    MISC = ('xk', 'xv', 'xT', 'xq', 'mT', 'otT', 'ctxT', 'wox', 'wo', 'we', 'wq', 'va', 'vb', 'ka', 'kb', 'fin')

    def keys_sem(way, st):
        return f'k_{way}{st[-1]}' if st[1] == 'F' else f'kx_{way}{st[-2]}{st[-1]}'

    group_at = {st[1:]: n for n, st in enumerate(st for st in everything if st[0] == 'mp')}

    def rows_sem(st):
        return f'm_in{group_at[st[1:5]] % 8}' if st[0] in ('md', 'st') else None

    def signals(st):
        k = st[0]
        if k == 'fin':
            return (('misc_written', 1), ('misc_read', 1), ('var_ready', 1), ('rstd_ready', 1))
        if k in MISC:
            return (('misc_written', 1), ('misc_read', 1))
        if k in ('kw', 'kr'):
            return ((keys_sem('out', st), 16),) if k == 'kw' else ((keys_sem('in', st), 96),)
        return {
            'st': (('st_done', 1), ('exp_done', 1)), 'pv': (('pv_done', 1),), 's': (('s_done', 1), ('max_done', 1)),
            'mp': (('mparts', 1),), 'otc': (('ot_copied', 1),), 'qs': (('q_split', 1),), 'ks': (('k_split', 1),),
            'ls': (('var_ready', 1), ('rstd_ready', 1)), 'ln': (('xn_ready', 1),),
            'qw': ((f'q_out{st[-1]}', 16),), 'qr': ((f'q_in{st[-1]}', 96),),
            'md': ((rows_sem(st), 16),),
            'wl_post': (('wpost_in', 16),), 'wl_v': (('wv_in', 16),), 'wl_k': (('wk_in', 16),),
        }.get(k, ())

    level, total, ordinal = {}, {}, {}
    for st in everything:
        ordinal[st] = total.setdefault(st[0], 0)
        total[st[0]] += 1
        for name, by in signals(st):
            total[name] = total.get(name, 0) + by
            level[name, st] = total[name]
    per_turn = {}
    for st in turns[0]:
        for name, by in signals(st):
            per_turn[name] = per_turn.get(name, 0) + by

    def count(name, st, turn):
        return level[name, st] if turn is None else turn * per_turn[name] + (level[name, st] - per_turn[name])

    def dyn(v, turn):
        return v if turn is None else turn + (v - 1)

    kv_split_of = {}

    with ExitStack() as ctx:
        def sb(name, shape, dt=f32):
            return ctx.enter_context(nc.sbuf_tensor(name, shape, dt))

        def pb(name, shape):
            return ctx.enter_context(nc.psum_tensor(name, shape, f32))

        def sem(name):
            return ctx.enter_context(nc.semaphore(name))

        X = sb("x_tok", [128, NT, D])
        NODE = sb("node_t", [128, NN + 1, NT * 128])
        QA = [sb(f"qa{i}", [128, 16, QW], bf16) for i in range(CH)]
        KAF = [sb(f"kaf{b}", [128, 8, SQ], bf16) for b in (0, 1)]
        KAX = [[sb(f"kax{L}{b}", [128, 16, SK], bf16) for b in (0, 1)] for L in (0, 1)]
        VFB = sb("vf", [128, 2, 4, 8, 32])
        VF = [VFB[:, b, :, :, :] for b in (0, 1)]
        SELE = VFB[:, :, :, :, :].rearrange("p b k h d -> p (b k h d)").bitcast(f16).rearrange("p (e n) -> p e n", n=128)
        VX = [[sb(f"vx{L}{b}", [128, 16, 32]) for b in (0, 1)] for L in (0, 1)]
        PT = [sb(f"pt{n}", [128, G, QW]) for n in range(PR)]
        NM = [sb(f"nm{n}", [128, 2, G]) for n in range(4)]
        MR = [sb(f"mr{n}", [128, 2, G]) for n in range(4)]
        MP = [sb(f"mp{n}", [128, 2, 3, G], bf16) for n in range(4)]
        MT = [sb(f"mt{n}", [3 * G, QW], bf16) for n in range(4)]
        OTS = [sb(f"ots{n}", [128, 2, QW]) for n in range(2)]
        REC = [sb(f"rec{n}", [128, 2, 8]) for n in range(2)]
        CTX = [sb(f"ctx{n}", [128, 2, D]) for n in range(2)]
        CTXT = [sb(f"ctxt{n}", [128, QW]) for n in range(2)]
        QT = [sb(f"qt{i}", [128, QW]) for i in range(CH)]
        QX = [sb(f"qx{n}", [128, QW]) for n in range(2)]
        QP = [sb(f"qp{n}", [128, 3, QW], bf16) for n in range(2)]
        QR = sb("qr", [128, QW])
        KIN = sb("kin", [128, SQ])
        KX = sb("kx", [128, SQ])
        KP = sb("kp", [128, 3, SQ], bf16)
        ZERO = sb("zero", [128, 2], bf16)
        KRS = sb("krs", [128, SQ])
        BNS = [sb(f"bns{n}", [128, 2, 6]) for n in range(CH)]
        MV = [sb(f"mv{n}", [128, 2, 2]) for n in range(CH)]
        VE = [sb(f"ve{n}", [128, 2]) for n in range(CH)]
        RSTD = [sb(f"rstd{n}", [128, 2]) for n in range(CH)]
        FT = [sb(f"ft{n}", [128, 2, D]) for n in range(2)]
        XN = [sb(f"xn{n}", [128, 2, D]) for n in range(2)]
        NEGHALF = sb("neghalf", [128, 2])
        CT = sb("ctx_in", [DC, B, SK])
        XW = sb("xw", [128, 2, 4, D])
        XB = sb("xb", [128, 2, 2])
        XBV = sb("xbv", [128, 2, 2, D])
        WPOST = sb("wpost", [128, 3, D])
        WK = sb("wk", [128, 2, D])
        WV = sb("wv", [128, 2, D])
        EW = sb("ew", [128, 3 * NN])
        BE = sb("be", [128, 3 * NN])
        EWBE = sb("ewbe", [128, 3 * NN])
        ACTW = sb("actw", [128, NN])
        GALL = sb("gall", [128, 4])
        TG = sb("tg", [128, 4])
        LNGB = sb("lngb", [128, 2, D])
        IDENT = sb("ident", [128, 128])
        IDB = sb("identb", [128, 128], bf16)
        IDH = sb("identh", [128, 128], f16)
        WR = sb("wr", [128, NE])
        BR = sb("br", [128, NE])
        WG = sb("wg", [128, NE * FE])
        WU = sb("wu", [128, NE * FE])
        WS = sb("ws", [128, 2 * FE])

        WD = NODE[:, 1:5, :].rearrange("p a t -> p (a t)")
        WSD = NODE[0:FE, 5, 0:D]
        MSC = [NODE[:, 6, 0:512], NODE[:, 6, 512:1024]]
        def qa_f32(i, lo, n):
            return QA[i][:, :, :].rearrange("p h t -> p (h t)").bitcast(f32)[:, lo:lo + n]

        ST = [pb(f"st{n}", [128, G, QW]) for n in range(2)]
        S = [pb(f"s{n}", [128, 512]) for n in range(2)]
        OT = pb("ot", [128, 2, QW])
        MISCB = pb("misc", [128, 512])

        names = ['load_x', 'load_c', 'load_w', 'load_f', 'load_m', 'load_d', 'zeroed', 'ready', 'dve_step', 'act_step', 'pool_step',
                 'tg_ready', 'gu_done', 'silu_done', 'ht_done', 'wb_done', 'y_done', 'yt_copied', 'y_tok', 'y_added', 'out_done',
                 'log_done', 'sig_done', 'w_ready', 'wT_done', 'wT_copied'] + [n for n in total if n not in {s[0] for s in everything}]
        sems = {n: sem(n) for n in dict.fromkeys(names)}

        qd = [nc.dram_tensor(f"q_parts{i}", (3, 128, QW), bf16, kind="Internal").ap() for i in range(CH)]
        kd = [nc.dram_tensor(f"k_parts{b}", (3, 128, SQ), bf16, kind="Internal").ap() for b in (0, 1)]
        kdx = [[nc.dram_tensor(f"kx_parts{L}{b}", (3, 128, SK), bf16, kind="Internal").ap() for b in (0, 1)] for L in (0, 1)]

        block = ctx.enter_context(nc.Block())

        def prior(kind, st, back=1):
            n = ordinal[st] - back
            return by_ordinal[kind][n] if n >= 0 else None

        by_ordinal = {}
        for s_ in everything:
            by_ordinal.setdefault(s_[0], []).append(s_)
        misc_order = [s_ for s_ in everything if s_[0] in MISC]
        misc_at = {s_: n for n, s_ in enumerate(misc_order)}
        tile_order = by_ordinal['st']
        group_order = by_ordinal['mp']

        def chain_of(kind, s):
            return s // 2 if kind == 'X' else s % CH

        def head0(kind, s, g):
            return (8 * (s % 2) if kind == 'X' else 0) + G * g

        def run(eng, emit, after_loop=lambda: None):
            for st in before:
                emit(st, None)
            if NN > 1:
                with eng.Fori(0, NN - 1) as turn:
                    for st in turns[1]:
                        emit(st, turn)
            else:
                for t in turns:
                    for st in t:
                        emit(st, None)
            after_loop()
            for st in after:
                emit(st, None)

        def node(idx, lo, n, turn_expr=None):
            if isinstance(idx, int):
                return NODE[:, idx, lo:lo + n]
            return NODE[:, :, :].rearrange("p a t -> p (a t)")[:, bass.ds(idx * (NT * 128) + lo, n)]

        def prior_otc(kind, L, s):
            n = ordinal['otc', kind, L, s]
            return by_ordinal['otc'][n - 1] if n else None

        WP = QA[3][:, 0:4, :].rearrange("p h t -> p (h t)").bitcast(f16).rearrange("p (t a e) -> p t a e", t=NT, a=2)
        WT = QA[3][:, 4:8, :].rearrange("p h t -> p (h t)").bitcast(f16)
        SG = [qa_f32(0, 0, 512), qa_f32(0, 512, 512)]
        T1 = [qa_f32(0, 1024, 512), qa_f32(0, 1536, 512)]
        HT = [qa_f32(1, 0, 512), qa_f32(1, 512, 512)]
        YT = qa_f32(1, 1024, 1024)
        def r3(i, lo):
            return qa_f32(i, lo, 512).rearrange("p (t e) -> p t e", t=NT)
        SC, SWB, GT, EQ = (r3(2, 512 * n) for n in range(4))
        MSK, CUM, ONE = r3(3, 1024), r3(3, 1536), MSC[1]
        M8 = MSC[0].rearrange("p (t g k) -> p t g k", t=NT, g=8)
        SM = MSC[1]

        @block.tensor
        def _(pe):
            W = lambda name, st, turn: pe.wait_ge(sems[name], count(name, st, turn))

            def emit(st, turn):
                k = st[0]
                if k in MISC:
                    n = misc_at[st]
                    if n:
                        W('misc_read', misc_order[n - 1], turn)
                if k == 'init':
                    pe.wait_ge(sems['load_c'], 16 * 12)
                    pe.wait_ge(sems['load_w'], 16 * 3)
                    pe.wait_ge(sems['ready'], 1)
                elif k == 'xk':
                    _, L, b = st
                    nc.tensor.matmul(MISCB[:, 0:SK], XW[0:DC, L, 1, :], CT[:, b, :], start=True, stop=True).then_inc(sems['misc_written'], 1)
                elif k == 'xv':
                    _, L, b = st
                    nc.tensor.matmul(MISCB[0:SK, 0:D], CT[:, b, :], XW[0:DC, L, 2, :], start=True, stop=True).then_inc(sems['misc_written'], 1)
                elif k == 'xT':
                    i = st[3]
                    W('xn_ready', ('ln',) + st[1:], turn)
                    n = ordinal['ln', st[1], st[2], i] % 2
                    for t in (0, 1):
                        last = nc.tensor.transpose(MISCB[:, 128 * t:128 * t + 128], XN[n][:, t, :], IDENT[:])
                    last.then_inc(sems['misc_written'], 1)
                elif k == 'xq':
                    _, L, i = st
                    W('misc_read', ('xT', 'X', L, i), turn)
                    nc.tensor.matmul(MISCB[:, 0:QW], XW[:, L, 0, :], node(0, QW * i, QW), start=True, stop=True).then_inc(sems['misc_written'], 1)
                elif k == 's':
                    _, kind, L, s, g, j = st
                    i, b = chain_of(kind, s), chain_of(kind, s) // 2
                    n = ordinal[st]
                    if n >= 2:
                        W('max_done', by_ordinal['s'][n - 2], turn)
                    if g == 0 and j == 0:
                        if kind == 'X':
                            W(f'q_in{i}', ('qr', 'X', L, i), turn)
                            W(f'kx_in{L}{b}', ('kr', 'X', L, b), turn)
                        else:
                            W(f'q_in{i}', ('qr', 'F', s // CH, i), turn)
                            W(f'k_in{b}', ('kr', 'F', s // CH, b), turn)
                    if kind == 'X':
                        for r in range(G):
                            h = head0(kind, s, g) + r
                            last = nc.tensor.matmul(S[n % 2][:, r * SK:(r + 1) * SK], QA[i][0:48, h, 128 * j:128 * j + 128],
                                                    KAX[L][b][0:48, h, :], start=True, stop=True)
                        last.then_inc(sems['s_done'], 1)
                    else:
                        t, r = divmod(j, 4)
                        h = G * g + r
                        nc.tensor.matmul(S[n % 2][:], QA[i][0:ROWS_M, h, 128 * t:128 * t + 128], KAF[b][0:ROWS_M, h, :],
                                         start=True, stop=True).then_inc(sems['s_done'], 1)
                elif k == 'mT':
                    n = group_at[st[1:]]
                    W('mparts', ('mp',) + st[1:], turn)
                    mb = MISCB[:, :].bitcast(bf16)
                    for t in (0, 1):
                        last = nc.tensor.transpose(mb[0:3 * G, 128 * t:128 * t + 128], MP[n % 4][:, t, :, :].rearrange("p a r -> p (a r)"), IDB[:])
                    last.then_inc(sems['misc_written'], 1)
                elif k == 'st':
                    _, kind, L, s, g, kt = st
                    i = chain_of(kind, s)
                    b = i // 2
                    n = ordinal[st]
                    if n >= 2:
                        W('exp_done', tile_order[n - 2], turn)
                    if kt == 0:
                        W(rows_sem(st), ('md', kind, L, s, g), turn)
                    for r in range(G):
                        h = head0(kind, s, g) + r
                        if kind == 'X':
                            last = nc.tensor.matmul(ST[n % 2][0:SK, r, :], KAX[L][b][0:KR, h, :], QA[i][0:KR, h, :], start=True, stop=True)
                        else:
                            last = nc.tensor.matmul(ST[n % 2][:, r, :], KAF[b][0:KR, h, 128 * kt:128 * kt + 128], QA[i][0:KR, h, :], start=True, stop=True)
                    last.then_inc(sems['st_done'], 1)
                elif k == 'pv':
                    _, kind, L, s, g, kt = st
                    i = chain_of(kind, s)
                    b = i // 2
                    tile = ('st',) + st[1:]
                    n = ordinal[tile]
                    W('exp_done', tile, turn)
                    if g == 0 and kt == 0:
                        before_it = prior_otc(kind, L, s)
                        if before_it:
                            W('ot_copied', before_it, turn)
                        if kind == 'F':
                            W('misc_read', ('vb', s // CH, b), turn)
                        else:
                            W('misc_read', ('xv', L, b), turn)
                    for r in range(G):
                        h = head0(kind, s, g) + r
                        if kind == 'X':
                            v, p = VX[L][b][0:SK, h, :], PT[n % PR][0:SK, r, :]
                        else:
                            v, p = VF[b][:, kt, h, :], PT[n % PR][:, r, :]
                        last = nc.tensor.matmul(OT[32 * r:32 * r + 32, g, :], v, p, start=(kt == 0), stop=(kt == KT[kind] - 1))
                    last.then_inc(sems['pv_done'], 1)
                elif k == 'otT':
                    _, kind, L, s = st
                    otc = ('otc',) + st[1:]
                    W('ot_copied', otc, turn)
                    o = OTS[ordinal[otc] % 2]
                    for t in (0, 1):
                        for g in (0, 1):
                            last = nc.tensor.transpose(MISCB[:, (2 * t + g) * 128:(2 * t + g) * 128 + 128], o[:, g, 128 * t:128 * t + 128], IDENT[:])
                    last.then_inc(sems['misc_written'], 1)
                elif k == 'ctxT':
                    i = st[3]
                    n = i % 2
                    for t in (0, 1):
                        last = nc.tensor.transpose(MISCB[:, 128 * t:128 * t + 128], CTX[n][:, t, :], IDENT[:])
                    last.then_inc(sems['misc_written'], 1)
                elif k == 'wox':
                    _, L, i = st
                    for t in (0, 1):
                        last = nc.tensor.matmul(MISCB[:, 128 * t:128 * t + 128], CTXT[i % 2][:, 128 * t:128 * t + 128], XW[:, L, 3, :], start=(t == 0), stop=True, skip_group_check=True)
                    last.then_inc(sems['misc_written'], 1)
                elif k == 'wo':
                    _, c, i = st
                    if i == 0:
                        W('wpost_in', ('wl_post', c), turn)
                    nc.tensor.matmul(MISCB[:, 0:QW], WPOST[:, 0, :], CTXT[i % 2][:, :], start=True, stop=True).then_inc(sems['misc_written'], 1)
                elif k == 'we_first':
                    pe.wait_ge(sems['load_f'], 16 * 8)
                elif k == 'we':
                    _, c, i = st
                    src = node(dyn(c, turn), QW * i, QW)
                    nc.tensor.matmul(MISCB[:, 0:QW], WPOST[:, 1, :], src, start=True, stop=True).then_inc(sems['misc_written'], 1)
                elif k == 'wq':
                    _, c, i = st
                    nc.tensor.matmul(MISCB[:, 0:QW], WPOST[:, 2, :], QT[i][:, :], start=True, stop=True).then_inc(sems['misc_written'], 1)
                elif k == 'ka':
                    _, c, b = st
                    if c and b == 0:
                        W('wk_in', ('wl_k', c), turn)
                    nc.tensor.matmul(MISCB[:], WK[:, 0, :], node(dyn(c, turn) // (NN - 1), SQ * b, SQ), start=True, stop=True).then_inc(sems['misc_written'], 1)
                elif k == 'kb':
                    nc.tensor.matmul(MISCB[:], WK[:, 1, :], KIN[:], start=True, stop=True).then_inc(sems['misc_written'], 1)
                elif k == 'va':
                    _, c, b = st
                    if c and b == 0:
                        W('wv_in', ('wl_v', c), turn)
                    nc.tensor.matmul(MISCB[:], WV[:, 0, :], node((dyn(c, turn) + 1) // 2, SQ * b, SQ), start=True, stop=True).then_inc(sems['misc_written'], 1)
                elif k == 'vb':
                    for kt in range(4):
                        last = nc.tensor.matmul(MISCB[:, 128 * kt:128 * kt + 128], KIN[:, 128 * kt:128 * kt + 128], WV[:, 1, :], start=(kt == 0), stop=True, skip_group_check=True)
                    last.then_inc(sems['misc_written'], 1)
                elif k == 'fin':
                    i = st[1]
                    for t in (0, 1):
                        last = nc.tensor.transpose(MISCB[:, 128 * t:128 * t + 128], node(NN, QW * i + 128 * t, 128), IDENT[:])
                    last.then_inc(sems['misc_written'], 1)
                elif k == 'moe':
                    pe_moe()

            def pe_moe():
                W('misc_read', ('xT', 'M', 0, CH - 1), None)
                pe.wait_ge(sems['load_m'], 16 * 5)
                for t in range(NT):
                    last = nc.tensor.matmul(MISCB[:, NE * t:NE * t + NE], node(0, 128 * t, 128), WR[:, :], start=(t == 0), stop=True, skip_group_check=True)
                last.then_inc(sems['log_done'], 1)
                pe.wait_ge(sems['w_ready'], 1)
                mh = MISCB[:, :].bitcast(f16)
                for t in range(NT):
                    last = nc.tensor.transpose(mh[:, 128 * t:128 * t + 128], WP[:, t, :, :].rearrange("p a e -> p (a e)"), IDH[:])
                last.then_inc(sems['wT_done'], 1)
                pe.wait_ge(sems['wT_copied'], 1)
                pe.wait_ge(sems['load_d'], 48)

                def down(n):
                    p, h = divmod(n, 2)
                    rows = 128 if p < NP else FE
                    pe.wait_ge(sems['ht_done'], n + 1)
                    y = OT[:, :, :].rearrange("p a t -> p (a t)") if h == 0 else MISCB[:, :]
                    w = WD[:, 128 * p:128 * p + 128] if p < NP else WSD
                    last = nc.tensor.matmul(y, w, HT[n % 2][0:rows, :], start=(p == 0), stop=(p == NP))
                    if p == NP:
                        last.then_inc(sems['y_done'], 1)

                for n in range(2 * NP + 2):
                    p, h = divmod(n, 2)
                    tok = node(0, 512 * h, 512)
                    gb, ub = (ST[n % 2][:, 0:2, :].rearrange("p a t -> p (a t)"), ST[n % 2][:, 2:4, :].rearrange("p a t -> p (a t)"))
                    if n >= 2:
                        pe.wait_ge(sems['ht_done'], n - 1)
                    if p < NP:
                        nc.tensor.matmul(gb, WG[:, 128 * p:128 * p + 128], tok, start=True, stop=True).then_inc(sems['gu_done'], 1)
                        nc.tensor.matmul(ub, WU[:, 128 * p:128 * p + 128], tok, start=True, stop=True)
                        nc.tensor.matmul(S[n % 2][:], SELE[:, p, :], WT[:, 512 * h:512 * h + 512], start=True, stop=True).then_inc(sems['wb_done'], 1)
                    else:
                        nc.tensor.matmul(gb[0:FE, :], WS[:, 0:FE], tok, start=True, stop=True).then_inc(sems['gu_done'], 1)
                        nc.tensor.matmul(ub[0:FE, :], WS[:, FE:2 * FE], tok, start=True, stop=True).then_inc(sems['wb_done'], 1)
                    if n >= 1:
                        down(n - 1)
                down(2 * NP + 1)
                pe.wait_ge(sems['yt_copied'], 2)
                for t in range(NT):
                    y = (ST[0] if t < 4 else ST[1])[:, 0:2, :].rearrange("p a t -> p (a t)")
                    last = nc.tensor.transpose(y[:, 128 * (t % 4):128 * (t % 4) + 128], YT[:, 128 * t:128 * t + 128], IDENT[:])
                    if t % 4 == 3:
                        last.then_inc(sems['y_tok'], 1)

            run(pe, emit)

        @block.scalar
        def _(act):
            W = lambda name, st, turn: act.wait_ge(sems[name], count(name, st, turn))

            def emit(st, turn):
                k = st[0]
                if k == 'init':
                    act.wait_ge(sems['load_c'], 16 * 12)
                    act.wait_ge(sems['load_w'], 16 * 3)
                    nc.scalar.activation(TG[:], GALL[:], ACT.Tanh).then_inc(sems['tg_ready'], 1)
                elif k == 'xk':
                    _, L, b = st
                    W('misc_written', st, turn)
                    if ordinal[st]:
                        o = by_ordinal['ks'][ordinal[st] - 1]
                        W(keys_sem('out', o), ('kw',) + o[1:], turn)
                    nc.scalar.activation(KP[:, 0, 0:SK], MISCB[:, 0:SK], ACT.Identity, bias=XB[:, L, 1:2])
                    nc.scalar.activation(KX[:, 0:SK], MISCB[:, 0:SK], ACT.Identity, bias=XB[:, L, 1:2]).then_inc(sems['misc_read'], 1)
                elif k == 'xT':
                    i = st[3]
                    W('misc_written', st, turn)
                    nc.scalar.activation(node(0, QW * i, QW), MISCB[:, 0:QW], ACT.Copy).then_inc(sems['misc_read'], 1)
                elif k in ('xq', 'wq'):
                    W('misc_written', st, turn)
                    q = ('qs', 'X' if k == 'xq' else 'F') + st[1:]
                    n = ordinal[q]
                    if n >= 2:
                        W('q_split', by_ordinal['qs'][n - 2], turn)
                        o = by_ordinal['qs'][n - 2]
                        W(f'q_out{o[-1]}', ('qw',) + o[1:], turn)
                    if k == 'xq':
                        nc.scalar.activation(QP[n % 2][:, 0, :], MISCB[:, 0:QW], ACT.Identity, bias=XB[:, st[1], 0:1])
                        nc.scalar.activation(QX[n % 2][:], MISCB[:, 0:QW], ACT.Identity, bias=XB[:, st[1], 0:1]).then_inc(sems['misc_read'], 1)
                    else:
                        nc.scalar.activation(QP[n % 2][:, 0, :], MISCB[:, 0:QW], ACT.Copy)
                        nc.scalar.activation(QX[n % 2][:], MISCB[:, 0:QW], ACT.Copy).then_inc(sems['misc_read'], 1)
                elif k == 'mT':
                    n = group_at[st[1:]]
                    W('misc_written', st, turn)
                    if n >= 4:
                        W(rows_sem(('md',) + group_order[n - 4][1:]), ('md',) + group_order[n - 4][1:], turn)
                    nc.scalar.activation(MT[n % 4][:], MISCB[:, :].bitcast(bf16)[0:3 * G, 0:QW], ACT.Copy).then_inc(sems['misc_read'], 1)
                elif k == 'st':
                    _, kind, L, s, g, kt = st
                    n = ordinal[st]
                    W('st_done', st, turn)
                    if n >= PR:
                        W('pv_done', ('pv',) + tile_order[n - PR][1:], turn)
                    rows = SK if kind == 'X' else 128
                    nc.scalar.activation(PT[n % PR][0:rows, :, :], ST[n % 2][0:rows, :, :], ACT.Exp, scale=float(DH[kind]) ** -0.5).then_inc(sems['exp_done'], 1)
                elif k == 'otc':
                    _, kind, L, s = st
                    W('pv_done', ('pv', kind, L, s, 1, KT[kind] - 1), turn)
                    n = ordinal[st]
                    if n >= 2:
                        W('misc_written', ('otT',) + by_ordinal['otc'][n - 2][1:], turn)
                    nc.scalar.activation(OTS[n % 2][:, :, :], OT[:, :, :], ACT.Copy).then_inc(sems['ot_copied'], 1)
                elif k == 'ctxT':
                    W('misc_written', st, turn)
                    nc.scalar.activation(CTXT[st[3] % 2][:], MISCB[:, 0:QW], ACT.Copy).then_inc(sems['misc_read'], 1)
                elif k == 'kb':
                    _, c, b = st
                    W('misc_written', st, turn)
                    ks = ('ks', 'F', c, b)
                    o = by_ordinal['ks'][ordinal[ks] - 1]
                    W(keys_sem('out', o), ('kw',) + o[1:], turn)
                    nc.scalar.activation(KP[:, 0, :], MISCB[:], ACT.Copy)
                    nc.scalar.activation(KX[:], MISCB[:], ACT.Copy).then_inc(sems['misc_read'], 1)
                elif k == 'vb':
                    _, c, b = st
                    W('misc_written', st, turn)
                    if c:
                        W('pv_done', ('pv', 'F', 0, CH * (c - 1) + 2 * b + 1, 1, 3), turn)
                    nc.scalar.activation(VF[b][:, :, :, 0:16], MISCB[:, :].rearrange("p (k h d) -> p k h d", k=4, h=8), ACT.Copy).then_inc(sems['misc_read'], 1)
                elif k == 'moe':
                    act_moe()

            def act_moe():
                act.wait_ge(sems['log_done'], 1)
                nc.scalar.activation(SC, MISCB[:, :].rearrange("p (t e) -> p t e", t=NT), ACT.Tanh, scale=0.5).then_inc(sems['sig_done'], 1)
                act.wait_ge(sems['wT_done'], 1)
                nc.scalar.activation(WT, MISCB[:, :].bitcast(f16), ACT.Copy).then_inc(sems['wT_copied'], 1)
                for n in range(2 * NP + 2):
                    rows = 128 if n // 2 < NP else FE
                    act.wait_ge(sems['gu_done'], n + 1)
                    nc.scalar.activation(SG[n % 2][0:rows, :], ST[n % 2][0:rows, 0:2, :].rearrange("p a t -> p (a t)"), ACT.Silu).then_inc(sems['silu_done'], 1)
                act.wait_ge(sems['y_done'], 2)
                nc.scalar.activation(YT[:, 0:512], OT[:, :, :].rearrange("p a t -> p (a t)"), ACT.Copy).then_inc(sems['yt_copied'], 1)

            run(act, emit)

        @block.vector
        def _(dve):
            W = lambda name, st, turn: dve.wait_ge(sems[name], count(name, st, turn))
            steps_in_turn = [0]
            done = [0, 0]

            def link(ins, turn):
                ins.then_inc(sems['dve_step'], 1)
                done[0] += 1
                v = done[0]
                if turn is not None:
                    v = v + turn * dve_per_turn
                dve.wait_ge(sems['dve_step'], v)

            dve_per_turn = sum({'mp': 3, 'otT': 1}.get(s_[0], 0) for s_ in turns[0])

            def emit(st, turn):
                k = st[0]
                if k == 'init':
                    for b in (0, 1):
                        nc.vector.memset(VF[b][:, :, :, 16:32], 1.0)
                    nc.vector.memset(NEGHALF[:], -0.5)
                    for L in (0, 1):
                        for b in (0, 1):
                            link(nc.vector.memset(VX[L][b][:, :, :], 1.0), turn)
                    dve.wait_ge(sems['load_c'], 16 * 12)
                    dve.wait_ge(sems['load_f'], 16 * 8)
                    link(nc.vector.tensor_tensor(EWBE[:], EW[:], BE[:], ALU.mult), turn)
                    nc.vector.memset(REC[0][:, :, :], 0.0).then_inc(sems['ready'], 1)
                    dve.wait_ge(sems['load_x'], 16)
                    dve.wait_ge(sems['tg_ready'], 1)
                elif k == 'xv':
                    _, L, b = st
                    W('misc_written', st, turn)
                    nc.vector.tensor_tensor(VX[L][b][0:SK, :, 0:8], MISCB[0:SK, 0:D].rearrange("p (h d) -> p h d", h=16),
                                            XBV[0:SK, L, 0, :].rearrange("p (h d) -> p h d", h=16), ALU.add).then_inc(sems['misc_read'], 1)
                elif k == 'ls':
                    _, kind, L, i = st
                    stats([X[:, 2 * i + t, :] for t in (0, 1)], 1e-5, i, turn)
                elif k == 'ln':
                    _, kind, L, i = st
                    n = ordinal[st] % 2
                    if ordinal[st] >= 2:
                        W('misc_written', ('xT',) + by_ordinal['ln'][ordinal[st] - 2][1:], turn)
                    W('rstd_ready', ('ls',) + st[1:], turn)
                    for t in (0, 1):
                        last = nc.vector.tensor_scalar(XN[n][:, t, :], X[:, 2 * i + t, :], MV[i][:, t, 0:1], RSTD[i][:, t:t + 1], ALU.subtract, ALU.mult)
                    last.then_inc(sems['xn_ready'], 1)
                elif k == 's':
                    _, kind, L, s, g, j = st
                    n = ordinal[st]
                    m = NM[group_at[kind, L, s, g] % 4]
                    W('s_done', st, turn)
                    if kind == 'X':
                        nc.vector.tensor_reduce(m[:, j, :], S[n % 2][:, 0:G * SK].rearrange("p (r t) -> p r t", r=G), AX.X, ALU.max, negate=True).then_inc(sems['max_done'], 1)
                    else:
                        t, r = divmod(j, 4)
                        nc.vector.tensor_reduce(m[:, t, r:r + 1], S[n % 2][:], AX.X, ALU.max, negate=True).then_inc(sems['max_done'], 1)
                elif k == 'mp':
                    _, kind, L, s, g = st
                    n = group_at[st[1:]] % 4
                    W('max_done', ('s', kind, L, s, g, 1 if kind == 'X' else 7), turn)
                    link(nc.vector.tensor_copy(MP[n][:, :, 0, :], NM[n][:, :, :]), turn)
                    link(nc.vector.tensor_tensor(MR[n][:, :, :], NM[n][:, :, :], MP[n][:, :, 0, :], ALU.subtract), turn)
                    link(nc.vector.tensor_copy(MP[n][:, :, 1, :], MR[n][:, :, :]), turn)
                    nc.vector.tensor_tensor(MP[n][:, :, 2, :], MR[n][:, :, :], MP[n][:, :, 1, :], ALU.subtract).then_inc(sems['mparts'], 1)
                elif k == 'otT':
                    _, kind, L, s = st
                    n = ordinal[st]
                    i = chain_of(kind, s)
                    d = DH[kind]
                    W('misc_written', st, turn)
                    o = MISCB[:, :].rearrange("p (t h e) -> p t h e", t=2, h=8)
                    link(nc.vector.reciprocal(REC[n % 2][:, :, :], o[:, :, :, d]), turn)
                    lo = 64 * (s % 2) if kind == 'X' else 0
                    c = CTX[i % 2][:, :, lo:lo + 8 * d].rearrange("p t (h e) -> p t h e", h=8)
                    nc.vector.tensor_tensor(c, o[:, :, :, 0:d], REC[n % 2][:, :, :].unsqueeze(3).broadcast_to([128, 2, 8, d]), ALU.mult).then_inc(sems['misc_read'], 1)
                elif k == 'wox':
                    _, L, i = st
                    W('misc_written', st, turn)
                    n = i % 2
                    link(nc.vector.tensor_tensor(XN[n][:, :, :], MISCB[:, 0:QW].rearrange("p (t d) -> p t d", t=2),
                                                 XBV[:, L, 1, :].unsqueeze(1).broadcast_to([128, 2, D]), ALU.add), turn)
                    link(nc.vector.scalar_tensor_tensor(X[:, 2 * i:2 * i + 2, :], XN[n][:, :, :], TG[:, L:L + 1], X[:, 2 * i:2 * i + 2, :], ALU.mult, ALU.add), turn)
                    nc.vector.memset(REC[0][:, :, 0:1], 1.0).then_inc(sems['misc_read'], 1)
                elif k == 'wo':
                    _, c, i = st
                    W('misc_written', st, turn)
                    nc.vector.scalar_tensor_tensor(node(dyn(c, turn) + 1, QW * i, QW), MISCB[:, 0:QW], ACTW[:, bass.ds(dyn(c, turn), 1)], QT[i][:, :], ALU.mult, ALU.add).then_inc(sems['misc_read'], 1)
                elif k == 'we':
                    _, c, i = st
                    W('misc_written', st, turn)
                    col = dyn(c, turn) * 3
                    nc.vector.tensor_scalar(QT[i][:, :], MISCB[:, 0:QW], BE[:, bass.ds(col, 1)], EW[:, bass.ds(col, 1)], ALU.add, ALU.mult).then_inc(sems['misc_read'], 1)
                elif k in ('ka', 'va'):
                    _, c, b = st
                    W('misc_written', st, turn)
                    col = dyn(c, turn) * 3 + (1 if k == 'ka' else 2)
                    nc.vector.tensor_scalar(KIN[:], MISCB[:], BE[:, bass.ds(col, 1)], EW[:, bass.ds(col, 1)], ALU.add, ALU.mult).then_inc(sems['misc_read'], 1)
                elif k == 'fin':
                    i = st[1]
                    W('misc_written', st, turn)
                    ins = nc.vector.tensor_copy(FT[i % 2][:, :, :], MISCB[:, 0:QW].rearrange("p (t d) -> p t d", t=2))
                    ins.then_inc(sems['misc_read'], 1)
                    W('misc_read', st, turn)
                    stats([FT[i % 2][:, t, :] for t in (0, 1)], 1e-6, i, turn)
                elif k == 'fl':
                    i = st[1]
                    W('rstd_ready', ('fin', i), turn)
                    last_norm(i, turn)
                elif k == 'moe':
                    dve_moe()

            def stats(src, eps, i, turn):
                for t in (0, 1):
                    last = nc.vector.bn_stats(BNS[i][:, t, :], src[t])
                link(last, turn)
                for t in (0, 1):
                    last = nc.vector.bn_aggr(MV[i][:, t, :], BNS[i][:, t, :])
                link(last, turn)
                nc.vector.tensor_scalar(VE[i][:], MV[i][:, :, 1], eps, None, ALU.add).then_inc(sems['var_ready'], 1)

            def last_norm(i, turn):
                n = i % 2
                y, xx = FT[n][:, :, :], X[:, 2 * i:2 * i + 2, :]
                for t in (0, 1):
                    last = nc.vector.tensor_scalar(FT[n][:, t, :], FT[n][:, t, :], MV[i][:, t, 0:1], RSTD[i][:, t:t + 1], ALU.subtract, ALU.mult)
                link(last, turn)
                link(nc.vector.tensor_tensor(y, y, LNGB[:, 0, :].unsqueeze(1).broadcast_to([128, 2, D]), ALU.mult), turn)
                link(nc.vector.tensor_tensor(y, y, LNGB[:, 1, :].unsqueeze(1).broadcast_to([128, 2, D]), ALU.add), turn)
                link(nc.vector.scalar_tensor_tensor(xx, y, TG[:, 2:3], xx, ALU.mult, ALU.add), turn)

            def first_of(sel, gt, eq, cum, src, thr, k, width, flat):
                n = NT
                b = thr.unsqueeze(2).broadcast_to([128, n, width])
                link(nc.vector.tensor_tensor(gt, src, b, ALU.is_gt), None)
                link(nc.vector.tensor_tensor(eq, src, b, ALU.is_equal), None)
                link(nc.vector.tensor_reduce(NEED[:, :], gt, AX.X, ALU.add), None)
                link(nc.vector.tensor_scalar(NEED[:, :], NEED[:, :], -1.0, float(k), ALU.mult, ALU.add), None)
                for t in range(n):
                    last = nc.vector.tensor_tensor_scan(cum[:, t, :], ONES64[:, 0:width], eq[:, t, :], 0.0, ALU.mult, ALU.add)
                link(last, None)
                link(nc.vector.tensor_tensor(cum, cum, NEED[:, :].unsqueeze(2).broadcast_to([128, n, width]), ALU.is_le), None)
                link(nc.vector.tensor_tensor(eq, eq, cum, ALU.mult), None)
                link(nc.vector.tensor_tensor(sel, gt, eq, ALU.add), None)

            NEED = SM[:, 0:8]
            ONES64 = SM[:, 8:72]
            GS = SM[:, 72:136].rearrange("p (t g) -> p t g", t=NT)
            GG = [SM[:, 136 + 64 * a:200 + 64 * a].rearrange("p (t g) -> p t g", t=NT) for a in range(4)]
            M8G = SM[:, 392:456].rearrange("p (t g) -> p t g", t=NT)
            SUM = SM[:, 456:464]

            def dve_moe():
                dve.wait_ge(sems['sig_done'], 1)
                link(nc.vector.memset(ONES64, 1.0), None)
                link(nc.vector.tensor_scalar(SC, SC, 0.5, 0.5, ALU.mult, ALU.add), None)
                link(nc.vector.tensor_tensor(SWB, SC, BR[:, :].unsqueeze(1).broadcast_to([128, NT, NE]), ALU.add), None)
                for t in range(NT):
                    for g in range(8):
                        last = nc.vector.max(M8[:, t, g, :], SWB[:, t, 8 * g:8 * g + 8])
                link(last, None)
                link(nc.vector.tensor_tensor(GS, M8[:, :, :, 0], M8[:, :, :, 1], ALU.add), None)
                for t in range(NT):
                    last = nc.vector.max(M8G[:, t, :], GS[:, t, :])
                link(last, None)
                first_of(GG[3], GG[0], GG[1], GG[2], GS, M8G[:, :, 3], 4, 8, None)
                link(nc.vector.tensor_tensor(SWB.rearrange("p t (g e) -> p t g e", g=8), SWB.rearrange("p t (g e) -> p t g e", g=8),
                                             GG[3].unsqueeze(3).broadcast_to([128, NT, 8, 8]), ALU.mult), None)
                for t in range(NT):
                    last = nc.vector.max(M8G[:, t, :], SWB[:, t, :])
                link(last, None)
                first_of(MSK, GT, EQ, CUM, SWB, M8G[:, :, 7], 8, NE, None)
                link(nc.vector.tensor_tensor(SC, SC, MSK, ALU.mult), None)
                link(nc.vector.tensor_reduce(SUM, SC, AX.X, ALU.add), None)
                link(nc.vector.tensor_scalar(SUM, SUM, 1e-20, None, ALU.add), None)
                link(nc.vector.reciprocal(SUM, SUM), None)
                link(nc.vector.tensor_scalar(SC, SC, 2.5, None, ALU.mult), None)
                link(nc.vector.tensor_tensor(SC, SC, SUM.unsqueeze(2).broadcast_to([128, NT, NE]), ALU.mult), None)
                link(nc.vector.tensor_copy(WP[:, :, 0, :], SC), None)
                link(nc.vector.tensor_tensor(SC, SC, WP[:, :, 0, :], ALU.subtract), None)
                nc.vector.tensor_scalar(WP[:, :, 1, :], SC, SHIFT, None, ALU.mult).then_inc(sems['w_ready'], 1)
                for n in range(2 * NP + 2):
                    shared = n // 2 == NP
                    rows = FE if shared else 128
                    dve.wait_ge(sems['wb_done'], n + 1)
                    dve.wait_ge(sems['silu_done'], n + 1)
                    u = ST[n % 2][0:rows, 2:4, :].rearrange("p a t -> p (a t)")
                    if shared:
                        nc.vector.tensor_tensor(HT[n % 2][0:rows, :], SG[n % 2][0:rows, :], u, ALU.mult).then_inc(sems['ht_done'], 1)
                    else:
                        link(nc.vector.tensor_tensor(T1[n % 2], SG[n % 2], u, ALU.mult), None)
                        nc.vector.tensor_tensor(HT[n % 2], T1[n % 2], S[n % 2][:], ALU.mult).then_inc(sems['ht_done'], 1)
                dve.wait_ge(sems['y_done'], 2)
                nc.vector.tensor_copy(YT[:, 512:1024], MISCB[:]).then_inc(sems['yt_copied'], 1)
                for h in (0, 1):
                    dve.wait_ge(sems['y_tok'], h + 1)
                    y = ST[h][:, 0:2, :].rearrange("p a t -> p (a t)")
                    xx = X[:, 4 * h:4 * h + 4, :].rearrange("p t d -> p (t d)")
                    nc.vector.scalar_tensor_tensor(xx, y, TG[:, 3:4], xx, ALU.mult, ALU.add).then_inc(sems['y_added'], 1)

            def after_loop():
                done[0] += (NN - 2) * dve_per_turn

            run(dve, emit, after_loop)

        @block.gpsimd
        def _(pool):
            W = lambda name, st, turn: pool.wait_ge(sems[name], count(name, st, turn))
            done = [0]
            pool_per_turn = sum({'qs': 2, 'ks': 2}.get(s_[0], 0) for s_ in turns[0])

            def link(ins, turn):
                ins.then_inc(sems['pool_step'], 1)
                done[0] += 1
                pool.wait_ge(sems['pool_step'], done[0] if turn is None else done[0] + turn * pool_per_turn)

            def parts(src, p, r, signal, turn):
                link(nc.gpsimd.tensor_tensor(r, src, p[0], ALU.subtract), turn)
                link(nc.gpsimd.tensor_tensor(p[1], r, ZERO[:, 0:1].broadcast_to([128, r.shape[1]]), ALU.add), turn)
                nc.gpsimd.tensor_tensor(p[2], r, p[1], ALU.subtract).then_inc(signal, 1)

            def emit(st, turn):
                k = st[0]
                if k == 'init':
                    for L in (0, 1):
                        for b in (0, 1):
                            nc.gpsimd.memset(KAX[L][b][:, :, :], 0.0).then_inc(sems['zeroed'], 1)
                    for i in range(CH):
                        nc.gpsimd.memset(QA[i][:, :, :].rearrange("p h t -> p (h t)").bitcast(u32), 0).then_inc(sems['zeroed'], 1)
                    link(nc.gpsimd.memset(ZERO[:, :], 0.0), turn)
                elif k in ('ls', 'fin'):
                    i = st[-1]
                    W('var_ready', st, turn)
                    nc.gpsimd.tensor_tensor(RSTD[i][:], VE[i][:], NEGHALF[:], ALU.pow).then_inc(sems['rstd_ready'], 1)
                elif k == 'qs':
                    _, kind, c, i = st
                    n = ordinal[st]
                    W('misc_read', ('xq', c, i) if kind == 'X' else ('wq', c, i), turn)
                    if n:
                        W('q_split', by_ordinal['qs'][n - 1], turn)
                    parts(QX[n % 2][:], [QP[n % 2][:, a, :] for a in range(3)], QR[:], sems['q_split'], turn)
                elif k == 'ks':
                    _, kind, c, b = st
                    n = ordinal[st]
                    W('misc_read', ('xk', c, b) if kind == 'X' else ('kb', c, b), turn)
                    w = SK if kind == 'X' else SQ
                    if n:
                        W('k_split', by_ordinal['ks'][n - 1], turn)
                    parts(KX[:, 0:w], [KP[:, a, 0:w] for a in range(3)], KRS[:, 0:w], sems['k_split'], turn)

            def after_loop():
                done[0] += (NN - 2) * pool_per_turn

            run(pool, emit, after_loop)

        @block.sync
        def _(sp):
            W = lambda name, st, turn: sp.wait_ge(sems[name], count(name, st, turn))

            def blocks(dst, dram, order, d, heads, sem_, w):
                for j in range(6):
                    sp.dma_start(dst[d * j:d * j + d, 0:heads, 0:w], dram[order[j]].rearrange("(h d) t -> d h t", d=d)).then_inc(sem_, 16)

            def emit(st, turn):
                k = st[0]
                if k == 'init':
                    sp.dma_start(X[:, :, :], x).then_inc(sems['load_x'], 16)
                    for dst, src in ((CT[:, :, :], ctx_t.rearrange("b d s -> d b s")), (XB[:, :, :], x_bqk), (XBV[:, :, :, :], x_bvo), (GALL[:], g_all),
                                     (IDENT[:], c_ident), (IDB[:], c_ident_bf), (IDH[:], c_ident_h)):
                        sp.dma_start(dst, src).then_inc(sems['load_c'], 16)
                    sp.dma_start(XW[:, :, 0, :], x_wq).then_inc(sems['load_w'], 16)
                    sp.dma_start(XW[:, :, 3, :], x_wo).then_inc(sems['load_w'], 16)
                    sp.dma_start(XW[0:DC, :, 1:3, :], x_wkv).then_inc(sems['load_w'], 16)
                    sp.wait_ge(sems['zeroed'], 4)
                    for L in (0, 1):
                        for b in (0, 1):
                            sp.dma_start(KAX[L][b][ROWS_M:KR, :, :], c_sel_x).then_inc(sems['load_c'], 16)
                    sp.dma_start(LNGB[:, :, :], ln_gb).then_inc(sems['load_c'], 16)
                    for dst, src in ((EW[:], f_ew), (BE[:], f_be), (ACTW[:], f_actw), (WPOST[:, :, :], f_wpost[0]), (WK[:, :, :], f_wk[0]), (WV[:, :, :], f_wv[0]),
                                     (KAF[0][ROWS_M:KR, :, :], c_sel_f), (KAF[1][ROWS_M:KR, :, :], c_sel_f)):
                        sp.dma_start(dst, src).then_inc(sems['load_f'], 16)
                elif k == 'we_first':
                    for dst, src in ((WR[:], w_router), (BR[:], b_router), (WG[:], moe_gate), (WU[:], moe_up), (WS[:], sh_gate_up)):
                        sp.dma_start(dst, src).then_inc(sems['load_m'], 16)
                elif k == 'qw':
                    _, kind, c, i = st
                    qs = ('qs',) + st[1:]
                    W('q_split', qs, turn)
                    sp.dma_start(qd[i].rearrange("a p t -> p a t"), QP[ordinal[qs] % 2][:, :, :]).then_inc(sems[f'q_out{i}'], 16)
                elif k == 'qr':
                    _, kind, c, i = st
                    if kind == 'X' and c == 0 and i == 0:
                        sp.wait_ge(sems['zeroed'], 8)
                    W(f'q_out{i}', ('qw',) + st[1:], turn)
                    blocks(QA[i], qd[i], QPART, DH[kind], HEADS[kind], sems[f'q_in{i}'], QW)
                elif k == 'kw':
                    _, kind, c, b = st
                    W('k_split', ('ks',) + st[1:], turn)
                    if kind == 'X':
                        sp.dma_start(kdx[c][b].rearrange("a p t -> p a t"), KP[:, :, 0:SK]).then_inc(sems[keys_sem('out', st)], 16)
                    else:
                        sp.dma_start(kd[b].rearrange("a p t -> p a t"), KP[:, :, :]).then_inc(sems[keys_sem('out', st)], 16)
                elif k == 'kr':
                    _, kind, c, b = st
                    written = count(keys_sem('out', st), ('kw',) + st[1:], turn)
                    read = count('st_done', ('st', 'F', 0, CH * (c - 1) + 2 * b + 1, 1, 3), turn) if kind == 'F' and c else None
                    if turn is not None:
                        read = sp.snap(sp.to_reg(read))
                    sp.wait_ge(sems[keys_sem('out', st)], written)
                    if kind == 'X':
                        blocks(KAX[c][b], kdx[c][b], KPART, 8, 16, sems[keys_sem('in', st)], SK)
                    else:
                        if read is not None:
                            sp.wait_ge(sems['st_done'], read)
                        blocks(KAF[b], kd[b], KPART, 16, 8, sems[keys_sem('in', st)], SQ)
                elif k == 'md':
                    _, kind, L, s, g = st
                    n = group_at[st[1:]] % 4
                    i, h = chain_of(kind, s), head0(kind, s, g)
                    W('misc_read', ('mT',) + st[1:], turn)
                    sp.dma_start(QA[i][ROWS_M:KR, h:h + G, :], MT[n][:, :].unsqueeze(1).broadcast_to([3 * G, G, QW])).then_inc(sems[rows_sem(st)], 16)
                elif k == 'wl_post':
                    c = st[1]
                    src = wrow(f_wpost, dyn(c + 1, turn))
                    W('misc_written', ('wq', c, CH - 1), turn)
                    sp.wait_ge(sems['load_f'], 16 * 8)
                    sp.dma_start(WPOST[:, :, :], src).then_inc(sems['wpost_in'], 16)
                elif k == 'wl_v':
                    c = st[1]
                    src = wrow(f_wv, dyn(c, turn))
                    W('misc_written', ('vb', c - 1, 1), turn)
                    sp.wait_ge(sems['load_f'], 16 * 8)
                    sp.dma_start(WV[:, :, :], src).then_inc(sems['wv_in'], 16)
                elif k == 'wl_k':
                    c = st[1]
                    src = wrow(f_wk, dyn(c, turn))
                    W('misc_written', ('kb', c - 1, 1), turn)
                    sp.wait_ge(sems['load_f'], 16 * 8)
                    sp.dma_start(WK[:, :, :], src).then_inc(sems['wk_in'], 16)
                elif k == 'fin' and st[1] == CH - 1:
                    W('misc_read', st, turn)
                    sp.dma_start(SELE, c_sel_e).then_inc(sems['load_d'], 16)
                    sp.dma_start(WD, moe_down).then_inc(sems['load_d'], 16)
                    sp.dma_start(WSD, sh_down).then_inc(sems['load_d'], 16)
                elif k == 'moe':
                    for h in (0, 1):
                        sp.wait_ge(sems['y_added'], h + 1)
                        sp.dma_start(out[:, 4 * h:4 * h + 4, :], X[:, 4 * h:4 * h + 4, :]).then_inc(sems['out_done'], 16)
                    sp.wait_ge(sems['out_done'], 32)

            def wrow(w, c):
                if isinstance(c, int):
                    return w[c]
                return w.rearrange("c p a n -> (c p) a n")[bass.ds(sp.snap(c * 128), 128)]

            run(sp, emit)


LOOP = True
_OUT = ((2, 512, 128), 'float32')


def kernel(**inputs):
    import numpy as np
    import concourse.bacc as bacc
    from concourse import mybir as _mybir
    from concourse.bass_utils import run_bass_kernel_spmd as run_spmd

    a = {k: np.asarray(v) for k, v in inputs.items()}
    f = np.float32
    NT, D = 8, 128

    def rows(v, n=128):
        return np.ascontiguousarray(np.broadcast_to(v, (n,) + v.shape))

    edge, lind = [], 0
    for c in range(6):
        n = min(c + 1, 5)
        edge.append((lind + n - 1, lind, lind + n // 2))
        lind += n
    We, be, Wq, Wk, Wv, Wo = (a[f'L0_ffn_{n}'] for n in ('We', 'be', 'Wq', 'Wk', 'Wv', 'Wo'))

    def side(*m):
        return np.stack(m, axis=1)
    wpost = [side(Wo[0], We[edge[0][0]], Wq[0])]
    for c in range(6):
        nx = min(c + 1, 5)
        wpost.append(side(Wo[c], We[edge[nx][0]], Wq[nx]))
    wk = [side(We[edge[c][1]], Wk[c]) for c in range(6)]
    wk.append(wk[-1])
    wv = [side(We[edge[c][2]], Wv[c]) for c in range(6)]
    xl = [{n: a[f'L0_xattn_{n.lower()}' if L == 0 else f'L1_xattn_{n}'] for n in ('Wq', 'bq', 'Wk', 'bk', 'Wv', 'bv', 'Wo', 'bo')} for L in (0, 1)]

    one = np.uint16(0x3F80)
    sel_x = np.zeros((12, 16, 77), np.uint16)
    sel_f = np.zeros((12, 8, 512), np.uint16)
    for p in range(3):
        for r in range(4):
            sel_x[4 * p + r, r::4, :] = one
            sel_f[4 * p + r, r::4, :] = one
    sel_e = np.zeros((128, 32, 128), np.float16)
    for e in range(64):
        sel_e[e, e // 2, 64 * (e % 2):64 * (e % 2) + 64] = 1.0
        sel_e[64 + e, e // 2, 64 * (e % 2):64 * (e % 2) + 64] = 1.0 / 2048.0

    arrays = [
        ('x', a['x'].reshape(NT, 128, D).transpose(1, 0, 2)),
        ('ctx_t', a['ctx_768'].transpose(0, 2, 1)),
        ('g_all', rows(np.concatenate([a['g_xattn'], a['g_ffn']]))),
        ('x_wq', side(xl[0]['Wq'], xl[1]['Wq'])),
        ('x_wkv', np.stack([side(xl[L]['Wk'], xl[L]['Wv']) for L in (0, 1)], axis=1)),
        ('x_wo', side(xl[0]['Wo'], xl[1]['Wo'])),
        ('x_bqk', np.stack([np.stack([xl[L]['bq'], xl[L]['bk']], axis=1) for L in (0, 1)], axis=1)),
        ('x_bvo', rows(np.stack([np.stack([xl[L]['bv'], xl[L]['bo']]) for L in (0, 1)]))),
        ('f_wpost', np.stack(wpost)), ('f_wk', np.stack(wk)), ('f_wv', np.stack(wv)),
        ('f_ew', rows(a['L0_ffn_ew'].reshape(-1))),
        ('f_be', be[np.array(edge).reshape(-1)].T),
        ('f_actw', rows(a['L0_ffn_act_w'])),
        ('ln_gb', rows(np.stack([a['L0_ffn_ln_g'], a['L0_ffn_ln_b']]))),
        ('w_router', a['L1_ffn_w_router']), ('b_router', rows(a['L1_ffn_b_router'])),
        ('moe_gate', a['L1_ffn_we_gate'].transpose(1, 0, 2).reshape(D, 64 * 64)),
        ('moe_up', a['L1_ffn_we_up'].transpose(1, 0, 2).reshape(D, 64 * 64)),
        ('moe_down', a['L1_ffn_we_down'].reshape(32, 128, D).transpose(1, 0, 2).reshape(128, 32 * D)),
        ('sh_gate_up', np.concatenate([a['L1_ffn_ws_gate'], a['L1_ffn_ws_up']], axis=1)),
        ('sh_down', a['L1_ffn_ws_down']),
        ('c_ident', np.eye(128, dtype=f)), ('c_ident_bf', np.where(np.eye(128) > 0, one, np.uint16(0)).astype(np.uint16)),
        ('c_sel_x', sel_x), ('c_sel_f', sel_f), ('c_sel_e', sel_e), ('c_ident_h', np.eye(128, dtype=np.float16)),
    ]
    nc = bacc.Bacc("TRN2", target_bir_lowering=False, num_devices=1)
    feeds, args = {}, {}
    for name, arr in arrays:
        arr = np.ascontiguousarray(arr)
        feeds[f"in_{name}"] = arr
        ap = nc.dram_tensor(f"in_{name}", arr.shape, _mybir.dt.from_np(arr.dtype), kind="ExternalInput").ap()
        args[name] = ap.bitcast(_mybir.dt.bfloat16) if arr.dtype == np.uint16 else ap
    out = nc.dram_tensor("out_x", (NT, 128, D), _mybir.dt.float32, kind="ExternalOutput").ap()
    flamingo_gated_two_layer(nc, out=out.rearrange("t p d -> p t d"), **args)
    r = run_spmd(nc, [feeds], core_ids=[0])
    return r.results[0]["out_x"].reshape(_OUT[0])
```

```python
import concourse.bass as bass
from concourse import mybir
from contextlib import ExitStack


def flamingo_gated_two_layer(
    nc,
    x, ctx_t, g_all,
    x_wq, x_wkv, x_wo, x_bqk, x_bvo,
    f_wpost, f_wk, f_wv, f_ew, f_be, f_actw, ln_gb,
    w_router, b_router, moe_gate, moe_up, moe_down, sh_gate_up, sh_down,
    c_ident, c_ident_bf, c_sel_x, c_sel_f, c_sel_e, c_ident_h,
    out,
):
    f32, bf16, f16 = mybir.dt.float32, mybir.dt.bfloat16, mybir.dt.float16
    u32 = mybir.dt.uint32
    ALU = mybir.AluOpType
    ACT = mybir.ActivationFunctionType
    AX = mybir.AxisListType

    D = 128
    NT = x.shape[1]
    CH = 4
    QW = NT * 128 // CH
    B = 2
    SQ = NT * 128 // B
    SK = ctx_t.shape[2]
    DC = ctx_t.shape[1]
    NN = 6
    G = 4
    ROWS_M = 96
    KR = ROWS_M + 3 * G
    NP = 32
    NE = 64
    FE = 64
    PIECE = NE * FE // (2 * (NN - 1)) // 128 * 128
    REST = NE * FE - 2 * (NN - 1) * PIECE
    WSCALE, XSCALE = 64.0, 1024.0
    SHIFT = 2048.0
    QPART = (0, 0, 0, 1, 1, 2)
    KPART = (0, 1, 2, 0, 1, 0)
    HEADS = {'X': 16, 'F': 8}
    DH = {'X': 8, 'F': 16}
    KT = {'X': 1, 'F': 4}
    PR = 4

    def x_slots(L, extras, follow):
        n = 4 * CH
        slots = dict(extras)

        def put(q, *steps):
            slots[q] = list(slots.get(q, [])) + list(steps)

        for s in range(2 * CH):
            put(2 * s + 3, ('otT', 'X', L, s))
            if s % 2:
                put(2 * s + 4, ('ctxT', 'X', L, s // 2))
                put(2 * s + 5, ('wox', L, s // 2))
                for k, steps in enumerate(follow(s // 2)):
                    put(2 * s + 5 + k, *steps)
        st = []
        for q in range(-4, max(slots) + 1):
            if 0 <= q < n:
                st.append(('st', 'X', L, q // 2, q % 2, 0))
            if q + 4 < n:
                at = ('X', L, (q + 4) // 2, q % 2)
                st += [('s',) + at + (t,) for t in (0, 1)] + [('mp',) + at]
            if 0 <= q + 3 < n:
                at = ('X', L, (q + 3) // 2, (q + 3) % 2)
                st += [('mT',) + at, ('md',) + at]
            if 0 <= q - 1 < n:
                st.append(('pv', 'X', L, (q - 1) // 2, (q - 1) % 2, 0))
                if q % 2 == 0:
                    st.append(('otc', 'X', L, (q - 1) // 2))
            st += slots.get(q, [])
        return st

    def x_keys(L, b):
        return [[('xk', L, b), ('ks', 'X', L, b)], [('xv', L, b)], [('kw', 'X', L, b)], [('kr', 'X', L, b)]]

    def x_query(L, i):
        return [[('ls', 'X', L, i)], [('ln', 'X', L, i)], [('xT', 'X', L, i)], [('xq', L, i), ('qs', 'X', L, i)], [('qw', 'X', L, i)], [('qr', 'X', L, i)]]

    def f_query(i):
        b = i // 2
        go = [[('ls', 'F', 0, i)], [('ln', 'F', 0, i)], [('xT', 'F', 0, i)], [('we', 0, i)], [('wq', 0, i), ('qs', 'F', 0, i)], [], [], [], []]
        if i < CH - 1:
            go[5] += [('qw', 'F', 0, i)]
            go[6] += [('qr', 'F', 0, i)]
        if i % 2:
            go[5] += [('ka', 0, b)]
            go[6] += [('kb', 0, b), ('ks', 'F', 0, b)]
            go[7] += [('kw', 'F', 0, b)]
            go[8] += [('kr', 'F', 0, b)]
        if i == 1:
            go[7] += [('va', 0, 0)]
            go[8] += [('vb', 0, 0)]
        return go

    def m_rows(i):
        return [[('ls', 'M', 0, i)], [('ln', 'M', 0, i)]] + [[]] * (i == CH - 2) + [[('xT', 'M', 0, i), ('xs', i)]]

    def f_tiles(s, g):
        return [('s', 'F', 0, s, g, j) for j in range(8)]

    def f_slot(s, extras={}):
        c, i = divmod(s, CH)
        last = CH * NN - 1
        st = []
        pc, pi = divmod(s - 1, CH)
        jobs = {0: [], 1: [('va', c, 1), ('vb', c, 1), ('ka', c + 1, 0), ('kb', c + 1, 0)],
                2: [('ka', c + 1, 1), ('kb', c + 1, 1)], 3: [('va', c + 1, 0), ('vb', c + 1, 0)]}[i]
        jobs = [j for j in jobs if j[1] < NN]
        at = {4: (0, 1, 5, 7), 2: (0, 7), 0: ()}[len(jobs)]
        for p in range(8):
            g, kt = divmod(p, 4)
            if p == 0:
                if i == 1:
                    st.append(('wl_post', c))
                if i == 2 and c + 1 < NN:
                    st.append(('wl_v', c + 1))
                if i == 3 and c + 1 < NN:
                    st.append(('wl_k', c + 2))
            st.append(('st', 'F', 0, s, g, kt))
            if s < last:
                st += [('s', 'F', 0, s + 1, g, 2 * kt), ('s', 'F', 0, s + 1, g, 2 * kt + 1)]
            if p == 1:
                st += [('mT', 'F', 0, s, 1), ('md', 'F', 0, s, 1)]
                if s >= 1 and (s - 2) // CH + 1 < NN:
                    qc, qi = divmod(s - 2, CH)
                    st += [('qw', 'F', qc + 1, qi)]
            if s >= 1:
                if p == 2:
                    st.append(('otT', 'F', 0, s - 1))
                    if i == 2 and c + 1 < NN:
                        st.append(('kw', 'F', c + 1, 0))
                    if s >= 1 and (s - 2) // CH + 1 < NN:
                        qc, qi = divmod(s - 2, CH)
                        st += [('qr', 'F', qc + 1, qi)]
                if p == 3:
                    st.append(('ctxT', 'F', 0, s - 1))
                if p == 4:
                    st.append(('wo', pc, pi))
                if p == 6 and pc + 1 < NN:
                    st += [('we', pc + 1, pi)]
                if p == 7 and pc + 1 < NN:
                    st += [('wq', pc + 1, pi), ('qs', 'F', pc + 1, pi)]
            for n, j in enumerate(jobs):
                if at[n] == p:
                    st.append(j)
                    if j[0] == 'kb':
                        st.append(('ks',) + ('F',) + j[1:])
            if i == 2 and p == 3 and c + 1 < NN:
                st += [('kr', 'F', c + 1, 0)]
            if i == 3 and p == 3 and c + 1 < NN:
                st += [('kw', 'F', c + 1, 1)]
            if i == 0 and p == 3 and c >= 1:
                st += [('kr', 'F', c, 1)]
            if s >= 1 and (s - 1) // CH < NN - 1 and p in (1, 6):
                st.append(('load_part' if p == 1 else 'part_split', (s - 1) // CH, (s - 1) % CH))
            st += extras.get((s, p), [])
            if s < last:
                if p == 3:
                    st.append(('mp', 'F', 0, s + 1, 0))
                if p == 5:
                    st += [('mT', 'F', 0, s + 1, 0), ('md', 'F', 0, s + 1, 0)]
                if p == 7:
                    st.append(('mp', 'F', 0, s + 1, 1))
            if s or p:
                q = 8 * s + p - 1
                st.append(('pv', 'F', 0, q // 8, q % 8 // 4, q % 4))
            if p == 0 and s >= 1:
                st.append(('otc', 'F', 0, s - 1))
        return st

    flat = lambda groups: [st for group in groups for st in group]
    before = [('init',), ('ls', 'X', 0, 0), ('ls', 'X', 0, 1)] + flat(x_keys(0, 0))
    for i in (0, 1):
        before += [('ln', 'X', 0, i), ('xT', 'X', 0, i), ('xq', 0, i), ('qs', 'X', 0, i), ('qw', 'X', 0, i)]
    before += [('qr', 'X', 0, 0), ('qr', 'X', 0, 1), ('ls', 'X', 0, 2), ('ls', 'X', 0, 3)]
    for i in (2, 3):
        before += [('ln', 'X', 0, i), ('xT', 'X', 0, i)]
    def first_query(i):
        return [[('xq', 0, i), ('qs', 'X', 0, i)], [('qw', 'X', 0, i)], [('qr', 'X', 0, i)]]

    more = {}
    for at, groups in ((-4, x_keys(0, 1)), (0, first_query(2)), (3, first_query(3))):
        for k, group in enumerate(groups):
            more[at + k] = more.get(at + k, []) + group
    more[10] = [('load_small',)]
    last_query = f_query(CH - 1)
    more[20] = flat(last_query[:7]) + f_tiles(0, 0) + [('mp', 'F', 0, 0, 0)]
    more[21] = f_tiles(0, 1) + [('mT', 'F', 0, 0, 0), ('md', 'F', 0, 0, 0), ('mp', 'F', 0, 0, 1)] + last_query[7]
    late = {}
    late[0, 1] = last_query[8]
    late[0, 2] = [('load_rest', k) for k in (0, 1)]
    late[0, 7] = [('rest_split', k) for k in (0, 1)]
    late[0, 6] = late.get((0, 6), []) + [('wl_k', 1)]
    before += x_slots(0, more, lambda i: f_query(i) if i < CH - 1 else []) + f_slot(0, late)
    turns = [sum((f_slot(CH * c + i) for i in (1, 2, 3, 4)), []) for c in range(NN - 1)]

    tail = {}
    for i in range(CH):
        go = [[('fin', i)], [('fl', i)]] + x_query(1, i)
        if i == 0:
            go[7:7] = [[], []]
        if i == CH - 1:
            go = [go[0], go[1] + go[2]] + go[3:]
        for k, group in enumerate(go):
            s_, p_ = divmod(8 * (CH * (NN - 1) + 1 + i) + (4 if i == CH - 1 else 5) + k, 8)
            tail.setdefault((s_, p_), []).extend(group)
    first = CH * (NN - 1) + 1
    for k, group in enumerate(x_keys(1, 0) + x_keys(1, 1) + [[('load_down', k)] for k in range(4)]):
        at = divmod(8 * first + k + 2, 8)
        tail[at] = tail.get(at, []) + group
    after = sum((f_slot(CH * (NN - 1) + i, tail) for i in (1, 2, 3)), [])
    n = CH * NN
    after += [('pv', 'F', 0, n - 1, 1, 3), ('otc', 'F', 0, n - 1)]
    early = {-4: tail.get((n, 0), []), -3: [('otT', 'F', 0, n - 1)] + tail.get((n, 1), []), -2: [('ctxT', 'F', 0, n - 1)] + tail.get((n, 2), []),
             -1: [('wo', NN - 1, CH - 1)] + tail.get((n, 3), []) + tail.get((n, 4), [])}
    for k in range(5, 16):
        early[k - 5] = tail.get((n + k // 8, k % 8), [])
    after += x_slots(1, early, m_rows) + [('moe',)]
    everything = before + sum(turns, []) + after

    MISC = ('xk', 'xv', 'xT', 'xq', 'mT', 'otT', 'ctxT', 'wox', 'wo', 'we', 'wq', 'va', 'vb', 'ka', 'kb', 'fin')

    def keys_sem(way, st):
        return f'k_{way}{st[-1]}' if st[1] == 'F' else f'kx_{way}{st[-2]}{st[-1]}'

    RING = 3
    bank_of, bank_before, held = {}, {}, {}
    for part in [before] + turns + [after]:
        for n, st in enumerate(st for st in part if st[0] == 's' or st[0] in MISC):
            bank_of[st] = n % RING
            bank_before[st] = held.get(n % RING)
            held[n % RING] = st

    def written(st):
        return f'bank_written{bank_of[st]}'

    def read(st):
        return f'bank_read{bank_of[st]}'

    group_at = {st[1:]: n for n, st in enumerate(st for st in everything if st[0] == 'mp')}

    def rows_sem(st):
        return f'm_in{group_at[st[1:5]] % 8}' if st[0] in ('md', 'st') else None

    def signals(st):
        k = st[0]
        if k == 's' or k in MISC:
            return ((written(st), 1), (read(st), 1)) + ((('var_ready', 1), ('rstd_ready', 1)) if k == 'fin' else ())
        if k in ('load_part', 'load_rest'):
            return ((f'stage_in{st[-1] % 2}', 16),)
        if k in ('kw', 'kr'):
            return ((keys_sem('out', st), 16),) if k == 'kw' else ((keys_sem('in', st), 96),)
        return {
            'st': (('st_done', 1), ('exp_done', 1)), 'pv': (('pv_done', 1),),
            'mp': (('mparts', 1),), 'otc': (('ot_copied', 1),), 'qs': (('q_split', 1),), 'ks': (('k_split', 1),),
            'ls': (('var_ready', 1), ('rstd_ready', 1)), 'ln': (('xn_ready', 1),),
            'qw': ((f'q_out{st[-1]}', 16),), 'qr': ((f'q_in{st[-1]}', 96),),
            'md': ((rows_sem(st), 16),),
            'part_split': (('w_split', 1),), 'rest_split': (('w_split', 1),), 'xs': (('x_split', 1),),
            'wl_post': (('wpost_in', 16),), 'wl_v': (('wv_in', 16),), 'wl_k': (('wk_in', 16),),
        }.get(k, ())

    level, total, ordinal = {}, {}, {}
    for st in everything:
        ordinal[st] = total.setdefault(st[0], 0)
        total[st[0]] += 1
        for name, by in signals(st):
            total[name] = total.get(name, 0) + by
            level[name, st] = total[name]
    per_turn = {}
    for st in turns[0]:
        for name, by in signals(st):
            per_turn[name] = per_turn.get(name, 0) + by

    def count(name, st, turn):
        if turn is None:
            return level[name, st]
        assert level[name, st] > per_turn[name], 'a wait of the first turn is against zero'
        return turn * per_turn[name] + (level[name, st] - per_turn[name])

    def dyn(v, turn):
        return v if turn is None else turn + (v - 1)

    with ExitStack() as ctx:
        def sb(name, shape, dt=f32):
            return ctx.enter_context(nc.sbuf_tensor(name, shape, dt))

        def pb(name, shape):
            return ctx.enter_context(nc.psum_tensor(name, shape, f32))

        def sem(name):
            return ctx.enter_context(nc.semaphore(name))

        X = sb("x_tok", [128, NT, D])
        NODE = sb("node_t", [128, NN + 1, NT * 128])
        QA = [sb(f"qa{i}", [128, 16, QW], bf16) for i in range(CH)]
        KAF = [sb(f"kaf{b}", [128, 8, SQ], bf16) for b in (0, 1)]
        KAX = [[sb(f"kax{L}{b}", [128, 16, SK], bf16) for b in (0, 1)] for L in (0, 1)]
        VFB = sb("vf", [128, 2, 4, 8, 32])
        VF = [VFB[:, b, :, :, :] for b in (0, 1)]
        SELE = VFB[:, :, :, :, :].rearrange("p b k h d -> p (b k h d)").bitcast(f16).rearrange("p (e n) -> p e n", n=128)
        VX = [[sb(f"vx{L}{b}", [128, 16, 32]) for b in (0, 1)] for L in (0, 1)]
        PT = [sb(f"pt{n}", [128, G, QW]) for n in range(PR)]
        NM = [sb(f"nm{n}", [128, 2, G]) for n in range(4)]
        MR = [sb(f"mr{n}", [128, 2, G]) for n in range(4)]
        MP = [sb(f"mp{n}", [128, 2, 3, G], bf16) for n in range(4)]
        MT = [sb(f"mt{n}", [3 * G, QW], bf16) for n in range(4)]
        OTS = [sb(f"ots{n}", [128, 2, QW]) for n in range(2)]
        REC = [sb(f"rec{n}", [128, 2, 8]) for n in range(2)]
        CTX = [sb(f"ctx{n}", [128, 2, D]) for n in range(2)]
        CTXT = [sb(f"ctxt{n}", [128, QW]) for n in range(2)]
        QT = [sb(f"qt{i}", [128, QW]) for i in range(CH)]
        QX = [sb(f"qx{n}", [128, QW]) for n in range(2)]
        QP = [sb(f"qp{n}", [128, 3, QW], bf16) for n in range(2)]
        QR = sb("qr", [128, QW])
        KIN = sb("kin", [128, SQ])
        KX = sb("kx", [128, SQ])
        KP = sb("kp", [128, 3, SQ], bf16)
        ZERO = sb("zero", [128, 2], bf16)
        KRS = sb("krs", [128, SQ])
        BNS = [sb(f"bns{n}", [128, 2, 6]) for n in range(CH)]
        MV = [sb(f"mv{n}", [128, 2, 2]) for n in range(CH)]
        VE = [sb(f"ve{n}", [128, 2]) for n in range(CH)]
        RSTD = [sb(f"rstd{n}", [128, 2]) for n in range(CH)]
        FT = [sb(f"ft{n}", [128, 2, D]) for n in range(2)]
        XN = [sb(f"xn{n}", [128, 2, D]) for n in range(2)]
        NEGHALF = sb("neghalf", [128, 2])
        CT = sb("ctx_in", [DC, B, SK])
        XW = sb("xw", [128, 2, 4, D])
        XB = sb("xb", [128, 2, 2])
        XBV = sb("xbv", [128, 2, 2, D])
        WPOST = sb("wpost", [128, 3, D])
        WK = sb("wk", [128, 2, D])
        WV = sb("wv", [128, 2, D])
        EW = sb("ew", [128, 3 * NN])
        BE = sb("be", [128, 3 * NN])
        ACTW = sb("actw", [128, NN])
        GALL = sb("gall", [128, 4])
        TG = sb("tg", [128, 4])
        LNGB = sb("lngb", [128, 2, D])
        IDENT = sb("ident", [128, 128])
        IDB = sb("identb", [128, 128], bf16)
        IDH = sb("identh", [128, 128], f16)
        WR = sb("wr", [128, NE])
        BR = sb("br", [128, NE])
        WG = sb("wg", [128, 2, NE * FE], f16)
        WU = sb("wu", [128, 2, NE * FE], f16)
        STAGE = [sb(f"stage{n}", [128, PIECE]) for n in (0, 1)]
        WSC = sb("wsc", [128, 2])
        WS = sb("ws", [128, 2 * FE])

        WD = NODE[:, 1:5, :].rearrange("p a t -> p (a t)")
        WSD = NODE[0:FE, 5, 0:D]
        MSC = [NODE[:, 6, 0:512], NODE[:, 6, 512:1024]]
        def qa_f32(i, lo, n):
            return QA[i][:, :, :].rearrange("p h t -> p (h t)").bitcast(f32)[:, lo:lo + n]

        ST = [pb(f"st{n}", [128, G, QW]) for n in range(2)]
        OT = pb("ot", [128, 2, QW])
        BANK = [pb(f"bank{n}", [128, 512]) for n in range(RING)]

        names = ['load_x', 'load_c', 'load_sel', 'load_w', 'load_f', 'load_m', 'load_d', 'zeroed', 'ready', 'dve_step', 'pool_step',
                 'tg_ready', 'gate_done', 'up_done', 'ahead_done', 'silu_done', 'ht_done', 'wb_done', 'y_done', 'yt_copied', 'y_tok', 'y_added', 'out_done',
                 'log_done', 'sig_done', 'w_ready', 'wT_done', 'wT_copied'] + [n for n in total if n not in {s[0] for s in everything}]
        sems = {n: sem(n) for n in dict.fromkeys(names)}

        qd = [nc.dram_tensor(f"q_parts{i}", (3, 128, QW), bf16, kind="Internal").ap() for i in range(CH)]
        kd = [nc.dram_tensor(f"k_parts{b}", (3, 128, SQ), bf16, kind="Internal").ap() for b in (0, 1)]
        kdx = [[nc.dram_tensor(f"kx_parts{L}{b}", (3, 128, SK), bf16, kind="Internal").ap() for b in (0, 1)] for L in (0, 1)]

        block = ctx.enter_context(nc.Block())

        by_ordinal = {}
        for s_ in everything:
            by_ordinal.setdefault(s_[0], []).append(s_)
        tile_order = by_ordinal['st']
        group_order = by_ordinal['mp']

        def chain_of(kind, s):
            return s // 2 if kind == 'X' else s % CH

        def head0(kind, s, g):
            return (8 * (s % 2) if kind == 'X' else 0) + G * g

        def run(eng, emit, after_loop=lambda: None):
            for st in before:
                emit(st, None)
            with eng.Fori(0, NN - 1) as turn:
                for st in turns[1]:
                    emit(st, turn)
            after_loop()
            for st in after:
                emit(st, None)

        def node(idx, lo, n):
            if isinstance(idx, int):
                return NODE[:, idx, lo:lo + n]
            return NODE[:, :, :].rearrange("p a t -> p (a t)")[:, bass.ds(idx * (NT * 128) + lo, n)]

        def prior_otc(kind, L, s):
            n = ordinal['otc', kind, L, s]
            return by_ordinal['otc'][n - 1] if n else None

        WP = QA[3][:, 0:4, :].rearrange("p h t -> p (h t)").bitcast(f16).rearrange("p (t a e) -> p t a e", t=NT, a=2)
        WT = QA[3][:, 4:8, :].rearrange("p h t -> p (h t)").bitcast(f16)
        SG = [qa_f32(0, 0, 512), qa_f32(0, 512, 512)]
        T1 = [qa_f32(0, 1024, 512), qa_f32(0, 1536, 512)]
        HT = [qa_f32(1, 0, 512), qa_f32(1, 512, 512)]
        YT = qa_f32(1, 1024, 1024)
        SA = [KAF[b][:, :, :].rearrange("p h t -> p (h t)").bitcast(f32)[:, 512 * n:512 * n + 512] for b in (0, 1) for n in range(4)]
        SA += [PT[b][:, 2 * n:2 * n + 2, :].rearrange("p h t -> p (h t)") for b in (0, 1) for n in (0, 1)]
        SA += [YT[:, 0:512], YT[:, 512:1024], KX[:, :], KP[:, 0:2, :].rearrange("p a t -> p (a t)").bitcast(f32)]
        SA += [OTS[n][:, :, :].rearrange("p a t -> p (a t)") for n in (0, 1)]
        UA = [PT[b][:, 2 * n:2 * n + 2, :].rearrange("p h t -> p (h t)") for b in (2, 3) for n in (0, 1)]
        AHEAD = len(SA)
        XHI, XLO = (t[:, :].bitcast(f16) for t in (KIN, KRS))

        def r3(i, lo):
            return qa_f32(i, lo, 512).rearrange("p (t e) -> p t e", t=NT)
        SC, SWB, GT, EQ = (r3(2, 512 * n) for n in range(4))
        MSK, CUM = r3(3, 1024), r3(3, 1536)
        M8 = MSC[0].rearrange("p (t g k) -> p t g k", t=NT, g=8)
        SM = MSC[1]

        @block.tensor
        def _(pe):
            W = lambda name, st, turn: pe.wait_ge(sems[name], count(name, st, turn))

            def emit(st, turn):
                k = st[0]
                bank = BANK[bank_of.get(st, 0)]
                if (k == 's' or k in MISC) and bank_before[st]:
                    W(read(bank_before[st]), bank_before[st], turn)
                if k == 'init':
                    pe.wait_ge(sems['load_c'], 16 * 7)
                    pe.wait_ge(sems['load_w'], 16 * 3)
                    pe.wait_ge(sems['ready'], 1)
                elif k == 'xk':
                    _, L, b = st
                    nc.tensor.matmul(bank[:, 0:SK], XW[0:DC, L, 1, :], CT[:, b, :], start=True, stop=True).then_inc(sems[written(st)], 1)
                elif k == 'xv':
                    _, L, b = st
                    nc.tensor.matmul(bank[0:SK, 0:D], CT[:, b, :], XW[0:DC, L, 2, :], start=True, stop=True).then_inc(sems[written(st)], 1)
                elif k == 'xT':
                    i = st[3]
                    W('xn_ready', ('ln',) + st[1:], turn)
                    n = ordinal['ln', st[1], st[2], i] % 2
                    for t in (0, 1):
                        last = nc.tensor.transpose(bank[:, 128 * t:128 * t + 128], XN[n][:, t, :], IDENT[:])
                    last.then_inc(sems[written(st)], 1)
                elif k == 'xq':
                    _, L, i = st
                    W(read(('xT', 'X', L, i)), ('xT', 'X', L, i), turn)
                    nc.tensor.matmul(bank[:, 0:QW], XW[:, L, 0, :], node(0, QW * i, QW), start=True, stop=True).then_inc(sems[written(st)], 1)
                elif k == 's':
                    _, kind, L, s, g, j = st
                    i, b = chain_of(kind, s), chain_of(kind, s) // 2
                    n = ordinal[st]
                    if g == 0 and j == 0:
                        if kind == 'X':
                            W(f'q_in{i}', ('qr', 'X', L, i), turn)
                            W(f'kx_in{L}{b}', ('kr', 'X', L, b), turn)
                        else:
                            W(f'q_in{i}', ('qr', 'F', s // CH, i), turn)
                            W(f'k_in{b}', ('kr', 'F', s // CH, b), turn)
                    if kind == 'X':
                        for r in range(G):
                            h = head0(kind, s, g) + r
                            last = nc.tensor.matmul(bank[:, r * SK:(r + 1) * SK], QA[i][0:48, h, 128 * j:128 * j + 128],
                                                    KAX[L][b][0:48, h, :], start=True, stop=True)
                        last.then_inc(sems[written(st)], 1)
                    else:
                        t, r = divmod(j, 4)
                        h = G * g + r
                        nc.tensor.matmul(bank[:], QA[i][0:ROWS_M, h, 128 * t:128 * t + 128], KAF[b][0:ROWS_M, h, :],
                                         start=True, stop=True).then_inc(sems[written(st)], 1)
                elif k == 'mT':
                    n = group_at[st[1:]]
                    W('mparts', ('mp',) + st[1:], turn)
                    mb = bank[:, :].bitcast(bf16)
                    for t in (0, 1):
                        last = nc.tensor.transpose(mb[0:3 * G, 128 * t:128 * t + 128], MP[n % 4][:, t, :, :].rearrange("p a r -> p (a r)"), IDB[:])
                    last.then_inc(sems[written(st)], 1)
                elif k == 'st':
                    _, kind, L, s, g, kt = st
                    i = chain_of(kind, s)
                    b = i // 2
                    n = ordinal[st]
                    if n >= 2:
                        W('exp_done', tile_order[n - 2], turn)
                    if n == 0:
                        pe.wait_ge(sems['load_sel'], 16 * 4)
                    if kt == 0:
                        W(rows_sem(st), ('md', kind, L, s, g), turn)
                    for r in range(G):
                        h = head0(kind, s, g) + r
                        if kind == 'X':
                            last = nc.tensor.matmul(ST[n % 2][0:SK, r, :], KAX[L][b][0:KR, h, :], QA[i][0:KR, h, :], start=True, stop=True)
                        else:
                            last = nc.tensor.matmul(ST[n % 2][:, r, :], KAF[b][0:KR, h, 128 * kt:128 * kt + 128], QA[i][0:KR, h, :], start=True, stop=True)
                    last.then_inc(sems['st_done'], 1)
                elif k == 'pv':
                    _, kind, L, s, g, kt = st
                    i = chain_of(kind, s)
                    b = i // 2
                    tile = ('st',) + st[1:]
                    n = ordinal[tile]
                    W('exp_done', tile, turn)
                    if g == 0 and kt == 0:
                        before_it = prior_otc(kind, L, s)
                        if before_it:
                            W('ot_copied', before_it, turn)
                        if kind == 'F':
                            W(read(('vb', s // CH, b)), ('vb', s // CH, b), turn)
                        else:
                            W(read(('xv', L, b)), ('xv', L, b), turn)
                    for r in range(G):
                        h = head0(kind, s, g) + r
                        if kind == 'X':
                            v, p = VX[L][b][0:SK, h, :], PT[n % PR][0:SK, r, :]
                        else:
                            v, p = VF[b][:, kt, h, :], PT[n % PR][:, r, :]
                        last = nc.tensor.matmul(OT[32 * r:32 * r + 32, g, :], v, p, start=(kt == 0), stop=(kt == KT[kind] - 1))
                    last.then_inc(sems['pv_done'], 1)
                elif k == 'otT':
                    _, kind, L, s = st
                    otc = ('otc',) + st[1:]
                    W('ot_copied', otc, turn)
                    o = OTS[ordinal[otc] % 2]
                    for t in (0, 1):
                        for g in (0, 1):
                            last = nc.tensor.transpose(bank[:, (2 * t + g) * 128:(2 * t + g) * 128 + 128], o[:, g, 128 * t:128 * t + 128], IDENT[:])
                    last.then_inc(sems[written(st)], 1)
                elif k == 'ctxT':
                    _, kind, L, i = st
                    s = i if kind == 'F' else 2 * i + 1
                    i = chain_of(kind, s)
                    W(read(('otT', kind, L, s)), ('otT', kind, L, s), turn)
                    for t in (0, 1):
                        last = nc.tensor.transpose(bank[:, 128 * t:128 * t + 128], CTX[i % 2][:, t, :], IDENT[:])
                    last.then_inc(sems[written(st)], 1)
                elif k == 'wox':
                    _, L, i = st
                    W(read(('ctxT', 'X', L, i)), ('ctxT', 'X', L, i), turn)
                    for t in (0, 1):
                        last = nc.tensor.matmul(bank[:, 128 * t:128 * t + 128], CTXT[i % 2][:, 128 * t:128 * t + 128], XW[:, L, 3, :], start=(t == 0), stop=True, skip_group_check=True)
                    last.then_inc(sems[written(st)], 1)
                elif k == 'wo':
                    _, c, i = st
                    W(read(('ctxT', 'F', 0, CH * c + i)), ('ctxT', 'F', 0, CH * c + i), turn)
                    if i == 0:
                        W('wpost_in', ('wl_post', c), turn)
                    nc.tensor.matmul(bank[:, 0:QW], WPOST[:, 0, :], CTXT[i % 2][:, :], start=True, stop=True).then_inc(sems[written(st)], 1)
                elif k == 'load_small':
                    pe.wait_ge(sems['load_f'], 16 * 9)
                elif k == 'we':
                    _, c, i = st
                    made = ('wo', c - 1, i) if c else ('xT', 'F', 0, i)
                    W(read(made), made, turn)
                    src = node(dyn(c, turn), QW * i, QW)
                    nc.tensor.matmul(bank[:, 0:QW], WPOST[:, 1, :], src, start=True, stop=True).then_inc(sems[written(st)], 1)
                elif k == 'wq':
                    _, c, i = st
                    W(read(('we', c, i)), ('we', c, i), turn)
                    nc.tensor.matmul(bank[:, 0:QW], WPOST[:, 2, :], QT[i][:, :], start=True, stop=True).then_inc(sems[written(st)], 1)
                elif k == 'ka':
                    _, c, b = st
                    if c and b == 0:
                        W('wk_in', ('wl_k', c), turn)
                    nc.tensor.matmul(bank[:], WK[:, 0, :], node(dyn(c, turn) // (NN - 1), SQ * b, SQ), start=True, stop=True).then_inc(sems[written(st)], 1)
                elif k == 'kb':
                    W(read(('ka',) + st[1:]), ('ka',) + st[1:], turn)
                    nc.tensor.matmul(bank[:], WK[:, 1, :], KIN[:], start=True, stop=True).then_inc(sems[written(st)], 1)
                elif k == 'va':
                    _, c, b = st
                    if c and b == 0:
                        W('wv_in', ('wl_v', c), turn)
                    nc.tensor.matmul(bank[:], WV[:, 0, :], node((dyn(c, turn) + 1) // 2, SQ * b, SQ), start=True, stop=True).then_inc(sems[written(st)], 1)
                elif k == 'vb':
                    W(read(('va',) + st[1:]), ('va',) + st[1:], turn)
                    for kt in range(4):
                        last = nc.tensor.matmul(bank[:, 128 * kt:128 * kt + 128], KIN[:, 128 * kt:128 * kt + 128], WV[:, 1, :], start=(kt == 0), stop=True, skip_group_check=True)
                    last.then_inc(sems[written(st)], 1)
                elif k == 'fin':
                    i = st[1]
                    W(read(('wo', NN - 1, i)), ('wo', NN - 1, i), turn)
                    for t in (0, 1):
                        last = nc.tensor.transpose(bank[:, 128 * t:128 * t + 128], node(NN, QW * i + 128 * t, 128), IDENT[:])
                    last.then_inc(sems[written(st)], 1)
                elif k == 'moe':
                    pe_moe()

            def gate_up(n):
                p, h = divmod(n, 2)
                t = slice(512 * h, 512 * h + 512)
                for a, (w, signal) in enumerate(((WG, 'gate_done'), (WU, 'up_done'))):
                    rows = 128 if p < NP else FE
                    to = ST[n % 2][0:rows, 2 * a:2 * a + 2, :].rearrange("p a t -> p (a t)")
                    if p < NP:
                        c = slice(128 * p, 128 * p + 128)
                        nc.tensor.matmul(to, w[:, 0, c], XHI[:, t], start=True, stop=False)
                        nc.tensor.matmul(to, w[:, 0, c], XLO[:, t], start=False, stop=False)
                        nc.tensor.matmul(to, w[:, 1, c], XHI[:, t], start=False, stop=True).then_inc(sems[signal], 1)
                    else:
                        nc.tensor.matmul(to, WS[:, FE * a:FE * a + FE], node(0, 512 * h, 512), start=True, stop=True).then_inc(sems[signal], 1)

            def pe_moe():
                for use in held.values():
                    W(read(use), use, None)
                for i in range(CH):
                    W(read(('xT', 'M', 0, i)), ('xT', 'M', 0, i), None)
                pe.wait_ge(sems['load_m'], 16 * 3)
                pe.wait_ge(sems['w_split'], total['w_split'])
                pe.wait_ge(sems['x_split'], CH)
                for t in range(NT):
                    last = nc.tensor.matmul(BANK[2][:, NE * t:NE * t + NE], node(0, 128 * t, 128), WR[:, :], start=(t == 0), stop=True, skip_group_check=True)
                last.then_inc(sems['log_done'], 1)
                for n in range(AHEAD):
                    if n >= 2:
                        pe.wait_ge(sems['silu_done'], n - 1)
                    gate_up(n)
                pe.wait_ge(sems['w_ready'], 1)
                mh = BANK[2][:, :].bitcast(f16)
                for t in range(NT):
                    last = nc.tensor.transpose(mh[:, 128 * t:128 * t + 128], WP[:, t, :, :].rearrange("p a e -> p (a e)"), IDH[:])
                last.then_inc(sems['wT_done'], 1)
                pe.wait_ge(sems['wT_copied'], 1)
                pe.wait_ge(sems['load_d'], 16 * 6)

                def down(n):
                    p, h = divmod(n, 2)
                    rows = 128 if p < NP else FE
                    pe.wait_ge(sems['ht_done'], n + 1)
                    y = OT[:, :, :].rearrange("p a t -> p (a t)") if h == 0 else BANK[2][:, :]
                    w = WD[:, 128 * p:128 * p + 128] if p < NP else WSD
                    last = nc.tensor.matmul(y, w, HT[n % 2][0:rows, :], start=(p == 0), stop=(p == NP))
                    if p == NP:
                        last.then_inc(sems['y_done'], 1)

                for n in range(2 * NP + 2):
                    p, h = divmod(n, 2)
                    if n >= 2:
                        pe.wait_ge(sems['ht_done'], n - 1)
                    if n >= AHEAD:
                        gate_up(n)
                    if p < NP:
                        nc.tensor.matmul(BANK[n % 2][:], SELE[:, p, :], WT[:, 512 * h:512 * h + 512], start=True, stop=True).then_inc(sems['wb_done'], 1)
                    if n >= 1:
                        down(n - 1)
                down(2 * NP + 1)
                pe.wait_ge(sems['yt_copied'], 2)
                for t in range(NT):
                    y = (ST[0] if t < 4 else ST[1])[:, 0:2, :].rearrange("p a t -> p (a t)")
                    last = nc.tensor.transpose(y[:, 128 * (t % 4):128 * (t % 4) + 128], YT[:, 128 * t:128 * t + 128], IDENT[:])
                    if t % 4 == 3:
                        last.then_inc(sems['y_tok'], 1)

            run(pe, emit)

        @block.scalar
        def _(act):
            W = lambda name, st, turn: act.wait_ge(sems[name], count(name, st, turn))

            def emit(st, turn):
                k = st[0]
                bank = BANK[bank_of.get(st, 0)]
                if k == 'init':
                    act.wait_ge(sems['load_c'], 16 * 7)
                    act.wait_ge(sems['load_w'], 16 * 3)
                    nc.scalar.activation(TG[:], GALL[:], ACT.Tanh).then_inc(sems['tg_ready'], 1)
                elif k == 'xk':
                    _, L, b = st
                    W(written(st), st, turn)
                    ks = ('ks', 'X', L, b)
                    if ordinal[ks]:
                        o = by_ordinal['ks'][ordinal[ks] - 1]
                        W(keys_sem('out', o), ('kw',) + o[1:], turn)
                    nc.scalar.activation(KP[:, 0, 0:SK], bank[:, 0:SK], ACT.Identity, bias=XB[:, L, 1:2])
                    nc.scalar.activation(KX[:, 0:SK], bank[:, 0:SK], ACT.Identity, bias=XB[:, L, 1:2]).then_inc(sems[read(st)], 1)
                elif k == 'xT':
                    i = st[3]
                    W(written(st), st, turn)
                    if st[1] == 'M':
                        nc.scalar.activation(XHI[:, QW * i:QW * i + QW], bank[:, 0:QW], ACT.Copy, scale=XSCALE)
                    nc.scalar.activation(node(0, QW * i, QW), bank[:, 0:QW], ACT.Copy).then_inc(sems[read(st)], 1)
                elif k in ('xq', 'wq'):
                    W(written(st), st, turn)
                    q = ('qs', 'X' if k == 'xq' else 'F') + st[1:]
                    n = ordinal[q]
                    if n >= 2:
                        W('q_split', by_ordinal['qs'][n - 2], turn)
                        o = by_ordinal['qs'][n - 2]
                        W(f'q_out{o[-1]}', ('qw',) + o[1:], turn)
                    if k == 'xq':
                        nc.scalar.activation(QP[n % 2][:, 0, :], bank[:, 0:QW], ACT.Identity, bias=XB[:, st[1], 0:1])
                        nc.scalar.activation(QX[n % 2][:], bank[:, 0:QW], ACT.Identity, bias=XB[:, st[1], 0:1]).then_inc(sems[read(st)], 1)
                    else:
                        nc.scalar.activation(QP[n % 2][:, 0, :], bank[:, 0:QW], ACT.Copy)
                        nc.scalar.activation(QX[n % 2][:], bank[:, 0:QW], ACT.Copy).then_inc(sems[read(st)], 1)
                elif k == 'mT':
                    n = group_at[st[1:]]
                    W(written(st), st, turn)
                    if n >= 4:
                        W(rows_sem(('md',) + group_order[n - 4][1:]), ('md',) + group_order[n - 4][1:], turn)
                    nc.scalar.activation(MT[n % 4][:], bank[:, :].bitcast(bf16)[0:3 * G, 0:QW], ACT.Copy).then_inc(sems[read(st)], 1)
                elif k == 'st':
                    _, kind, L, s, g, kt = st
                    n = ordinal[st]
                    W('st_done', st, turn)
                    if n >= PR:
                        W('pv_done', ('pv',) + tile_order[n - PR][1:], turn)
                    rows = SK if kind == 'X' else 128
                    nc.scalar.activation(PT[n % PR][0:rows, :, :], ST[n % 2][0:rows, :, :], ACT.Exp, scale=float(DH[kind]) ** -0.5).then_inc(sems['exp_done'], 1)
                elif k == 'otc':
                    _, kind, L, s = st
                    W('pv_done', ('pv', kind, L, s, 1, KT[kind] - 1), turn)
                    n = ordinal[st]
                    if n >= 2:
                        W(written(('otT',) + by_ordinal['otc'][n - 2][1:]), ('otT',) + by_ordinal['otc'][n - 2][1:], turn)
                    nc.scalar.activation(OTS[n % 2][:, :, :], OT[:, :, :], ACT.Copy).then_inc(sems['ot_copied'], 1)
                elif k == 'ctxT':
                    W(written(st), st, turn)
                    nc.scalar.activation(CTXT[st[3] % 2][:], bank[:, 0:QW], ACT.Copy).then_inc(sems[read(st)], 1)
                elif k == 'kb':
                    _, c, b = st
                    W(written(st), st, turn)
                    ks = ('ks', 'F', c, b)
                    o = by_ordinal['ks'][ordinal[ks] - 1]
                    W(keys_sem('out', o), ('kw',) + o[1:], turn)
                    nc.scalar.activation(KP[:, 0, :], bank[:], ACT.Copy)
                    nc.scalar.activation(KX[:], bank[:], ACT.Copy).then_inc(sems[read(st)], 1)
                elif k == 'vb':
                    _, c, b = st
                    W(written(st), st, turn)
                    if c:
                        W('pv_done', ('pv', 'F', 0, CH * (c - 1) + 2 * b + 1, 1, 3), turn)
                    nc.scalar.activation(VF[b][:, :, :, 0:16], bank[:, :].rearrange("p (k h d) -> p k h d", k=4, h=8), ACT.Copy).then_inc(sems[read(st)], 1)
                elif k == 'moe':
                    act_moe()

            def act_moe():
                act.wait_ge(sems['log_done'], 1)
                nc.scalar.activation(SC, BANK[2][:, :].rearrange("p (t e) -> p t e", t=NT), ACT.Tanh, scale=0.5).then_inc(sems['sig_done'], 1)
                for n in range(AHEAD):
                    act.wait_ge(sems['gate_done'], n + 1)
                    nc.scalar.activation(SA[n], ST[n % 2][:, 0:2, :].rearrange("p a t -> p (a t)"), ACT.Silu, scale=1 / (WSCALE * XSCALE))
                    act.wait_ge(sems['up_done'], n + 1)
                    if n >= 4:
                        act.wait_ge(sems['ahead_done'], n - 3)
                    nc.scalar.activation(UA[n % 4], ST[n % 2][:, 2:4, :].rearrange("p a t -> p (a t)"), ACT.Copy, scale=1 / (WSCALE * XSCALE)).then_inc(sems['silu_done'], 1)
                act.wait_ge(sems['wT_done'], 1)
                nc.scalar.activation(WT, BANK[2][:, :].bitcast(f16), ACT.Copy).then_inc(sems['wT_copied'], 1)
                for n in range(AHEAD, 2 * NP + 2):
                    rows = 128 if n // 2 < NP else FE
                    act.wait_ge(sems['gate_done'], n + 1)
                    nc.scalar.activation(SG[n % 2][0:rows, :], ST[n % 2][0:rows, 0:2, :].rearrange("p a t -> p (a t)"), ACT.Silu,
                                         scale=1 / (WSCALE * XSCALE) if n // 2 < NP else 1.0).then_inc(sems['silu_done'], 1)
                act.wait_ge(sems['y_done'], 2)
                nc.scalar.activation(YT[:, 0:512], OT[:, :, :].rearrange("p a t -> p (a t)"), ACT.Copy).then_inc(sems['yt_copied'], 1)

            run(act, emit)

        @block.vector
        def _(dve):
            W = lambda name, st, turn: dve.wait_ge(sems[name], count(name, st, turn))
            done = [0, 0]

            def link(ins, turn):
                ins.then_inc(sems['dve_step'], 1)
                done[0] += 1
                v = done[0]
                if turn is not None:
                    v = v + turn * dve_per_turn
                dve.wait_ge(sems['dve_step'], v)

            dve_per_turn = sum({'mp': 3, 'otT': 1}.get(s_[0], 0) for s_ in turns[0])

            def emit(st, turn):
                k = st[0]
                bank = BANK[bank_of.get(st, 0)]
                if k == 'init':
                    for b in (0, 1):
                        nc.vector.memset(VF[b][:, :, :, 16:32], 1.0)
                    nc.vector.memset(NEGHALF[:], -0.5)
                    for L in (0, 1):
                        for b in (0, 1):
                            link(nc.vector.memset(VX[L][b][:, :, :], 1.0), turn)
                    dve.wait_ge(sems['load_c'], 16 * 7)
                    nc.vector.memset(REC[0][:, :, :], 0.0).then_inc(sems['ready'], 1)
                    dve.wait_ge(sems['load_x'], 16)
                    dve.wait_ge(sems['tg_ready'], 1)
                elif k == 'xv':
                    _, L, b = st
                    W(written(st), st, turn)
                    nc.vector.tensor_tensor(VX[L][b][0:SK, :, 0:8], bank[0:SK, 0:D].rearrange("p (h d) -> p h d", h=16),
                                            XBV[0:SK, L, 0, :].rearrange("p (h d) -> p h d", h=16), ALU.add).then_inc(sems[read(st)], 1)
                elif k == 'ls':
                    _, kind, L, i = st
                    stats([X[:, 2 * i + t, :] for t in (0, 1)], 1e-5, i, turn)
                elif k == 'ln':
                    _, kind, L, i = st
                    n = ordinal[st] % 2
                    if ordinal[st] >= 2:
                        W(written(('xT',) + by_ordinal['ln'][ordinal[st] - 2][1:]), ('xT',) + by_ordinal['ln'][ordinal[st] - 2][1:], turn)
                    W('rstd_ready', ('ls',) + st[1:], turn)
                    for t in (0, 1):
                        last = nc.vector.tensor_scalar(XN[n][:, t, :], X[:, 2 * i + t, :], MV[i][:, t, 0:1], RSTD[i][:, t:t + 1], ALU.subtract, ALU.mult)
                    last.then_inc(sems['xn_ready'], 1)
                elif k == 's':
                    _, kind, L, s, g, j = st
                    n = ordinal[st]
                    m = NM[group_at[kind, L, s, g] % 4]
                    W(written(st), st, turn)
                    if kind == 'X':
                        nc.vector.tensor_reduce(m[:, j, :], bank[:, 0:G * SK].rearrange("p (r t) -> p r t", r=G), AX.X, ALU.max, negate=True).then_inc(sems[read(st)], 1)
                    else:
                        t, r = divmod(j, 4)
                        nc.vector.tensor_reduce(m[:, t, r:r + 1], bank[:], AX.X, ALU.max, negate=True).then_inc(sems[read(st)], 1)
                elif k == 'mp':
                    _, kind, L, s, g = st
                    n = group_at[st[1:]] % 4
                    W(read(('s', kind, L, s, g, 1 if kind == 'X' else 7)), ('s', kind, L, s, g, 1 if kind == 'X' else 7), turn)
                    link(nc.vector.tensor_copy(MP[n][:, :, 0, :], NM[n][:, :, :]), turn)
                    link(nc.vector.tensor_tensor(MR[n][:, :, :], NM[n][:, :, :], MP[n][:, :, 0, :], ALU.subtract), turn)
                    link(nc.vector.tensor_copy(MP[n][:, :, 1, :], MR[n][:, :, :]), turn)
                    nc.vector.tensor_tensor(MP[n][:, :, 2, :], MR[n][:, :, :], MP[n][:, :, 1, :], ALU.subtract).then_inc(sems['mparts'], 1)
                elif k == 'otT':
                    _, kind, L, s = st
                    n = ordinal[st]
                    i = chain_of(kind, s)
                    d = DH[kind]
                    W(written(st), st, turn)
                    o = bank[:, :].rearrange("p (t h e) -> p t h e", t=2, h=8)
                    link(nc.vector.reciprocal(REC[n % 2][:, :, :], o[:, :, :, d]), turn)
                    lo = 64 * (s % 2) if kind == 'X' else 0
                    c = CTX[i % 2][:, :, lo:lo + 8 * d].rearrange("p t (h e) -> p t h e", h=8)
                    nc.vector.tensor_tensor(c, o[:, :, :, 0:d], REC[n % 2][:, :, :].unsqueeze(3).broadcast_to([128, 2, 8, d]), ALU.mult).then_inc(sems[read(st)], 1)
                elif k == 'wox':
                    _, L, i = st
                    W(written(st), st, turn)
                    n = i % 2
                    link(nc.vector.tensor_tensor(XN[n][:, :, :], bank[:, 0:QW].rearrange("p (t d) -> p t d", t=2),
                                                 XBV[:, L, 1, :].unsqueeze(1).broadcast_to([128, 2, D]), ALU.add), turn)
                    link(nc.vector.scalar_tensor_tensor(X[:, 2 * i:2 * i + 2, :], XN[n][:, :, :], TG[:, L:L + 1], X[:, 2 * i:2 * i + 2, :], ALU.mult, ALU.add), turn)
                    nc.vector.memset(REC[0][:, :, 0:1], 1.0).then_inc(sems[read(st)], 1)
                elif k == 'wo':
                    _, c, i = st
                    W(written(st), st, turn)
                    nc.vector.scalar_tensor_tensor(node(dyn(c, turn) + 1, QW * i, QW), bank[:, 0:QW], ACTW[:, bass.ds(dyn(c, turn), 1)], QT[i][:, :], ALU.mult, ALU.add).then_inc(sems[read(st)], 1)
                elif k == 'we':
                    _, c, i = st
                    W(written(st), st, turn)
                    col = dyn(c, turn) * 3
                    nc.vector.tensor_scalar(QT[i][:, :], bank[:, 0:QW], BE[:, bass.ds(col, 1)], EW[:, bass.ds(col, 1)], ALU.add, ALU.mult).then_inc(sems[read(st)], 1)
                elif k in ('ka', 'va'):
                    _, c, b = st
                    W(written(st), st, turn)
                    col = dyn(c, turn) * 3 + (1 if k == 'ka' else 2)
                    nc.vector.tensor_scalar(KIN[:], bank[:], BE[:, bass.ds(col, 1)], EW[:, bass.ds(col, 1)], ALU.add, ALU.mult).then_inc(sems[read(st)], 1)
                elif k == 'fin':
                    i = st[1]
                    W(written(st), st, turn)
                    ins = nc.vector.tensor_copy(FT[i % 2][:, :, :], bank[:, 0:QW].rearrange("p (t d) -> p t d", t=2))
                    ins.then_inc(sems[read(st)], 1)
                    W(read(st), st, turn)
                    stats([FT[i % 2][:, t, :] for t in (0, 1)], 1e-6, i, turn)
                elif k == 'fl':
                    i = st[1]
                    W('rstd_ready', ('fin', i), turn)
                    last_norm(i, turn)
                elif k == 'xs':
                    i = st[1]
                    W(read(('xT', 'M', 0, i)), ('xT', 'M', 0, i), turn)
                    nc.vector.scalar_tensor_tensor(XLO[:, QW * i:QW * i + QW], node(0, QW * i, QW), XSCALE, XHI[:, QW * i:QW * i + QW], ALU.mult, ALU.subtract).then_inc(sems['x_split'], 1)
                elif k == 'moe':
                    dve_moe()

            def stats(src, eps, i, turn):
                for t in (0, 1):
                    last = nc.vector.bn_stats(BNS[i][:, t, :], src[t])
                link(last, turn)
                for t in (0, 1):
                    last = nc.vector.bn_aggr(MV[i][:, t, :], BNS[i][:, t, :])
                link(last, turn)
                nc.vector.tensor_scalar(VE[i][:], MV[i][:, :, 1], eps, None, ALU.add).then_inc(sems['var_ready'], 1)

            def last_norm(i, turn):
                n = i % 2
                y, xx = FT[n][:, :, :], X[:, 2 * i:2 * i + 2, :]
                for t in (0, 1):
                    last = nc.vector.tensor_scalar(FT[n][:, t, :], FT[n][:, t, :], MV[i][:, t, 0:1], RSTD[i][:, t:t + 1], ALU.subtract, ALU.mult)
                link(last, turn)
                link(nc.vector.tensor_tensor(y, y, LNGB[:, 0, :].unsqueeze(1).broadcast_to([128, 2, D]), ALU.mult), turn)
                link(nc.vector.tensor_tensor(y, y, LNGB[:, 1, :].unsqueeze(1).broadcast_to([128, 2, D]), ALU.add), turn)
                link(nc.vector.scalar_tensor_tensor(xx, y, TG[:, 2:3], xx, ALU.mult, ALU.add), turn)

            def first_of(sel, gt, eq, cum, src, thr, k, width):
                n = NT
                b = thr.unsqueeze(2).broadcast_to([128, n, width])
                link(nc.vector.tensor_tensor(gt, src, b, ALU.is_gt), None)
                link(nc.vector.tensor_tensor(eq, src, b, ALU.is_equal), None)
                link(nc.vector.tensor_reduce(NEED[:, :], gt, AX.X, ALU.add), None)
                link(nc.vector.tensor_scalar(NEED[:, :], NEED[:, :], -1.0, float(k), ALU.mult, ALU.add), None)
                for t in range(n):
                    last = nc.vector.tensor_tensor_scan(cum[:, t, :], ONES64[:, 0:width], eq[:, t, :], 0.0, ALU.mult, ALU.add)
                link(last, None)
                link(nc.vector.tensor_tensor(cum, cum, NEED[:, :].unsqueeze(2).broadcast_to([128, n, width]), ALU.is_le), None)
                link(nc.vector.tensor_tensor(eq, eq, cum, ALU.mult), None)
                link(nc.vector.tensor_tensor(sel, gt, eq, ALU.add), None)

            NEED = SM[:, 0:8]
            ONES64 = SM[:, 8:72]
            GS = SM[:, 72:136].rearrange("p (t g) -> p t g", t=NT)
            GG = [SM[:, 136 + 64 * a:200 + 64 * a].rearrange("p (t g) -> p t g", t=NT) for a in range(4)]
            M8G = SM[:, 392:456].rearrange("p (t g) -> p t g", t=NT)
            SUM = SM[:, 456:464]

            def dve_moe():
                dve.wait_ge(sems['sig_done'], 1)
                link(nc.vector.memset(ONES64, 1.0), None)
                link(nc.vector.tensor_scalar(SC, SC, 0.5, 0.5, ALU.mult, ALU.add), None)
                link(nc.vector.tensor_tensor(SWB, SC, BR[:, :].unsqueeze(1).broadcast_to([128, NT, NE]), ALU.add), None)
                for t in range(NT):
                    for g in range(8):
                        last = nc.vector.max(M8[:, t, g, :], SWB[:, t, 8 * g:8 * g + 8])
                link(last, None)
                link(nc.vector.tensor_tensor(GS, M8[:, :, :, 0], M8[:, :, :, 1], ALU.add), None)
                for t in range(NT):
                    last = nc.vector.max(M8G[:, t, :], GS[:, t, :])
                link(last, None)
                first_of(GG[3], GG[0], GG[1], GG[2], GS, M8G[:, :, 3], 4, 8)
                link(nc.vector.tensor_tensor(SWB.rearrange("p t (g e) -> p t g e", g=8), SWB.rearrange("p t (g e) -> p t g e", g=8),
                                             GG[3].unsqueeze(3).broadcast_to([128, NT, 8, 8]), ALU.mult), None)
                for t in range(NT):
                    last = nc.vector.max(M8G[:, t, :], SWB[:, t, :])
                link(last, None)
                first_of(MSK, GT, EQ, CUM, SWB, M8G[:, :, 7], 8, NE)
                link(nc.vector.tensor_tensor(SC, SC, MSK, ALU.mult), None)
                link(nc.vector.tensor_reduce(SUM, SC, AX.X, ALU.add), None)
                link(nc.vector.tensor_scalar(SUM, SUM, 1e-20, None, ALU.add), None)
                link(nc.vector.reciprocal(SUM, SUM), None)
                link(nc.vector.tensor_scalar(SC, SC, 2.5, None, ALU.mult), None)
                link(nc.vector.tensor_tensor(SC, SC, SUM.unsqueeze(2).broadcast_to([128, NT, NE]), ALU.mult), None)
                link(nc.vector.tensor_copy(WP[:, :, 0, :], SC), None)
                link(nc.vector.tensor_tensor(SC, SC, WP[:, :, 0, :], ALU.subtract), None)
                nc.vector.tensor_scalar(WP[:, :, 1, :], SC, SHIFT, None, ALU.mult).then_inc(sems['w_ready'], 1)
                for n in range(2 * NP + 2):
                    shared = n // 2 == NP
                    rows = FE if shared else 128
                    if not shared:
                        dve.wait_ge(sems['wb_done'], n + 1)
                    if n < AHEAD:
                        dve.wait_ge(sems['ahead_done'], n + 1)
                        nc.vector.tensor_tensor(HT[n % 2], SA[n], BANK[n % 2][:], ALU.mult).then_inc(sems['ht_done'], 1)
                        continue
                    dve.wait_ge(sems['up_done'], n + 1)
                    dve.wait_ge(sems['silu_done'], n + 1)
                    u = ST[n % 2][0:rows, 2:4, :].rearrange("p a t -> p (a t)")
                    if shared:
                        nc.vector.tensor_tensor(HT[n % 2][0:rows, :], SG[n % 2][0:rows, :], u, ALU.mult).then_inc(sems['ht_done'], 1)
                    else:
                        link(nc.vector.scalar_tensor_tensor(T1[n % 2], u, 1 / (WSCALE * XSCALE), SG[n % 2], ALU.mult, ALU.mult), None)
                        nc.vector.tensor_tensor(HT[n % 2], T1[n % 2], BANK[n % 2][:], ALU.mult).then_inc(sems['ht_done'], 1)
                dve.wait_ge(sems['y_done'], 2)
                nc.vector.tensor_copy(YT[:, 512:1024], BANK[2][:]).then_inc(sems['yt_copied'], 1)
                for h in (0, 1):
                    dve.wait_ge(sems['y_tok'], h + 1)
                    y = ST[h][:, 0:2, :].rearrange("p a t -> p (a t)")
                    xx = X[:, 4 * h:4 * h + 4, :].rearrange("p t d -> p (t d)")
                    nc.vector.scalar_tensor_tensor(xx, y, TG[:, 3:4], xx, ALU.mult, ALU.add).then_inc(sems['y_added'], 1)

            def after_loop():
                done[0] += (NN - 2) * dve_per_turn

            run(dve, emit, after_loop)

        @block.gpsimd
        def _(pool):
            W = lambda name, st, turn: pool.wait_ge(sems[name], count(name, st, turn))
            done = [0]
            pool_per_turn = sum({'qs': 2, 'ks': 2, 'part_split': 2}.get(s_[0], 0) for s_ in turns[0])

            def link(ins, turn):
                ins.then_inc(sems['pool_step'], 1)
                done[0] += 1
                pool.wait_ge(sems['pool_step'], done[0] if turn is None else done[0] + turn * pool_per_turn)

            def parts(src, p, r, signal, turn):
                link(nc.gpsimd.tensor_tensor(r, src, p[0], ALU.subtract), turn)
                link(nc.gpsimd.tensor_tensor(p[1], r, ZERO[:, 0:1].broadcast_to([128, r.shape[1]]), ALU.add), turn)
                nc.gpsimd.tensor_tensor(p[2], r, p[1], ALU.subtract).then_inc(signal, 1)

            def emit(st, turn):
                k = st[0]
                if k == 'init':
                    for L in (0, 1):
                        for b in (0, 1):
                            nc.gpsimd.memset(KAX[L][b][:, :, :], 0.0).then_inc(sems['zeroed'], 1)
                    for i in range(CH):
                        nc.gpsimd.memset(QA[i][:, :, :].rearrange("p h t -> p (h t)").bitcast(u32), 0).then_inc(sems['zeroed'], 1)
                    nc.gpsimd.memset(WSC[:, :], WSCALE)
                    link(nc.gpsimd.memset(ZERO[:, :], 0.0), turn)
                elif k in ('ls', 'fin'):
                    i = st[-1]
                    W('var_ready', st, turn)
                    nc.gpsimd.tensor_tensor(RSTD[i][:], VE[i][:], NEGHALF[:], ALU.pow).then_inc(sems['rstd_ready'], 1)
                elif k == 'qs':
                    _, kind, c, i = st
                    n = ordinal[st]
                    W(read(('xq', c, i) if kind == 'X' else ('wq', c, i)), ('xq', c, i) if kind == 'X' else ('wq', c, i), turn)
                    if n:
                        W('q_split', by_ordinal['qs'][n - 1], turn)
                    parts(QX[n % 2][:], [QP[n % 2][:, a, :] for a in range(3)], QR[:], sems['q_split'], turn)
                elif k == 'ks':
                    _, kind, c, b = st
                    n = ordinal[st]
                    W(read(('xk', c, b) if kind == 'X' else ('kb', c, b)), ('xk', c, b) if kind == 'X' else ('kb', c, b), turn)
                    w = SK if kind == 'X' else SQ
                    if n:
                        W('k_split', by_ordinal['ks'][n - 1], turn)
                    parts(KX[:, 0:w], [KP[:, a, 0:w] for a in range(3)], KRS[:, 0:w], sems['k_split'], turn)

                elif k in ('part_split', 'rest_split'):
                    i = st[-1]
                    if k == 'part_split':
                        w, n = (WG, WU)[i // 2], PIECE
                        lo = dyn(st[1], turn) * (2 * PIECE) + (i % 2) * PIECE
                    else:
                        w, n, lo = (WG, WU)[i], REST, NE * FE - REST
                    if turn is not None:
                        lo = pool.snap(lo)
                    W(f'stage_in{i % 2}', ('load_part' if k == 'part_split' else 'load_rest',) + st[1:], turn)
                    b = STAGE[i % 2][:, 0:n]
                    link(nc.gpsimd.tensor_tensor(b, b, WSC[:, 0:1].broadcast_to([128, n]), ALU.mult), turn)
                    link(nc.gpsimd.tensor_tensor(w[:, 0, bass.ds(lo, n)], b, ZERO[:, 0:1].broadcast_to([128, n]), ALU.add), turn)
                    nc.gpsimd.tensor_tensor(w[:, 1, bass.ds(lo, n)], b, w[:, 0, bass.ds(lo, n)], ALU.subtract).then_inc(sems['w_split'], 1)
                elif k == 'moe':
                    for n in range(AHEAD):
                        pool.wait_ge(sems['silu_done'], n + 1)
                        nc.gpsimd.tensor_tensor(SA[n], SA[n], UA[n % 4], ALU.mult).then_inc(sems['ahead_done'], 1)

            def after_loop():
                done[0] += (NN - 2) * pool_per_turn

            run(pool, emit, after_loop)

        @block.sync
        def _(sp):
            W = lambda name, st, turn: sp.wait_ge(sems[name], count(name, st, turn))

            def blocks(dst, dram, order, d, heads, sem_, w):
                for j in range(6):
                    sp.dma_start(dst[d * j:d * j + d, 0:heads, 0:w], dram[order[j]].rearrange("(h d) t -> d h t", d=d)).then_inc(sem_, 16)

            def emit(st, turn):
                k = st[0]
                if k == 'init':
                    sp.dma_start(X[:, :, :], x).then_inc(sems['load_x'], 16)
                    for dst, src in ((CT[:, :, :], ctx_t.rearrange("b d s -> d b s")), (XB[:, :, :], x_bqk), (XBV[:, :, :, :], x_bvo), (GALL[:], g_all),
                                     (IDENT[:], c_ident), (IDB[:], c_ident_bf), (IDH[:], c_ident_h)):
                        sp.dma_start(dst, src).then_inc(sems['load_c'], 16)
                    sp.dma_start(XW[:, :, 0, :], x_wq).then_inc(sems['load_w'], 16)
                    sp.dma_start(XW[:, :, 3, :], x_wo).then_inc(sems['load_w'], 16)
                    sp.dma_start(XW[0:DC, :, 1:3, :], x_wkv).then_inc(sems['load_w'], 16)
                    sp.wait_ge(sems['zeroed'], 4)
                    for L in (0, 1):
                        for b in (0, 1):
                            sp.dma_start(KAX[L][b][ROWS_M:KR, :, :], c_sel_x).then_inc(sems['load_sel'], 16)
                    for dst, src in ((EW[:], f_ew), (BE[:], f_be), (ACTW[:], f_actw), (WPOST[:, :, :], f_wpost[0]), (WK[:, :, :], f_wk[0]), (WV[:, :, :], f_wv[0]),
                                     (LNGB[:, :, :], ln_gb), (KAF[0][ROWS_M:KR, :, :], c_sel_f), (KAF[1][ROWS_M:KR, :, :], c_sel_f)):
                        sp.dma_start(dst, src).then_inc(sems['load_f'], 16)
                elif k == 'load_small':
                    for dst, src in ((WR[:], w_router), (BR[:], b_router), (WS[:], sh_gate_up)):
                        sp.dma_start(dst, src).then_inc(sems['load_m'], 16)
                elif k == 'load_part':
                    _, c, i = st
                    lo = dyn(c, turn) * (2 * PIECE) + (i % 2) * PIECE
                    if turn is not None:
                        lo = sp.snap(lo)
                    W('w_split', ('part_split', c, i - 2) if i >= 2 else ('part_split', c - 1, i + 2), turn)
                    sp.dma_start(STAGE[i % 2][:], (moe_gate if i < 2 else moe_up)[:, bass.ds(lo, PIECE)]).then_inc(sems[f'stage_in{i % 2}'], 16)
                elif k == 'load_rest':
                    i = st[1]
                    sp.dma_start(STAGE[i][:, 0:REST], (moe_gate, moe_up)[i][:, NE * FE - REST:]).then_inc(sems[f'stage_in{i}'], 16)
                elif k == 'load_down':
                    a, n = st[1], NT * 128
                    if a == 0:
                        W(written(('va', NN - 1, 1)), ('va', NN - 1, 1), turn)
                        sp.dma_start(WSD, sh_down).then_inc(sems['load_d'], 16)
                    sp.dma_start(WD[:, a * n:a * n + n], moe_down[:, a * n:a * n + n]).then_inc(sems['load_d'], 16)
                elif k == 'qw':
                    _, kind, c, i = st
                    qs = ('qs',) + st[1:]
                    W('q_split', qs, turn)
                    sp.dma_start(qd[i].rearrange("a p t -> p a t"), QP[ordinal[qs] % 2][:, :, :]).then_inc(sems[f'q_out{i}'], 16)
                elif k == 'qr':
                    _, kind, c, i = st
                    if kind == 'X' and c == 0 and i == 0:
                        sp.wait_ge(sems['zeroed'], 8)
                    W(f'q_out{i}', ('qw',) + st[1:], turn)
                    blocks(QA[i], qd[i], QPART, DH[kind], HEADS[kind], sems[f'q_in{i}'], QW)
                elif k == 'kw':
                    _, kind, c, b = st
                    W('k_split', ('ks',) + st[1:], turn)
                    if kind == 'X':
                        sp.dma_start(kdx[c][b].rearrange("a p t -> p a t"), KP[:, :, 0:SK]).then_inc(sems[keys_sem('out', st)], 16)
                    else:
                        sp.dma_start(kd[b].rearrange("a p t -> p a t"), KP[:, :, :]).then_inc(sems[keys_sem('out', st)], 16)
                elif k == 'kr':
                    _, kind, c, b = st
                    in_dram = count(keys_sem('out', st), ('kw',) + st[1:], turn)
                    unused = count('st_done', ('st', 'F', 0, CH * (c - 1) + 2 * b + 1, 1, 3), turn) if kind == 'F' and c else None
                    if turn is not None:
                        unused = sp.snap(sp.to_reg(unused))
                    sp.wait_ge(sems[keys_sem('out', st)], in_dram)
                    if kind == 'X':
                        blocks(KAX[c][b], kdx[c][b], KPART, 8, 16, sems[keys_sem('in', st)], SK)
                    else:
                        if unused is not None:
                            sp.wait_ge(sems['st_done'], unused)
                        blocks(KAF[b], kd[b], KPART, 16, 8, sems[keys_sem('in', st)], SQ)
                elif k == 'md':
                    _, kind, L, s, g = st
                    n = group_at[st[1:]] % 4
                    i, h = chain_of(kind, s), head0(kind, s, g)
                    W(read(('mT',) + st[1:]), ('mT',) + st[1:], turn)
                    sp.dma_start(QA[i][ROWS_M:KR, h:h + G, :], MT[n][:, :].unsqueeze(1).broadcast_to([3 * G, G, QW])).then_inc(sems[rows_sem(st)], 16)
                elif k == 'wl_post':
                    c = st[1]
                    src = wrow(f_wpost, dyn(c + 1, turn))
                    W(written(('wq', c, CH - 1)), ('wq', c, CH - 1), turn)
                    sp.wait_ge(sems['load_f'], 16 * 9)
                    sp.dma_start(WPOST[:, :, :], src).then_inc(sems['wpost_in'], 16)
                elif k == 'wl_v':
                    c = st[1]
                    src = wrow(f_wv, dyn(c, turn))
                    W(written(('vb', c - 1, 1)), ('vb', c - 1, 1), turn)
                    sp.wait_ge(sems['load_f'], 16 * 9)
                    sp.dma_start(WV[:, :, :], src).then_inc(sems['wv_in'], 16)
                elif k == 'wl_k':
                    c = st[1]
                    src = wrow(f_wk, dyn(c, turn))
                    W(written(('kb', c - 1, 1)), ('kb', c - 1, 1), turn)
                    sp.wait_ge(sems['load_f'], 16 * 9)
                    sp.dma_start(WK[:, :, :], src).then_inc(sems['wk_in'], 16)
                elif k == 'fin' and st[1] == CH - 1:
                    W(read(st), st, turn)
                    sp.dma_start(SELE, c_sel_e).then_inc(sems['load_d'], 16)
                elif k == 'moe':
                    for h in (0, 1):
                        sp.wait_ge(sems['y_added'], h + 1)
                        sp.dma_start(out[:, 4 * h:4 * h + 4, :], X[:, 4 * h:4 * h + 4, :]).then_inc(sems['out_done'], 16)
                    sp.wait_ge(sems['out_done'], 32)

            def wrow(w, c):
                if isinstance(c, int):
                    return w[c]
                return w.rearrange("c p a n -> (c p) a n")[bass.ds(sp.snap(c * 128), 128)]

            run(sp, emit)


_OUT = ((2, 512, 128), 'float32')


def kernel(**inputs):
    import numpy as np
    import concourse.bacc as bacc
    from concourse import mybir as _mybir
    from concourse.bass_utils import run_bass_kernel_spmd as run_spmd

    a = {k: np.asarray(v) for k, v in inputs.items()}
    f = np.float32
    NT, D = 8, 128

    def rows(v, n=128):
        return np.ascontiguousarray(np.broadcast_to(v, (n,) + v.shape))

    edge, lind = [], 0
    for c in range(6):
        n = min(c + 1, 5)
        edge.append((lind + n - 1, lind, lind + n // 2))
        lind += n
    We, be, Wq, Wk, Wv, Wo = (a[f'L0_ffn_{n}'] for n in ('We', 'be', 'Wq', 'Wk', 'Wv', 'Wo'))

    def side(*m):
        return np.stack(m, axis=1)
    wpost = [side(Wo[0], We[edge[0][0]], Wq[0])]
    for c in range(6):
        nx = min(c + 1, 5)
        wpost.append(side(Wo[c], We[edge[nx][0]], Wq[nx]))
    wk = [side(We[edge[c][1]], Wk[c]) for c in range(6)]
    wk.append(wk[-1])
    wv = [side(We[edge[c][2]], Wv[c]) for c in range(6)]
    xl = [{n: a[f'L0_xattn_{n.lower()}' if L == 0 else f'L1_xattn_{n}'] for n in ('Wq', 'bq', 'Wk', 'bk', 'Wv', 'bv', 'Wo', 'bo')} for L in (0, 1)]

    one = np.uint16(0x3F80)
    sel_x = np.zeros((12, 16, 77), np.uint16)
    sel_f = np.zeros((12, 8, 512), np.uint16)
    for p in range(3):
        for r in range(4):
            sel_x[4 * p + r, r::4, :] = one
            sel_f[4 * p + r, r::4, :] = one
    sel_e = np.zeros((128, 32, 128), np.float16)
    for e in range(64):
        sel_e[e, e // 2, 64 * (e % 2):64 * (e % 2) + 64] = 1.0
        sel_e[64 + e, e // 2, 64 * (e % 2):64 * (e % 2) + 64] = 1.0 / 2048.0

    arrays = [
        ('x', a['x'].reshape(NT, 128, D).transpose(1, 0, 2)),
        ('ctx_t', a['ctx_768'].transpose(0, 2, 1)),
        ('g_all', rows(np.concatenate([a['g_xattn'], a['g_ffn']]))),
        ('x_wq', side(xl[0]['Wq'], xl[1]['Wq'])),
        ('x_wkv', np.stack([side(xl[L]['Wk'], xl[L]['Wv']) for L in (0, 1)], axis=1)),
        ('x_wo', side(xl[0]['Wo'], xl[1]['Wo'])),
        ('x_bqk', np.stack([np.stack([xl[L]['bq'], xl[L]['bk']], axis=1) for L in (0, 1)], axis=1)),
        ('x_bvo', rows(np.stack([np.stack([xl[L]['bv'], xl[L]['bo']]) for L in (0, 1)]))),
        ('f_wpost', np.stack(wpost)), ('f_wk', np.stack(wk)), ('f_wv', np.stack(wv)),
        ('f_ew', rows(a['L0_ffn_ew'].reshape(-1))),
        ('f_be', be[np.array(edge).reshape(-1)].T),
        ('f_actw', rows(a['L0_ffn_act_w'])),
        ('ln_gb', rows(np.stack([a['L0_ffn_ln_g'], a['L0_ffn_ln_b']]))),
        ('w_router', a['L1_ffn_w_router']), ('b_router', rows(a['L1_ffn_b_router'])),
        ('moe_gate', a['L1_ffn_we_gate'].transpose(1, 0, 2).reshape(D, 64 * 64)),
        ('moe_up', a['L1_ffn_we_up'].transpose(1, 0, 2).reshape(D, 64 * 64)),
        ('moe_down', a['L1_ffn_we_down'].reshape(32, 128, D).transpose(1, 0, 2).reshape(128, 32 * D)),
        ('sh_gate_up', np.concatenate([a['L1_ffn_ws_gate'], a['L1_ffn_ws_up']], axis=1)),
        ('sh_down', a['L1_ffn_ws_down']),
        ('c_ident', np.eye(128, dtype=f)), ('c_ident_bf', np.where(np.eye(128) > 0, one, np.uint16(0)).astype(np.uint16)),
        ('c_sel_x', sel_x), ('c_sel_f', sel_f), ('c_sel_e', sel_e), ('c_ident_h', np.eye(128, dtype=np.float16)),
    ]
    nc = bacc.Bacc("TRN2", target_bir_lowering=False, num_devices=1)
    feeds, args = {}, {}
    for name, arr in arrays:
        arr = np.ascontiguousarray(arr)
        feeds[f"in_{name}"] = arr
        ap = nc.dram_tensor(f"in_{name}", arr.shape, _mybir.dt.from_np(arr.dtype), kind="ExternalInput").ap()
        args[name] = ap.bitcast(_mybir.dt.bfloat16) if arr.dtype == np.uint16 else ap
    out = nc.dram_tensor("out_x", (NT, 128, D), _mybir.dt.float32, kind="ExternalOutput").ap()
    flamingo_gated_two_layer(nc, out=out.rearrange("t p d -> p t d"), **args)
    r = run_spmd(nc, [feeds], core_ids=[0])
    return r.results[0]["out_x"].reshape(_OUT[0])
```
